# Optimizing a Trainium2 kernel written in Bass

```python
import numpy as np
import jax
import jax.numpy as jnp

def _softmax(x, axis=-1):
    return jax.nn.softmax(x, axis=axis)

def _gelu(x):
    return jax.nn.gelu(x, approximate=True)

def _silu(x):
    return jax.nn.silu(x)

def _sigmoid(x):
    return jax.nn.sigmoid(x)

def _layernorm(x, axis=-1, eps=1e-05):
    m = jnp.mean(x, axis=axis, keepdims=True)
    v = jnp.var(x, axis=axis, keepdims=True)
    return (x - m) / jnp.sqrt(v + eps)

def _scatter_add(tgt, idx, src, axis=0):
    return tgt.at[idx].add(src)

def _segment_sum(src, seg, n):
    return jax.ops.segment_sum(src, seg, n)
kernel_name = 'mk_xattn_seq_d4_seqx_r8_e57279'

def setup_inputs(seed: int=0):
    np.random.seed(seed)
    _w = jnp.asarray

    def _rec_inputs():
        import jax
        import jax.numpy as jnp
        _rk = jax.random.key(seed)
        x = 7.22e-05 + 1 * jax.random.normal(jax.random.fold_in(_rk, 1), (8, 56, 256), jnp.float32)
        _lenS = 56 - jax.random.randint(jax.random.fold_in(_rk, 7), (8,), 0, max(1, 56 // 4) + 1, jnp.int32)
        _lenS2 = 1500 - jax.random.randint(jax.random.fold_in(_rk, 8), (8,), 0, max(1, 1500 // 4) + 1, jnp.int32)
        _ctx_2048P = jax.random.normal(jax.random.fold_in(_rk, 11), (8, 16, 256), jnp.float32)
        _ctx_2048c = jax.random.dirichlet(jax.random.fold_in(_rk, 511), 0.3 * jnp.ones((16,), jnp.float32), (8, 1500))
        _ctx_2048t = jnp.einsum('bsk,bkd->bsd', _ctx_2048c, _ctx_2048P)
        _ctx_2048t = _ctx_2048t * jax.lax.rsqrt(jnp.mean(jnp.square(_ctx_2048t)) + 1e-12) * 0.953939
        ctx_2048 = 4.13588e-05 + 0.999923 * (_ctx_2048t + 0.3 * jax.random.normal(jax.random.fold_in(_rk, 611), (8, 1500, 256), jnp.float32))
        _validS = jnp.arange(56)[None, :] < _lenS[:, None]
        _validS2 = jnp.arange(1500)[None, :] < _lenS2[:, None]
        _causal = jnp.tril(jnp.ones((56, 56), dtype=bool))
        mask_Bx1xSxS2_ff0 = jnp.where(jnp.ones((8, 1, 56, 1500), dtype=bool), 0.0, -1000000000.0).astype(jnp.float32)
        mask_BxS2_bf1 = jnp.ones((8, 1500), dtype=bool)
        mask_BxS2_ik0 = jnp.where(jnp.broadcast_to(_validS2[:, :], (8, 1500)), 0, 1).astype(jnp.int32)
        return (x, ctx_2048, mask_Bx1xSxS2_ff0, mask_BxS2_bf1, mask_BxS2_ik0)
    x, ctx_2048, mask_Bx1xSxS2_ff0, mask_BxS2_bf1, mask_BxS2_ik0 = _rec_inputs()

    def _L0_xattn_setup():
        import jax, jax.numpy as jnp
        import numpy as np
        H = 256
        NH = 32
        KVH = 8
        HD = H // NH
        GROUPS = NH // KVH
        EPS = 1e-06
        B, L, S = (4, 128, 128)

        def _gqa_forward(hidden_state, encoder_hidden_state, encoder_attention_mask, Wq, bq, Wk, bk, Wv, bv, Wo, bo, gamma, beta):
            b, l, _ = hidden_state.shape
            s = encoder_hidden_state.shape[1]
            q = hidden_state @ Wq + bq
            k = encoder_hidden_state @ Wk + bk
            v = encoder_hidden_state @ Wv + bv
            q = q.reshape(b, l, KVH, GROUPS, HD).transpose(0, 2, 3, 1, 4)
            k = k.reshape(b, s, KVH, HD).transpose(0, 2, 1, 3)
            v = v.reshape(b, s, KVH, HD).transpose(0, 2, 1, 3)
            scale = 1.0 / jnp.sqrt(jnp.asarray(HD, q.dtype))
            scores = jnp.einsum('bkgld,bksd->bkgls', q, k) * scale
            scores = scores + encoder_attention_mask[:, :, None, :, :]
            attn = jax.nn.softmax(scores, axis=-1)
            out = jnp.einsum('bkgls,bksd->bkgld', attn, v)
            out = out.transpose(0, 3, 1, 2, 4).reshape(b, l, H)
            out = out @ Wo + bo
            x = out + hidden_state
            mu = jnp.mean(x, axis=-1, keepdims=True)
            var = jnp.var(x, axis=-1, keepdims=True)
            return (x - mu) * jax.lax.rsqrt(var + EPS) * gamma + beta
        key = jax.random.key(seed)
        ks = jax.random.split(key, 12)
        sd = 0.02
        return {'hidden_state': jax.random.normal(ks[0], (B, L, H), jnp.float32), 'encoder_hidden_state': jax.random.normal(ks[1], (B, S, H), jnp.float32), 'encoder_attention_mask': jnp.zeros((B, 1, L, S), jnp.float32), 'Wq': jax.random.normal(ks[2], (H, H), jnp.float32) * sd, 'bq': jnp.zeros((H,), jnp.float32), 'Wk': jax.random.normal(ks[3], (H, KVH * HD), jnp.float32) * sd, 'bk': jnp.zeros((KVH * HD,), jnp.float32), 'Wv': jax.random.normal(ks[4], (H, KVH * HD), jnp.float32) * sd, 'bv': jnp.zeros((KVH * HD,), jnp.float32), 'Wo': jax.random.normal(ks[5], (H, H), jnp.float32) * sd, 'bo': jnp.zeros((H,), jnp.float32), 'gamma': jnp.ones((H,), jnp.float32), 'beta': jnp.zeros((H,), jnp.float32)}
    _L0_xattn_all = _L0_xattn_setup()
    _L0_xattn_in = {k: v for k, v in _L0_xattn_all.items() if k in ('Wq', 'bq', 'Wk', 'bk', 'Wv', 'bv', 'Wo', 'bo', 'gamma', 'beta')}
    del _L0_xattn_all

    def _L1_xattn_setup():
        import jax, jax.numpy as jnp
        import numpy as np
        HIDDEN = 256
        HEADS = 16
        HEAD_DIM = HIDDEN // HEADS
        LN_EPS = 1e-05
        GATE_INIT = 0.5

        def _layer_norm(x, gamma, beta):
            mu = jnp.mean(x, axis=-1, keepdims=True)
            var = jnp.mean(jnp.square(x - mu), axis=-1, keepdims=True)
            return (x - mu) * jax.lax.rsqrt(var + LN_EPS) * gamma + beta
        key = jax.random.key(seed)
        ks = jax.random.split(key, 8)
        B, T_TEXT, T_AUDIO = (4, 256, 1500)
        s = 0.02
        return {'hidden_states': jax.random.normal(ks[0], (B, T_TEXT, HIDDEN), jnp.float32), 'audio_kv': jax.random.normal(ks[1], (B, T_AUDIO, HIDDEN), jnp.float32), 'audio_attention_mask': jnp.ones((B, T_AUDIO), dtype=bool), 'Wq': jax.random.normal(ks[2], (HIDDEN, HIDDEN), jnp.float32) * s, 'Wk': jax.random.normal(ks[3], (HIDDEN, HIDDEN), jnp.float32) * s, 'Wv': jax.random.normal(ks[4], (HIDDEN, HIDDEN), jnp.float32) * s, 'Wo': jax.random.normal(ks[5], (HIDDEN, HIDDEN), jnp.float32) * s, 'ln_gamma': jnp.ones((HIDDEN,), jnp.float32), 'ln_beta': jnp.zeros((HIDDEN,), jnp.float32), 'gate': jnp.array([GATE_INIT], jnp.float32)}
    _L1_xattn_all = _L1_xattn_setup()
    _L1_xattn_in = {k: v for k, v in _L1_xattn_all.items() if k in ('Wq', 'Wk', 'Wv', 'Wo', 'ln_gamma', 'ln_beta', 'gate')}
    del _L1_xattn_all

    def _L2_xattn_setup():
        import jax, jax.numpy as jnp
        import numpy as np
        B, P, K, H, NH = (4, 256, 32, 256, 16)
        DH = H // NH
        EPS = 1e-06

        def rmsnorm(x, w):
            var = jnp.mean(jnp.square(x), axis=-1, keepdims=True)
            return x * jax.lax.rsqrt(var + EPS) * w
        key = jax.random.key(seed)
        ks = jax.random.split(key, 12)
        s = 0.02
        return {'x': jax.random.normal(ks[0], (B, P, H), jnp.float32), 'latents': jax.random.normal(ks[1], (B, K, H), jnp.float32), 'attention_mask': jax.random.randint(ks[2], (B, P), 0, 2, jnp.int32), 'q_w': s * jax.random.normal(ks[3], (H, H), jnp.float32), 'q_b': jnp.zeros((H,), jnp.float32), 'kv_w': s * jax.random.normal(ks[4], (H, 2 * H), jnp.float32), 'kv_b': jnp.zeros((2 * H,), jnp.float32), 'out_w': s * jax.random.normal(ks[5], (H, H), jnp.float32), 'out_b': jnp.zeros((H,), jnp.float32), 'postnorm_w': jnp.ones((H,), jnp.float32), 'mlp_w1': s * jax.random.normal(ks[6], (H, 4 * H), jnp.float32), 'mlp_b1': jnp.zeros((4 * H,), jnp.float32), 'mlp_w2': s * jax.random.normal(ks[7], (4 * H, H), jnp.float32), 'mlp_b2': jnp.zeros((H,), jnp.float32)}
    _L2_xattn_all = _L2_xattn_setup()
    _L2_xattn_in = {k: v for k, v in _L2_xattn_all.items() if k in ('q_w', 'q_b', 'kv_w', 'kv_b', 'out_w', 'out_b', 'postnorm_w', 'mlp_w1', 'mlp_b1', 'mlp_w2', 'mlp_b2')}
    del _L2_xattn_all

    def _L3_xattn_setup():
        import jax, jax.numpy as jnp
        import numpy as np
        D = 256
        H = 16
        HD = D // H
        INNER = 4 * D
        EPS = 1e-05

        def layer_norm(x, w, b):
            mu = jnp.mean(x, axis=-1, keepdims=True)
            var = jnp.mean(jnp.square(x - mu), axis=-1, keepdims=True)
            return (x - mu) * jax.lax.rsqrt(var + EPS) * w + b
        key = jax.random.key(seed)
        ks = jax.random.split(key, 12)
        B, LQ, LK = (4, 128, 256)
        std = 0.02
        inp = {'hidden_states': jax.random.normal(ks[0], (B, LQ, D), jnp.float32), 'encoder_hidden_states': jax.random.normal(ks[1], (B, LK, D), jnp.float32), 'encoder_attention_mask': jnp.ones((B, LK), dtype=bool), 'ln1_w': jnp.ones((D,), jnp.float32), 'ln1_b': jnp.zeros((D,), jnp.float32), 'q_w': jax.random.normal(ks[2], (D, D), jnp.float32) * std, 'q_b': jnp.zeros((D,), jnp.float32), 'k_w': jax.random.normal(ks[3], (D, D), jnp.float32) * std, 'k_b': jnp.zeros((D,), jnp.float32), 'v_w': jax.random.normal(ks[4], (D, D), jnp.float32) * std, 'v_b': jnp.zeros((D,), jnp.float32), 'cproj_w': jax.random.normal(ks[5], (D, D), jnp.float32) * std, 'cproj_b': jnp.zeros((D,), jnp.float32), 'ln2_w': jnp.ones((D,), jnp.float32), 'ln2_b': jnp.zeros((D,), jnp.float32), 'fc_w': jax.random.normal(ks[6], (D, INNER), jnp.float32) * std, 'fc_b': jnp.zeros((INNER,), jnp.float32), 'proj_w': jax.random.normal(ks[7], (INNER, D), jnp.float32) * std, 'proj_b': jnp.zeros((D,), jnp.float32)}
        return inp
    _L3_xattn_all = _L3_xattn_setup()
    _L3_xattn_in = {k: v for k, v in _L3_xattn_all.items() if k in ('ln1_w', 'ln1_b', 'q_w', 'q_b', 'k_w', 'k_b', 'v_w', 'v_b', 'cproj_w', 'cproj_b', 'ln2_w', 'ln2_b', 'fc_w', 'fc_b', 'proj_w', 'proj_b')}
    del _L3_xattn_all
    return {'x': x, 'ctx_2048': ctx_2048, 'mask_Bx1xSxS2_ff0': mask_Bx1xSxS2_ff0, 'mask_BxS2_bf1': mask_BxS2_bf1, 'mask_BxS2_ik0': mask_BxS2_ik0, 'L0_xattn_Wq': _L0_xattn_in['Wq'], 'L0_xattn_bq': _L0_xattn_in['bq'], 'L0_xattn_Wk': _L0_xattn_in['Wk'], 'L0_xattn_bk': _L0_xattn_in['bk'], 'L0_xattn_Wv': _L0_xattn_in['Wv'], 'L0_xattn_bv': _L0_xattn_in['bv'], 'L0_xattn_Wo': _L0_xattn_in['Wo'], 'L0_xattn_bo': _L0_xattn_in['bo'], 'L0_xattn_gamma': _L0_xattn_in['gamma'], 'L0_xattn_beta': _L0_xattn_in['beta'], 'L1_xattn_Wq': _L1_xattn_in['Wq'], 'L1_xattn_Wk': _L1_xattn_in['Wk'], 'L1_xattn_Wv': _L1_xattn_in['Wv'], 'L1_xattn_Wo': _L1_xattn_in['Wo'], 'L1_xattn_ln_gamma': _L1_xattn_in['ln_gamma'], 'L1_xattn_ln_beta': _L1_xattn_in['ln_beta'], 'L1_xattn_gate': _L1_xattn_in['gate'], 'L2_xattn_q_w': _L2_xattn_in['q_w'], 'L2_xattn_q_b': _L2_xattn_in['q_b'], 'L2_xattn_kv_w': _L2_xattn_in['kv_w'], 'L2_xattn_kv_b': _L2_xattn_in['kv_b'], 'L2_xattn_out_w': _L2_xattn_in['out_w'], 'L2_xattn_out_b': _L2_xattn_in['out_b'], 'L2_xattn_postnorm_w': _L2_xattn_in['postnorm_w'], 'L2_xattn_mlp_w1': _L2_xattn_in['mlp_w1'], 'L2_xattn_mlp_b1': _L2_xattn_in['mlp_b1'], 'L2_xattn_mlp_w2': _L2_xattn_in['mlp_w2'], 'L2_xattn_mlp_b2': _L2_xattn_in['mlp_b2'], 'L3_xattn_ln1_w': _L3_xattn_in['ln1_w'], 'L3_xattn_ln1_b': _L3_xattn_in['ln1_b'], 'L3_xattn_q_w': _L3_xattn_in['q_w'], 'L3_xattn_q_b': _L3_xattn_in['q_b'], 'L3_xattn_k_w': _L3_xattn_in['k_w'], 'L3_xattn_k_b': _L3_xattn_in['k_b'], 'L3_xattn_v_w': _L3_xattn_in['v_w'], 'L3_xattn_v_b': _L3_xattn_in['v_b'], 'L3_xattn_cproj_w': _L3_xattn_in['cproj_w'], 'L3_xattn_cproj_b': _L3_xattn_in['cproj_b'], 'L3_xattn_ln2_w': _L3_xattn_in['ln2_w'], 'L3_xattn_ln2_b': _L3_xattn_in['ln2_b'], 'L3_xattn_fc_w': _L3_xattn_in['fc_w'], 'L3_xattn_fc_b': _L3_xattn_in['fc_b'], 'L3_xattn_proj_w': _L3_xattn_in['proj_w'], 'L3_xattn_proj_b': _L3_xattn_in['proj_b']}

def reference(x, ctx_2048, mask_Bx1xSxS2_ff0, mask_BxS2_bf1, mask_BxS2_ik0, L0_xattn_Wq, L0_xattn_bq, L0_xattn_Wk, L0_xattn_bk, L0_xattn_Wv, L0_xattn_bv, L0_xattn_Wo, L0_xattn_bo, L0_xattn_gamma, L0_xattn_beta, L1_xattn_Wq, L1_xattn_Wk, L1_xattn_Wv, L1_xattn_Wo, L1_xattn_ln_gamma, L1_xattn_ln_beta, L1_xattn_gate, L2_xattn_q_w, L2_xattn_q_b, L2_xattn_kv_w, L2_xattn_kv_b, L2_xattn_out_w, L2_xattn_out_b, L2_xattn_postnorm_w, L2_xattn_mlp_w1, L2_xattn_mlp_b1, L2_xattn_mlp_w2, L2_xattn_mlp_b2, L3_xattn_ln1_w, L3_xattn_ln1_b, L3_xattn_q_w, L3_xattn_q_b, L3_xattn_k_w, L3_xattn_k_b, L3_xattn_v_w, L3_xattn_v_b, L3_xattn_cproj_w, L3_xattn_cproj_b, L3_xattn_ln2_w, L3_xattn_ln2_b, L3_xattn_fc_w, L3_xattn_fc_b, L3_xattn_proj_w, L3_xattn_proj_b):
    import jax
    import jax.numpy as jnp

    def _L0_xattn_ref(hidden_state, encoder_hidden_state, encoder_attention_mask, Wq, bq, Wk, bk, Wv, bv, Wo, bo, gamma, beta):
        import jax, jax.numpy as jnp
        import numpy as np
        H = 256
        NH = 32
        KVH = 8
        HD = H // NH
        GROUPS = NH // KVH
        EPS = 1e-06
        B, L, S = (4, 128, 128)

        def _gqa_forward(hidden_state, encoder_hidden_state, encoder_attention_mask, Wq, bq, Wk, bk, Wv, bv, Wo, bo, gamma, beta):
            b, l, _ = hidden_state.shape
            s = encoder_hidden_state.shape[1]
            q = hidden_state @ Wq + bq
            k = encoder_hidden_state @ Wk + bk
            v = encoder_hidden_state @ Wv + bv
            q = q.reshape(b, l, KVH, GROUPS, HD).transpose(0, 2, 3, 1, 4)
            k = k.reshape(b, s, KVH, HD).transpose(0, 2, 1, 3)
            v = v.reshape(b, s, KVH, HD).transpose(0, 2, 1, 3)
            scale = 1.0 / jnp.sqrt(jnp.asarray(HD, q.dtype))
            scores = jnp.einsum('bkgld,bksd->bkgls', q, k) * scale
            scores = scores + encoder_attention_mask[:, :, None, :, :]
            attn = jax.nn.softmax(scores, axis=-1)
            out = jnp.einsum('bkgls,bksd->bkgld', attn, v)
            out = out.transpose(0, 3, 1, 2, 4).reshape(b, l, H)
            out = out @ Wo + bo
            x = out + hidden_state
            mu = jnp.mean(x, axis=-1, keepdims=True)
            var = jnp.var(x, axis=-1, keepdims=True)
            return (x - mu) * jax.lax.rsqrt(var + EPS) * gamma + beta
        return _gqa_forward(hidden_state, encoder_hidden_state, encoder_attention_mask, Wq, bq, Wk, bk, Wv, bv, Wo, bo, gamma, beta)

    def _L1_xattn_ref(hidden_states, audio_kv, audio_attention_mask, Wq, Wk, Wv, Wo, ln_gamma, ln_beta, gate):
        import jax, jax.numpy as jnp
        import numpy as np
        HIDDEN = 256
        HEADS = 16
        HEAD_DIM = HIDDEN // HEADS
        LN_EPS = 1e-05
        GATE_INIT = 0.5

        def _layer_norm(x, gamma, beta):
            mu = jnp.mean(x, axis=-1, keepdims=True)
            var = jnp.mean(jnp.square(x - mu), axis=-1, keepdims=True)
            return (x - mu) * jax.lax.rsqrt(var + LN_EPS) * gamma + beta
        B, Tt, D = hidden_states.shape
        Ta = audio_kv.shape[1]
        scale = HEAD_DIM ** (-0.5)
        a = _layer_norm(audio_kv, ln_gamma, ln_beta)
        Q = (hidden_states @ Wq.T).reshape(B, Tt, HEADS, HEAD_DIM).transpose(0, 2, 1, 3)
        K = (a @ Wk.T).reshape(B, Ta, HEADS, HEAD_DIM).transpose(0, 2, 1, 3)
        V = (a @ Wv.T).reshape(B, Ta, HEADS, HEAD_DIM).transpose(0, 2, 1, 3)
        scores = jnp.einsum('bhtd,bhsd->bhts', Q, K) * scale
        mask = audio_attention_mask[:, None, None, :]
        scores = jnp.where(mask, scores, jnp.float32(-jnp.inf))
        attn = jax.nn.softmax(scores, axis=-1)
        out = jnp.einsum('bhts,bhsd->bhtd', attn, V)
        out = out.transpose(0, 2, 1, 3).reshape(B, Tt, D)
        out = out @ Wo.T
        return hidden_states + jnp.tanh(gate) * out

    def _L2_xattn_ref(x, latents, attention_mask, q_w, q_b, kv_w, kv_b, out_w, out_b, postnorm_w, mlp_w1, mlp_b1, mlp_w2, mlp_b2):
        import jax, jax.numpy as jnp
        import numpy as np
        B, P, K, H, NH = (4, 256, 32, 256, 16)
        DH = H // NH
        EPS = 1e-06

        def rmsnorm(x, w):
            var = jnp.mean(jnp.square(x), axis=-1, keepdims=True)
            return x * jax.lax.rsqrt(var + EPS) * w
        b, p, _ = x.shape
        k_len = latents.shape[1]
        residual = latents
        h = jnp.concatenate([x, latents], axis=1)
        q = (latents @ q_w + q_b).reshape(b, k_len, NH, DH)
        kv = (h @ kv_w + kv_b).reshape(b, p + k_len, NH, DH, 2)
        kmat, v = (kv[..., 0], kv[..., 1])
        attn = jnp.einsum('bkhd,bnhd->bhkn', q, kmat) / DH
        full_mask = jnp.concatenate([attention_mask.astype(bool), jnp.ones((b, k_len), bool)], axis=-1)
        attn = jnp.where(full_mask[:, None, None, :], attn, -jnp.inf)
        attn = jax.nn.softmax(attn.astype(jnp.float32), axis=-1).astype(q.dtype)
        attn_out = jnp.einsum('bhkn,bnhd->bkhd', attn, v).reshape(b, k_len, H)
        attn_out = attn_out @ out_w + out_b + residual
        out = rmsnorm(attn_out, postnorm_w)
        out = jax.nn.gelu(out @ mlp_w1 + mlp_b1) @ mlp_w2 + mlp_b2
        return out + residual

    def _L3_xattn_ref(hidden_states, encoder_hidden_states, encoder_attention_mask, ln1_w, ln1_b, q_w, q_b, k_w, k_b, v_w, v_b, cproj_w, cproj_b, ln2_w, ln2_b, fc_w, fc_b, proj_w, proj_b):
        import jax, jax.numpy as jnp
        import numpy as np
        D = 256
        H = 16
        HD = D // H
        INNER = 4 * D
        EPS = 1e-05

        def layer_norm(x, w, b):
            mu = jnp.mean(x, axis=-1, keepdims=True)
            var = jnp.mean(jnp.square(x - mu), axis=-1, keepdims=True)
            return (x - mu) * jax.lax.rsqrt(var + EPS) * w + b
        B, LQ, _ = hidden_states.shape
        LK = encoder_hidden_states.shape[1]
        residual = hidden_states
        x = layer_norm(hidden_states, ln1_w, ln1_b)
        q = (x @ q_w + q_b).reshape(B, LQ, H, HD).transpose(0, 2, 1, 3)
        k = (encoder_hidden_states @ k_w + k_b).reshape(B, LK, H, HD).transpose(0, 2, 1, 3)
        v = (encoder_hidden_states @ v_w + v_b).reshape(B, LK, H, HD).transpose(0, 2, 1, 3)
        scale = 1.0 / np.sqrt(HD).astype(np.float32)
        scores = jnp.einsum('bhqd,bhkd->bhqk', q, k) * scale
        mask = encoder_attention_mask[:, None, None, :]
        mask_value = jnp.finfo(scores.dtype).min
        scores = jnp.where(mask, scores, mask_value)
        attn = jax.nn.softmax(scores, axis=-1)
        out = jnp.einsum('bhqk,bhkd->bhqd', attn, v)
        out = out.transpose(0, 2, 1, 3).reshape(B, LQ, D)
        out = out @ cproj_w + cproj_b
        hidden = out + residual
        residual = hidden
        y = layer_norm(hidden, ln2_w, ln2_b)
        y = jax.nn.gelu(y @ fc_w + fc_b, approximate=True)
        y = y @ proj_w + proj_b
        return residual + y
    x = _L0_xattn_ref(x, ctx_2048, mask_Bx1xSxS2_ff0, L0_xattn_Wq, L0_xattn_bq, L0_xattn_Wk, L0_xattn_bk, L0_xattn_Wv, L0_xattn_bv, L0_xattn_Wo, L0_xattn_bo, L0_xattn_gamma, L0_xattn_beta)
    x = _L1_xattn_ref(x, ctx_2048, mask_BxS2_bf1, L1_xattn_Wq, L1_xattn_Wk, L1_xattn_Wv, L1_xattn_Wo, L1_xattn_ln_gamma, L1_xattn_ln_beta, L1_xattn_gate)
    x = _L2_xattn_ref(ctx_2048, x, mask_BxS2_ik0, L2_xattn_q_w, L2_xattn_q_b, L2_xattn_kv_w, L2_xattn_kv_b, L2_xattn_out_w, L2_xattn_out_b, L2_xattn_postnorm_w, L2_xattn_mlp_w1, L2_xattn_mlp_b1, L2_xattn_mlp_w2, L2_xattn_mlp_b2)
    x = _L3_xattn_ref(x, ctx_2048, mask_BxS2_bf1, L3_xattn_ln1_w, L3_xattn_ln1_b, L3_xattn_q_w, L3_xattn_q_b, L3_xattn_k_w, L3_xattn_k_b, L3_xattn_v_w, L3_xattn_v_b, L3_xattn_cproj_w, L3_xattn_cproj_b, L3_xattn_ln2_w, L3_xattn_ln2_b, L3_xattn_fc_w, L3_xattn_fc_b, L3_xattn_proj_w, L3_xattn_proj_b)
    return x

_drawn_inputs = setup_inputs


def setup_inputs(seed=0):
    import zlib

    import numpy as np

    out = dict(_drawn_inputs(seed))
    spreads = {'L0_xattn_bq': (0.0, 0.8),
     'L0_xattn_bk': (0.0, 2.0),
     'L0_xattn_bv': (0.0, 0.1),
     'L0_xattn_bo': (0.0, 0.1),
     'L0_xattn_gamma': (1.0, 0.2),
     'L0_xattn_beta': (0.0, 0.1),
     'L1_xattn_ln_gamma': (1.0, 0.6),
     'L1_xattn_ln_beta': (0.0, 0.8),
     'L2_xattn_q_b': (0.0, 0.8),
     'L2_xattn_kv_b': (0.0, 0.8),
     'L2_xattn_out_b': (0.0, 1.9),
     'L2_xattn_postnorm_w': (1.0, 0.6),
     'L2_xattn_mlp_b1': (0.0, 0.1),
     'L2_xattn_mlp_b2': (0.0, 0.1),
     'L3_xattn_ln1_w': (1.0, 0.6),
     'L3_xattn_ln1_b': (0.0, 0.8),
     'L3_xattn_q_b': (0.0, 0.8),
     'L3_xattn_k_b': (0.0, 2.0),
     'L3_xattn_v_b': (0.0, 0.1),
     'L3_xattn_cproj_b': (0.0, 0.1),
     'L3_xattn_ln2_w': (1.0, 0.6),
     'L3_xattn_ln2_b': (0.0, 0.715),
     'L3_xattn_fc_b': (0.0, 0.1),
     'L3_xattn_proj_b': (0.0, 0.1)}
    factors = {'L0_xattn_Wq': 8.0,
     'L0_xattn_Wk': 8.0,
     'L1_xattn_Wq': 8.0,
     'L1_xattn_Wk': 8.0,
     'L2_xattn_q_w': 8.0,
     'L2_xattn_kv_w': 8.0,
     'L2_xattn_out_w': 8.0,
     'L3_xattn_q_w': 8.0,
     'L3_xattn_k_w': 8.0}
    for name, (base, spread) in spreads.items():
        noise = np.random.default_rng([zlib.crc32(name.encode()), seed]).standard_normal(out[name].shape)
        drawn = base * np.exp(spread * noise) if base else spread * noise
        out[name] = jnp.asarray(drawn.astype(out[name].dtype))
    for name, factor in factors.items():
        out[name] = (out[name] * factor).astype(out[name].dtype)
    return out
```

```python
from contextlib import ExitStack

import concourse.bass as bass
from concourse import mybir

F32 = mybir.dt.float32
F32R = mybir.dt.float32r
BF16 = mybir.dt.bfloat16
U8 = mybir.dt.uint8
I32 = mybir.dt.int32
ALU = mybir.AluOpType
ACT = mybir.ActivationFunctionType
AX = mybir.AxisListType

NB = 8
LQ = 56
LK = 1500
D = 256
KT = D // 128
NT = -(-LK // 128)
LKP = NT * 128
LAST = LK - (NT - 1) * 128
PAIR = 2 * LQ
GW = 8 * LQ
NEG = -float(2.0 ** 100)
GELU_C = 0.044715
GELU_S = 0.7978845608028654

HEADS = (32, 16, 16, 16)
HD = (8, 16, 16, 16)
SCALE = (8 ** -0.5, 0.25, 1.0 / 16, 0.25)
KEYS = (LK, LK, LK + LQ, LK)
KV = (64, 256, 256, 256)
KOFF = (0, 128, 640, 1152)
KVCOLS = 1664
STEP_W = (2, 8, 8, 8)

VP = {}
for _name, _n in (("bk0", 1), ("bk2", 2), ("bk3", 2), ("bq0", 4), ("bq2", 2), ("bq3", 2), ("g1", 2), ("b1", 2),
                  ("pw", 2), ("ln1w", 2), ("ln1b", 2), ("ln2w", 2), ("ln2b", 2), ("mb2", 8), ("mb3", 8),
                  ("hm", 8), ("hm0", 8), ("e56", LQ), ("ident", 128)):
    VP[_name] = (sum(n for _, n in VP.values()), _n)
VPW = sum(n for _, n in VP.values())
RP = {n: i for i, n in enumerate(("bv0", "bo0", "g0", "be0", "bv2", "ob2", "b22", "bv3", "cb3", "b23", "bv1"))}
RPN = 10


def units(layer):
    return ((0, 376), (752, 374)) if layer != 2 else ((0, 390), (780, 388))


def key_tiles(layer):
    t = [(128 * i, 128) for i in range(NT - 1)] + [(128 * (NT - 1), LAST)]
    return t + [(LK, LQ)] if layer == 2 else t


KCHUNKS = ((0, 512), (512, 512), (1024, LK - 1024))


def project_uses():
    s0 = []
    for c in range(3):
        s0 += [("at", c, 0), ("at", c, 1), ("k", 1, 0, c), ("k", 1, 1, c), ("v", 1, 2 * c), ("v", 1, 2 * c + 1)]
    kk = lambda l: [("k", l, g, c) for c in range(3) for g in range(2)]
    vv = lambda l: [("v", l, j) for j in range(NT // 2)]
    tail = [("ct", j) for j in range(NT // 2)] + [("k", 0, 0, c) for c in range(3)] + [("v0", j) for j in range(2)]
    return {"s0": s0, "c1": kk(2), "s2": vv(2), "c2": kk(3), "s3": vv(3), "c3": tail}


CHAIN = {
    "q0": ["xt", "q"],
    "post0": ["ot", "norm_a", "norm_b", "ont", "o"],
    "post1": ["ot", "norm", "ont", "o"],
    "post2": ["ot", "norm", "ont", "o"],
    "post3": ["ot", "norm", "ont", "o"],
    "mlp": ["yt", "up", "down"],
}


def spread(steps, uses, first=0):
    out, n, done = [], len(steps) - first, 0
    for i, s in enumerate(steps):
        out.append(s)
        if i >= first:
            want = len(uses) * (i - first + 1) // n
            out += [("p", *u) for u in uses[done:want]]
            done = want
    return out


def batch_order():
    u = project_uses()
    su = lambda l: [("s", l, p, h) for p in range(HEADS[l] // 2) for h in range(2)]
    ch = lambda l, names: [("c", l, n) for n in names]
    att = lambda l: [("m", l), ("t", l)]
    o = ch(0, ["xt", "q"])
    o += spread(su(0), u["s0"]) + att(0)
    o += ch(0, CHAIN["post0"]) + ch(1, ["xt", "q"])
    o += su(1) + att(1)
    o += spread(ch(1, CHAIN["post1"]) + ch(2, ["xt", "q", "lat"]), u["c1"])
    o += spread(su(2), u["s2"]) + att(2)
    o += spread(ch(2, CHAIN["post2"]) + ch(2, CHAIN["mlp"]) + ch(3, ["xt", "q"]), u["c2"])
    o += spread(su(3), u["s3"]) + att(3)
    o += [("pre",)]
    o += spread(ch(3, CHAIN["post3"]) + ch(3, CHAIN["mlp"]), u["c3"]) + [("ln",)]
    return o


def first_order():
    return [("pre",)] + [("p", *x) for x in project_uses()["c3"]] + [("ln",)]


ON_PE = {"xt", "q", "lat", "norm", "norm_a", "norm_b", "ont", "o", "yt", "up", "down"}


def fused_attention_kernel(nc, ctx, x, mask0, mask_bool, mask_int, w_kv, w_f, w_mlp, vecs, rows, out):
    with ExitStack() as es:
        def sb(name, shape, dt=F32):
            return es.enter_context(nc.sbuf_tensor(name, shape, dt))

        def pb(name, shape):
            return es.enter_context(nc.psum_tensor(name, shape, F32))

        score = pb("score", [128, 4, 512])
        accum = pb("accum", [128, 512])
        chain = pb("chain", [128, 512])
        proj = pb("proj", [128, 2, 512])

        raw = sb("raw", [128, NT, D])
        ctx_hi = sb("ctx_hi", [128, KT, LKP], F32R)
        ctx_lo = sb("ctx_lo", [128, KT, LKP], F32R)
        a_hi = sb("a_hi", [128, KT, 512], F32R)
        a_lo = sb("a_lo", [128, KT, 512], F32R)
        k0_hi = sb("k0_hi", [128, LK], F32R)
        k0_lo = sb("k0_lo", [128, LK], F32R)
        k_hi = sb("k_hi", [128, 2, LK + LQ], F32R)
        k_lo = sb("k_lo", [128, 2, LK + LQ], F32R)
        v0 = sb("v0", [128, NT, 8, 9])
        v = sb("v", [128, NT + 1, 16, 17])
        NPR = 3
        probs = sb("probs", [128, NPR, GW])
        q0_hi = sb("q0_hi", [128, 4 * GW], F32R)
        q_x = sb("q_x", [128, 4 * GW], F32R)
        rawmask = sb("rawmask", [128, LK])
        mask_row = sb("mask_row", [33, LK], BF16)
        mask_b = sb("mask_b", [128, LK], BF16)
        mask_i = sb("mask_i", [128, LK + LQ], BF16)
        key_bias = sb("key_bias", [128, 2, NT + 1])
        wkv_hi = sb("wkv_hi", [128, KT, KVCOLS], F32R)
        wkv_lo = sb("wkv_lo", [128, KT, KVCOLS], F32R)
        wf = sb("wf", [128, 8, KT, D])
        wmlp = sb("wmlp", [128, 4096])
        vp = sb("vp", [128, VPW])
        rp = sb("rp", [LQ, 11 * D])
        gate = sb("gate", [LQ, 1])
        tgate = sb("tgate", [LQ, 1])
        bk1 = sb("bk1", [128, 2])
        xcur = sb("xcur", [LQ, D])
        xres = sb("xres", [LQ, D])
        ya = sb("ya", [LQ, D])
        xt = sb("xt", [128, KT, LQ])
        xt_hi, xt_lo = a_hi[:, :, 0:LQ], a_lo[:, :, 0:LQ]
        hid, hu, ot, qs = probs[:, 0], probs[:, 1], probs[:, 2], probs[:, 2, 0:4 * LQ]
        ql = probs[:, 1, 0:4 * LQ]
        qh = a_hi[:, 1, 64:64 + 4 * LQ]
        row_max = sb("row_max", [PAIR, 16, 2])
        neg_max = sb("neg_max", [PAIR, 16])
        mx0_hi, mx0_lo = a_lo[0:16, 1, 0:PAIR], a_lo[0:16, 1, 128:128 + PAIR]
        diag_max = q0_hi[0:8, 0:8 * PAIR]
        ones8 = sb("ones8", [8, 128], F32R)
        one_row = rawmask[0:1, :]
        one_bf = sb("one_bf", [33, 1], BF16)
        st = sb("st", [LQ, 16])
        rec = sb("rec", [LQ, 16])
        half_pow = sb("half_pow", [128, NT])
        cst = sb("cst", [128, NT, 6])
        cmv = sb("cmv", [128, NT, 2])
        cvar = sb("cvar", [128, NT])
        crs = sb("crs", [128, NT])
        cshift = sb("cshift", [128, NT])

        def vec(name, n=None, p0=0, p1=128):
            a, w = VP[name]
            return vp[p0:p1, a:a + w] if n is None else vp[p0:p1, a + n:a + n + 1]

        def row(name):
            return rp[:, RP[name] * D:(RP[name] + 1) * D]

        ident = vec("ident")
        up_w = wmlp[:, 0:2048].rearrange("p (k n) -> p k n", k=KT)
        down_w = wmlp[:, 2048:4096].rearrange("p (t n) -> p t n", t=8)
        wq = [wf[:, 2 * l] for l in range(4)]
        wo = [wf[:, 2 * l + 1] for l in range(4)]

        def sems(*names):
            return [es.enter_context(nc.semaphore(n)) for n in names]

        (setup_loaded, setup_mem, setup_gate, setup_split, setup_pe, setup_copied, setup_row, setup_fold) = sems(
            "setup_loaded", "setup_mem", "setup_gate", "setup_split", "setup_pe", "setup_copied", "setup_row",
            "setup_fold")
        turn = sems(
            "ctx_loaded", "x_loaded", "mask_loaded", "mlp_loaded", "max_moved", "out_stored",
            "proj_ready", "proj_hi", "proj_free0", "proj_free1",
            "unit_ready", "unit_read", "max_ready", "max_turned", "max_rows",
            "step_ready", "exp_done", "pv_done",
            "chain_pe", "chain_out", "dve_link", "var_ready", "rstd_ready", "act_in", "act_out",
            "q_ready", "qlo_ready", "mask_ready", "mask_wide", "bias_ready", "bias_done",
            "stats_ready", "shift_ready", "norm_done", "mask0_done", "ln1_ready")
        (ctx_loaded, x_loaded, mask_loaded, mlp_loaded, max_moved, out_stored,
         proj_ready, proj_hi, proj_free0, proj_free1,
         unit_ready, unit_read, max_ready, max_turned, max_rows,
         step_ready, exp_done, pv_done,
         chain_pe, chain_out, dve_link, var_ready, rstd_ready, act_in, act_out,
         q_ready, qlo_ready, mask_ready, mask_wide, bias_ready, bias_done,
         stats_ready, shift_ready, norm_done, mask0_done, ln1_ready) = turn
        turn_sems = range(turn[0].num, turn[-1].num + 1)
        assert len(turn_sems) == len(turn)
        proj_free = (proj_free0, proj_free1)

        unscaled = raw[:, 4:8, :].rearrange("p (k t) d -> p k (t d)", k=KT)
        with nc.Block() as block:
            @block.sync
            def _(sp):
                sp.dma_start(wmlp[:, 0:KT * KVCOLS], w_kv).then_inc(setup_loaded, 16)
                sp.dma_start(vp[:, :], vecs).then_inc(setup_loaded, 16)
                sp.dma_start(rp[:, 0:RPN * D], rows[0:1, 0:RPN * D].broadcast_to([LQ, RPN * D])).then_inc(setup_loaded, 16)
                sp.dma_start(gate[:, :], rows[0:1, RPN * D:RPN * D + 1].broadcast_to([LQ, 1])).then_inc(setup_loaded, 16)
                sp.dma_start(wf[:, :, :, :].rearrange("p a k n -> p (a k n)"), w_f).then_inc(setup_loaded, 16)
                sp.wait_ge(setup_mem, 6)
                sp.dma_start(k0_hi[120:121, :].bitcast(F32), one_row).then_inc(setup_row, 16)
                sp.dma_start(k0_lo[121:122, :].bitcast(F32), one_row).then_inc(setup_row, 16)
                sp.wait_ge(setup_row, 32)

            @block.gpsimd
            def _(pool):
                fills = [(k0_hi[96:128, :].bitcast(F32), 0.0), (k0_lo[96:128, :].bitcast(F32), 0.0), (one_row, 1.0),
                         (ones8[:, :].bitcast(F32), 1.0), (one_bf[:, :], 1.0), (half_pow[:, :], -0.5),
                         (raw[:, NT - 1, :], 0.0),
                         (v0[:, :, :, :], 1.0), (v[:, :, :, :], 1.0),
                         (mask_i[:, LK:LK + LQ], 0.0), (key_bias[:, :, :], 0.0)]
                for n, (tile, value) in enumerate(fills):
                    nc.gpsimd.memset(tile, value).then_inc(setup_mem, 1)
                    pool.wait_ge(setup_mem, n + 1)

            @block.scalar
            def _(act):
                act.wait_ge(setup_loaded, 80)
                nc.scalar.activation(tgate[:, :], gate[:, :], ACT.Tanh).then_inc(setup_gate, 1)

            @block.vector
            def _(dve):
                nc.vector.memset(accum[:, :], 0.0).then_inc(setup_split, 1)
                dve.wait_ge(setup_loaded, 80)
                src = wmlp[:, 0:KT * KVCOLS].rearrange("p (k n) -> p k n", k=KT)
                scaled = raw[:, 0:4, :].rearrange("p (k t) d -> p k (t d)", k=KT)
                for k in range(KT):
                    nc.vector.tensor_scalar(scaled[:, k, :], src[:, k, 128:640], vec("g1", k), None,
                                            ALU.mult).then_inc(setup_split, 1)
                dve.wait_ge(setup_split, 3)
                for k in range(KT):
                    nc.vector.tensor_copy(unscaled[:, k, :], src[:, k, 128:640]).then_inc(setup_split, 1)
                dve.wait_ge(setup_split, 5)
                for k in range(KT):
                    nc.vector.tensor_copy(src[:, k, 128:640], scaled[:, k, :]).then_inc(setup_split, 1)
                dve.wait_ge(setup_split, 7)
                nc.vector.tensor_copy(wkv_hi[:, :, :], src).then_inc(setup_split, 1)
                dve.wait_ge(setup_split, 8)
                nc.vector.tensor_tensor(wkv_lo[:, :, :], src, wkv_hi[:, :, :].bitcast(F32), ALU.subtract)\
                    .then_inc(setup_split, 1)
                for k in range(KT):
                    nc.vector.tensor_copy(xt[:, k, :], vec("b1", k).broadcast_to([128, LQ])).then_inc(setup_split, 1)
                e0, _ = VP["e56"]
                eye = vp[64:64 + LQ, e0:e0 + LQ].unsqueeze(1).broadcast_to([LQ, 32, LQ])
                nc.vector.tensor_copy(q0_hi[64:64 + LQ, :].rearrange("p (h q) -> p h q", h=32), eye)\
                    .then_inc(setup_split, 1)
                dve.wait_ge(setup_pe, 2)
                nc.vector.tensor_copy(bk1[:, :], chain[:, 0:2]).then_inc(setup_fold, 1)
                nc.vector.tensor_copy(row("bv1"), chain[0:LQ, 256:512]).then_inc(setup_fold, 1)

            @block.tensor
            def _(pe):
                pe.wait_ge(setup_split, 12)
                w = unscaled
                for g in range(2):
                    for k in range(KT):
                        mm = nc.tensor.matmul(chain[:, g:g + 1], w[:, k, g * 128:(g + 1) * 128],
                                              vec("b1", k), start=(k == 0), stop=(k == KT - 1))
                mm.then_inc(setup_pe, 1)
                for k in range(KT):
                    mm = nc.tensor.matmul(chain[0:LQ, 256:512], xt[:, k, :], w[:, k, 256:512],
                                          start=(k == 0), stop=(k == KT - 1))
                mm.then_inc(setup_pe, 1)

        def turn_block(order, batch, ahead):
            looped = batch is not None
            uses, use_no = [s for s in order if s[0] == "p"], {}
            for n, s in enumerate(uses):
                use_no[s] = n
            chain_steps = [s for s in order if s[0] == "c"]
            out_before = {s: n for n, s in enumerate(chain_steps)}
            pe_before = {s: sum(t[2] in ON_PE for t in chain_steps[:n]) for n, s in enumerate(chain_steps)}
            unit_steps = [s for s in order if s[0] == "s"]
            unit_no = {s: n for n, s in enumerate(unit_steps)}
            layers = range(4) if looped else ()
            parts = lambda l: 4 if l == 0 else 2
            steps_of = [parts(l) * len(key_tiles(l)) for l in range(4)]
            steps_before = [sum(steps_of[:l]) for l in range(5)]
            units_before = [sum(HEADS[:l]) for l in range(5)]
            norm_no = {(0, "o"): 1, (2, "o"): 2, (3, "pre"): 3, (3, "o"): 5}
            ln_no = 4 if looped else 1

            def k_bias(l, g):
                return bk1[:, g:g + 1] if l == 1 else vec("bk%d" % l, g)

            with nc.Block() as block:
                @block.sync
                def _(sp):
                    if looped:
                        sp.dma_start(xcur[:, :], x[batch]).then_inc(x_loaded, 16)
                        sp.dma_start(wmlp[:, :], w_mlp[0]).then_inc(mlp_loaded, 16)
                        sp.wait_ge(proj_ready, use_no[("p", "at", 2, 1)] + 1)
                    sp.dma_start(raw[:, 0:NT - 1, :],
                                 ctx[ahead][0:128 * (NT - 1), :].rearrange("(t p) d -> p t d", p=128))\
                        .then_inc(ctx_loaded, 16)
                    sp.dma_start(raw[0:LAST, NT - 1, :], ctx[ahead][128 * (NT - 1):LK, :]).then_inc(ctx_loaded, 16)
                    sp.dma_start(rawmask[64:64 + LQ, :], mask0[ahead]).then_inc(mask_loaded, 16)
                    sp.dma_start(rawmask[0:1, :].bitcast(I32), mask_int[ahead]).then_inc(mask_loaded, 16)
                    sp.dma_start(rawmask[32:33, 0:LK // 4].bitcast(U8), mask_bool[ahead]).then_inc(mask_loaded, 16)
                    if looped:
                        sp.wait_ge(max_rows, 2)
                        sp.dma_start(q0_hi[120:121, :].bitcast(F32), mx0_hi.bitcast(F32)).then_inc(max_moved, 16)
                        sp.dma_start(q0_hi[121:122, :].bitcast(F32), mx0_lo.bitcast(F32)).then_inc(max_moved, 16)
                        sp.wait_ge(chain_pe, pe_before[("c", 2, "down")] + 1)
                        sp.dma_start(wmlp[:, :], w_mlp[1]).then_inc(mlp_loaded, 16)
                        sp.wait_ge(chain_out, out_before[("c", 3, "down")] + 1)
                        sp.dma_start(out[batch], ya[:, :]).then_inc(out_stored, 16)
                        sp.wait_ge(out_stored, 16)

                @block.gpsimd
                def _(pool):
                    def rstd(n, o, i, w):
                        pool.wait_ge(var_ready, n)
                        nc.gpsimd.tensor_tensor(o, i, w, ALU.pow).then_inc(rstd_ready, 1)
                        pool.wait_ge(rstd_ready, n)

                    for s in order:
                        if s[0] == "c" and s[2] == "q":
                            l = s[1]
                            pool.wait_ge(q_ready, l + 1)
                            if l == 0:
                                hm = vec("hm0", None, 0, 64).unsqueeze(2).broadcast_to([64, 8, 4 * LQ])
                                src = ql[0:64, :].unsqueeze(1).broadcast_to([64, 8, 4 * LQ])
                                nc.gpsimd.tensor_tensor(q_x[0:64, :].rearrange("p (h c) -> p h c", h=8), src, hm,
                                                        ALU.mult).then_inc(qlo_ready, 1)
                            else:
                                for g in range(2):
                                    hm = vec("hm").unsqueeze(2).broadcast_to([128, 8, LQ])
                                    src = ql[:, g * LQ:(g + 1) * LQ].unsqueeze(1).broadcast_to([128, 8, LQ])
                                    ins = nc.gpsimd.tensor_tensor(
                                        q_x[:, (2 + g) * GW:(3 + g) * GW].rearrange("p (h q) -> p h q", h=8),
                                        src, hm, ALU.mult)
                                ins.then_inc(qlo_ready, 1)
                            pool.wait_ge(qlo_ready, l + 1)
                        if s[0] == "c" and s[1:] in ((0, "o"), (2, "o"), (3, "o")):
                            rstd(norm_no[s[1:]], st[:, 9:10], st[:, 8:9], half_pow[0:LQ, 0:1])
                        if s[0] == "c" and s[1:] == (3, "xt"):
                            rstd(norm_no[(3, "pre")], st[:, 9:10], st[:, 8:9], half_pow[0:LQ, 0:1])
                        if s[0] == "pre":
                            pool.wait_ge(mask_ready, 2)
                            nc.gpsimd.partition_broadcast(mask_b[:, 0:LK], mask_row[32:33, :]).then_inc(mask_wide, 1)
                            pool.wait_ge(mask_wide, 1)
                            nc.gpsimd.partition_broadcast(mask_i[:, 0:LK], mask_row[0:1, :]).then_inc(mask_wide, 1)
                            pool.wait_ge(mask_wide, 2)
                            rstd(ln_no, crs[:, :], cvar[:, :], half_pow[:, :])
                        if s[0] == "ln":
                            pool.wait_ge(proj_ready, use_no[("p", "ct", NT // 2 - 1)] + 1)
                            pool.wait_ge(shift_ready, 1)
                            for t in range(NT):
                                ins = nc.gpsimd.tensor_scalar(raw[:, t, :], raw[:, t, :], crs[:, t:t + 1],
                                                              cshift[:, t:t + 1], ALU.mult, ALU.add)
                            ins.then_inc(norm_done, 1)

                @block.scalar
                def _(act):
                    def evacuate_hi(s):
                        n = use_no[s]
                        b = n % 2
                        act.wait_ge(proj_ready, n + 1)
                        kind = s[1]
                        if kind in ("ct", "at"):
                            src = proj[:, b, :].rearrange("p (t k c) -> p t k c", t=2, k=KT)
                            if kind == "ct":
                                dst = ctx_hi[:, :, s[2] * 256:(s[2] + 1) * 256]
                            else:
                                if s[2]:
                                    act.wait_ge(proj_ready, use_no[("p", "v", 1, 2 * s[2] - 1)] + 1)
                                dst = a_hi[:, :, s[3] * 256:(s[3] + 1) * 256]
                            nc.scalar.activation(dst.rearrange("p k (t c) -> p t k c", t=2), src, ACT.Copy)\
                                .then_inc(proj_hi, 1)
                        elif kind == "k":
                            l, g, c = s[2:]
                            k, w = KCHUNKS[c]
                            if l == 0:
                                nc.scalar.activation(k0_hi[0:64, k:k + w], proj[0:64, b, 0:w], ACT.Identity,
                                                     bias=vec("bk0", 0, 0, 64)).then_inc(proj_hi, 1)
                            else:
                                nc.scalar.activation(k_hi[:, g, k:k + w], proj[:, b, 0:w], ACT.Identity,
                                                     bias=k_bias(l, g)).then_inc(proj_hi, 1)
                        elif kind == "v0":
                            j = s[2]
                            nc.scalar.activation(v0[:, 6 * j:6 * j + 6, :, 0:8],
                                                 proj[:, b, 0:384].rearrange("p (t h d) -> p t h d", t=6, h=8),
                                                 ACT.Copy).then_inc(proj_free[b], 1)
                        else:
                            j = s[3]
                            nc.scalar.activation(v[:, 2 * j:2 * j + 2, :, 0:16],
                                                 proj[:, b, :].rearrange("p (t h d) -> p t h d", t=2, h=16),
                                                 ACT.Copy).then_inc(proj_free[b], 1)

                    tanh_no = 0
                    for s in order:
                        if s[0] == "p":
                            evacuate_hi(s)
                        elif s[0] == "t":
                            l = s[1]
                            for j in range(steps_before[l], steps_before[l + 1]):
                                t = (j - steps_before[l]) % len(key_tiles(l))
                                kt = key_tiles(l)[t][1]
                                act.wait_ge(step_ready, j + 1)
                                if j >= NPR:
                                    act.wait_ge(pv_done, j - NPR + 1)
                                bias = 0.0 if l == 0 else key_bias[0:kt, int(l == 2), t:t + 1]
                                nc.scalar.activation(probs[0:kt, j % NPR, :], score[0:kt, j % 4, 0:GW], ACT.Exp,
                                                     bias=bias).then_inc(exp_done, 1)
                        elif s[0] == "c" and s[2] == "up":
                            tanh_no += 1
                            act.wait_ge(act_in, tanh_no)
                            nc.scalar.activation(hu[:, :], hu[:, :], ACT.Tanh, scale=GELU_S).then_inc(act_out, 1)

                @block.vector
                def _(dve):
                    linked = [0]

                    def link(ins):
                        linked[0] += 1
                        ins.then_inc(dve_link, 1)
                        dve.wait_ge(dve_link, linked[0])

                    tt, ts, stt, cp = (nc.vector.tensor_tensor, nc.vector.tensor_scalar,
                                       nc.vector.scalar_tensor_tensor, nc.vector.tensor_copy)

                    def evacuate_lo(s):
                        n, kind = use_no[s], s[1]
                        b = n % 2
                        if kind in ("v", "v0"):
                            return
                        dve.wait_ge(proj_hi, sum(u[1] not in ("v", "v0") for u in uses[:n]) + 1)
                        if kind in ("ct", "at"):
                            src = proj[:, b, :].rearrange("p (t k c) -> p k t c", t=2, k=KT)
                            hi, lo = (ctx_hi, ctx_lo) if kind == "ct" else (a_hi, a_lo)
                            c = (s[2] if kind == "ct" else s[3]) * 256
                            for k in range(KT):
                                ins = tt(lo[:, k, c:c + 256].rearrange("p (t c) -> p t c", t=2), src[:, k],
                                         hi[:, k, c:c + 256].bitcast(F32).rearrange("p (t c) -> p t c", t=2),
                                         ALU.subtract)
                            ins.then_inc(proj_free[b], 1)
                        else:
                            l, g, c = s[2:]
                            k, w = KCHUNKS[c]
                            if l == 0:
                                stt(k0_lo[0:64, k:k + w], proj[0:64, b, 0:w], vec("bk0", 0, 0, 64),
                                    k0_hi[0:64, k:k + w].bitcast(F32), ALU.add, ALU.subtract)\
                                    .then_inc(proj_free[b], 1)
                            else:
                                stt(k_lo[:, g, k:k + w], proj[:, b, 0:w], k_bias(l, g),
                                    k_hi[:, g, k:k + w].bitcast(F32), ALU.add, ALU.subtract)\
                                    .then_inc(proj_free[b], 1)

                    def unit_max(s):
                        _, l, p, h = s
                        n = unit_no[s]
                        k, w = units(l)[h]
                        dve.wait_ge(unit_ready, n + 1)
                        src = score[0:PAIR, 2 * (n % 2):2 * (n % 2) + 2, 0:w]
                        if l == 0:
                            ins = nc.vector.tensor_reduce(row_max[:, p, h:h + 1], src, AX.XY, ALU.max)
                        else:
                            m = mask_i if l == 2 else mask_b
                            ins = nc.vector.tensor_tensor_reduce(
                                src, src,
                                m[0:PAIR, k:k + 2 * w].rearrange("p (b w) -> p b w", b=2),
                                1.0, -3.0e38, ALU.add, ALU.max, row_max[:, p, h:h + 1])
                        ins.then_inc(unit_read, 1)

                    def max_to_rows(l):
                        np_ = HEADS[l] // 2
                        dve.wait_ge(unit_read, units_before[l + 1])
                        nc.vector.tensor_reduce(neg_max[:, 0:np_], row_max[:, 0:np_, :], AX.X, ALU.max, negate=True)\
                            .then_inc(max_ready, 1)
                        dve.wait_ge(max_turned, l + 1)
                        if l == 0:
                            cp(mx0_hi[:, :], chain[0:16, 0:PAIR]).then_inc(max_rows, 1)
                            dve.wait_ge(max_rows, 1)
                            tt(mx0_lo[:, :], chain[0:16, 0:PAIR], mx0_hi[:, :].bitcast(F32), ALU.subtract)\
                                .then_inc(max_rows, 1)
                        else:
                            tt(diag_max.rearrange("p (h c) -> p h c", h=8),
                               chain[0:8, 0:PAIR].unsqueeze(1).broadcast_to([8, 8, PAIR]),
                               vec("ident", None, 0, 8)[:, 0:8].unsqueeze(2).broadcast_to([8, 8, PAIR]),
                               ALU.mult).then_inc(max_rows, 1)

                    def stats(src, n, centred):
                        if centred:
                            link(nc.vector.bn_stats(st[:, 0:6], src))
                            link(nc.vector.bn_aggr(st[:, 6:8], st[:, 0:6]))
                            ts(st[:, 8:9], st[:, 7:8], 1e-6 if n == 1 else 1e-5, None, ALU.add).then_inc(var_ready, 1)
                        else:
                            link(nc.vector.tensor_tensor_reduce(hid[0:LQ, 0:D], src, src, 1.0, 0.0, ALU.mult, ALU.add,
                                                                st[:, 7:8]))
                            ts(st[:, 8:9], st[:, 7:8], 1.0 / D, 1e-6, ALU.mult, ALU.add).then_inc(var_ready, 1)
                        dve.wait_ge(rstd_ready, n)

                    def chain_step(s):
                        _, l, name = s
                        if name in ON_PE:
                            dve.wait_ge(chain_pe, pe_before[s] + 1)
                        if out_before[s]:
                            dve.wait_ge(chain_out, out_before[s])
                        last = None
                        if name == "ot":
                            dve.wait_ge(pv_done, steps_before[l + 1])
                            w = 448 if l == 0 else 224
                            last = cp(ot[:, 0:w], accum[:, 0:w])
                        elif name in ("norm", "norm_a", "norm_b"):
                            hd, half = HD[l], (name == "norm_b")
                            full = chain[0:LQ, :].rearrange("q (c j e) -> q c j e", c=4, j=4)
                            link(nc.vector.reciprocal(rec[:, :].rearrange("q (c j) -> q c j", c=4), full[:, :, :, hd]))
                            if l == 0:
                                dst = ya[:, half * 128:half * 128 + 128].rearrange("q (j c d) -> q c j d", j=4, c=4)
                            else:
                                dst = ya[:, :].rearrange("q (c j d) -> q c j d", c=4, j=4)
                            for c in range(4):
                                ins = tt(dst[:, c], full[:, c, :, 0:hd],
                                         rec[:, 4 * c:4 * c + 4].unsqueeze(2).broadcast_to([LQ, 4, hd]), ALU.mult)
                            if name == "norm_a":
                                last = ins
                            else:
                                link(ins)
                                last = tt(ya[:, :], ya[:, :], row("bv%d" % l), ALU.add)
                        elif name == "ont":
                            last = cp(xt[:, :, :], chain[:, 0:KT * LQ].rearrange("p (k q) -> p k q", k=KT))
                        elif name == "o":
                            y = chain[0:LQ, 0:D]
                            if l == 0:
                                link(tt(ya[:, :], y, xres[:, :], ALU.add))
                                stats(ya[:, :], norm_no[(0, "o")], True)
                                link(ts(ya[:, :], ya[:, :], st[:, 6:7], st[:, 9:10], ALU.subtract, ALU.mult))
                                link(tt(ya[:, :], ya[:, :], row("g0"), ALU.mult))
                                last = tt(xcur[:, :], ya[:, :], row("be0"), ALU.add)
                            elif l == 1:
                                last = stt(xcur[:, :], y, tgate[:, 0:1], xcur[:, :], ALU.mult, ALU.add)
                            elif l == 2:
                                link(tt(ya[:, :], y, xres[:, :], ALU.add))
                                stats(ya[:, :], norm_no[(2, "o")], False)
                                last = ts(ya[:, :], ya[:, :], st[:, 9:10], None, ALU.mult)
                            else:
                                link(tt(xcur[:, :], y, xres[:, :], ALU.add))
                                stats(xcur[:, :], norm_no[(3, "o")], True)
                                last = ts(ya[:, :], xcur[:, :], st[:, 6:7], st[:, 9:10], ALU.subtract, ALU.mult)
                        elif name == "yt":
                            src = chain[:, 0:KT * LQ].rearrange("p (k q) -> p k q", k=KT)
                            for k in range(KT):
                                if l == 2:
                                    last = ts(xt[:, k, :], src[:, k, :], vec("pw", k), None, ALU.mult)
                                else:
                                    last = ts(xt[:, k, :], src[:, k, :], vec("ln2w", k), vec("ln2b", k),
                                              ALU.mult, ALU.add)
                        elif name == "up":
                            b = vec("mb%d" % l).unsqueeze(2).broadcast_to([128, 8, LQ])
                            link(tt(hid[:, :].rearrange("p (t q) -> p t q", t=8),
                                    chain[:, 0:GW].rearrange("p (t q) -> p t q", t=8), b, ALU.add))
                            link(tt(hu[:, :], hid[:, :], hid[:, :], ALU.mult))
                            link(ts(hu[:, :], hu[:, :], GELU_C, 1.0, ALU.mult, ALU.add))
                            tt(hu[:, :], hu[:, :], hid[:, :], ALU.mult).then_inc(act_in, 1)
                            dve.wait_ge(act_out, 1 if l == 2 else 2)
                            last = stt(hid[:, :], hu[:, :], 1.0, hid[:, :], ALU.add, ALU.mult)
                        elif name == "down":
                            link(tt(xres[:, :], xcur[:, :], row("b22" if l == 2 else "b23"), ALU.add))
                            last = stt(xcur[:, :] if l == 2 else ya[:, :], chain[0:LQ, 0:D], 0.5, xres[:, :],
                                       ALU.mult, ALU.add)
                        elif name == "xt":
                            src = chain[:, 0:KT * LQ].rearrange("p (k q) -> p k q", k=KT)
                            if l == 3:
                                for k in range(KT):
                                    last = ts(xt[:, k, :], src[:, k, :], vec("ln1w", k), vec("ln1b", k),
                                              ALU.mult, ALU.add)
                            elif l == 2:
                                link(cp(xt[:, :, :], src))
                                link(cp(xt_hi, xt[:, :, :]))
                                last = tt(xt_lo, xt[:, :, :], xt_hi.bitcast(F32), ALU.subtract)
                            else:
                                last = cp(xt[:, :, :], src)
                        elif name == "q":
                            if l == 0:
                                dst, p, n = q0_hi[0:64, :], 64, 4
                                hm = vec("hm0", None, 0, 64).unsqueeze(2).broadcast_to([64, 8, 4 * LQ])
                            else:
                                dst, p, n = None, 128, 2
                            w = n * LQ
                            if l == 1:
                                link(ts(qs[:, 0:w], chain[:, 0:w], SCALE[l], None, ALU.mult))
                            else:
                                for g in range(n):
                                    ins = ts(qs[0:p, g * LQ:(g + 1) * LQ], chain[0:p, g * LQ:(g + 1) * LQ],
                                             vec("bq%d" % l, g, 0, p), SCALE[l], ALU.add, ALU.mult)
                                link(ins)
                            link(cp(qh[0:p, 0:w], qs[0:p, 0:w]))
                            if l:
                                dve.wait_ge(qlo_ready, l)
                            tt(ql[0:p, 0:w], qs[0:p, 0:w], qh[0:p, 0:w].bitcast(F32), ALU.subtract)\
                                .then_inc(q_ready, 1)
                            if l == 0:
                                last = tt(dst.rearrange("p (h c) -> p h c", h=8),
                                          qh[0:64, :].bitcast(F32).unsqueeze(1).broadcast_to([64, 8, 4 * LQ]), hm,
                                          ALU.mult)
                            else:
                                for g in range(2):
                                    last = tt(q_x[:, g * GW:(g + 1) * GW].rearrange("p (h q) -> p h q", h=8),
                                              qh[:, g * LQ:(g + 1) * LQ].bitcast(F32).unsqueeze(1)
                                              .broadcast_to([128, 8, LQ]),
                                              vec("hm").unsqueeze(2).broadcast_to([128, 8, LQ]), ALU.mult)
                        elif name == "lat":
                            for g in range(2):
                                link(ts(qs[:, g * LQ:(g + 1) * LQ], chain[:, g * LQ:(g + 1) * LQ],
                                        vec("bk2", g), None, ALU.add))
                            for g in range(2):
                                link(cp(k_hi[:, g, LK:LK + LQ], qs[:, g * LQ:(g + 1) * LQ]))
                            for g in range(2):
                                tt(k_lo[:, g, LK:LK + LQ], qs[:, g * LQ:(g + 1) * LQ],
                                   k_hi[:, g, LK:LK + LQ].bitcast(F32), ALU.subtract)
                            last = cp(v[0:LQ, NT, :, 0:16], chain[0:LQ, 256:512].rearrange("q (h d) -> q h d", h=16))
                        last.then_inc(chain_out, 1)

                    def before(s):
                        _, l, name = s
                        if name == "xt":
                            if l == 0:
                                dve.wait_ge(x_loaded, 16)
                                tt(xres[:, :], xcur[:, :], row("bo0"), ALU.add)
                            elif l in (2, 3):
                                if out_before[s]:
                                    dve.wait_ge(chain_out, out_before[s])
                                ins = tt(xres[:, :], xcur[:, :], row("ob2" if l == 2 else "cb3"), ALU.add)
                                if l == 3:
                                    stats(xcur[:, :], norm_no[(3, "pre")], True)
                                    ts(ya[:, :], xcur[:, :], st[:, 6:7], st[:, 9:10], ALU.subtract, ALU.mult)\
                                        .then_inc(ln1_ready, 1)

                    for s in order:
                        if s[0] == "p":
                            evacuate_lo(s)
                        elif s[0] == "s":
                            unit_max(s)
                        elif s[0] == "m":
                            max_to_rows(s[1])
                        elif s[0] == "c":
                            before(s)
                            chain_step(s)
                        elif s[0] == "pre":
                            dve.wait_ge(mask_loaded, 48)
                            link(cp(k0_hi[64:64 + LQ, :], rawmask[64:64 + LQ, :]))
                            tt(k0_lo[64:64 + LQ, :], rawmask[64:64 + LQ, :], k0_hi[64:64 + LQ, :].bitcast(F32),
                               ALU.subtract).then_inc(mask0_done, 1)
                            ts(mask_row[0:1, :], rawmask[0:1, :].bitcast(I32), 0, NEG, ALU.is_equal, ALU.mult)\
                                .then_inc(mask_ready, 1)
                            ts(mask_row[32:33, :], rawmask[32:33, 0:LK // 4].bitcast(U8), 0, NEG, ALU.is_equal,
                               ALU.mult).then_inc(mask_ready, 1)
                            dve.wait_ge(bias_ready, 1)
                            if looped:
                                dve.wait_ge(exp_done, steps_before[4])
                            for m in range(2):
                                src = (score[:, 0], chain)[m]
                                cp(key_bias[:, m, 0:NT - 1], src[:, 0:NT - 1])
                                ins = cp(key_bias[0:LAST, m, NT - 1:NT], src[0:LAST, NT - 1:NT])
                            ins.then_inc(bias_done, 1)
                            dve.wait_ge(ctx_loaded, 32)
                            for t in range(NT):
                                ins = nc.vector.bn_stats(cst[:, t, :], raw[:, t, :])
                            link(ins)
                            for t in range(NT):
                                ins = nc.vector.bn_aggr(cmv[:, t, :], cst[:, t, :])
                            link(ins)
                            ts(cvar[:, :], cmv[:, :, 1], 1e-5, None, ALU.add).then_inc(var_ready, 1)
                        elif s[0] == "ln":
                            dve.wait_ge(rstd_ready, ln_no)
                            stt(cshift[:, :], cmv[:, :, 0], -1.0, crs[:, :], ALU.mult, ALU.mult)\
                                .then_inc(shift_ready, 1)

                @block.tensor
                def _(pe):
                    mm = nc.tensor.matmul

                    def mm3(o, lh, ll, rh, rl, first=True, last=True):
                        mm(o, lh, rh, start=first, stop=False)
                        mm(o, ll, rh, start=False, stop=False)
                        return mm(o, lh, rl, start=False, stop=last)

                    def project(s):
                        n, kind = use_no[s], s[1]
                        b = n % 2
                        if n >= 2:
                            pe.wait_ge(proj_free[b], n // 2)
                        if kind in ("ct", "at"):
                            if kind == "ct":
                                pe.wait_ge(ctx_loaded, 32)
                            t0 = 2 * s[2] if kind == "ct" else 4 * s[2] + 2 * s[3]
                            for t in range(2):
                                for k in range(KT):
                                    ins = nc.tensor.transpose(proj[:, b, (2 * t + k) * 128:(2 * t + k + 1) * 128],
                                                              raw[:, t0 + t, k * 128:(k + 1) * 128], ident)
                        elif kind == "k":
                            l, g, c = s[2:]
                            k0, w = KCHUNKS[c]
                            m = min(KV[l], 128)
                            if l == 1:
                                sh, sl, at = a_hi, a_lo, 0
                                wait_lo(("p", "at", c, 1))
                            else:
                                sh, sl, at = ctx_hi, ctx_lo, k0
                                if l == 0:
                                    wait_lo(("p", "ct", NT // 2 - 1))
                            o = KOFF[l] + g * 128
                            for k in range(KT):
                                ins = mm3(proj[0:m, b, 0:w], wkv_hi[:, k, o:o + m], wkv_lo[:, k, o:o + m],
                                          sh[:, k, at:at + w], sl[:, k, at:at + w], k == 0, k == KT - 1)
                        else:
                            if kind == "v0":
                                l, tiles, o = 0, range(6 * s[2], 6 * s[2] + 6), KOFF[0] + 64
                            else:
                                l, tiles, o = s[2], range(2 * s[3], 2 * s[3] + 2), KOFF[s[2]] + 256
                            for i, t in enumerate(tiles):
                                if l == 1:
                                    sh, sl, at = a_hi, a_lo, (t % 4) * 128
                                else:
                                    sh, sl, at = ctx_hi, ctx_lo, t * 128
                                w = KV[l]
                                for k in range(KT):
                                    ins = mm3(proj[:, b, i * w:(i + 1) * w], sh[:, k, at:at + 128],
                                              sl[:, k, at:at + 128], wkv_hi[:, k, o:o + w], wkv_lo[:, k, o:o + w],
                                              k == 0, k == KT - 1)
                        ins.then_inc(proj_ready, 1)

                    def wait_lo(s):
                        n = use_no[s]
                        pe.wait_ge(proj_free[n % 2], n // 2 + 1)
                        pe.wait_ge(proj_free[1 - n % 2], (n + 1) // 2)

                    def score_unit(s):
                        _, l, p, h = s
                        n = unit_no[s]
                        if p == 0 and h == 0:
                            if l:
                                pe.wait_ge(exp_done, steps_before[l])
                            pe.wait_ge(chain_out, out_before[("c", l, "q")] + 1)
                            if l == 2:
                                pe.wait_ge(chain_out, out_before[("c", 2, "lat")] + 1)
                            if l:
                                wait_k(l)
                        if n >= 2:
                            pe.wait_ge(unit_read, n - 1)
                        k, w = units(l)[h]
                        for b in range(2):
                            o = score[0:PAIR, 2 * (n % 2) + b, 0:w]
                            c = k + b * w
                            if l == 0:
                                q = q0_hi[0:120, p * PAIR:(p + 1) * PAIR]
                                mm(o, q, k0_hi[0:120, c:c + w], start=True, stop=False)
                                ins = mm(o, q, k0_lo[0:120, c:c + w], start=False, stop=True)
                            else:
                                ins = mm(o, q_x[:, p * PAIR:(p + 1) * PAIR], k_hi[:, p // 4, c:c + w],
                                         start=True, stop=True)
                        ins.then_inc(unit_ready, 1)

                    def wait_k(l):
                        wait_lo(("p", "k", l, 1, 2))

                    def wait_v(l):
                        u = ("p", "v", l, NT // 2 - 1)
                        wait_lo(u)

                    def turn_max(l):
                        np_ = HEADS[l] // 2
                        pe.wait_ge(max_ready, l + 1)
                        last = [t for t in chain_steps[:] if order.index(t) < order.index(("m", l))][-1]
                        pe.wait_ge(chain_out, out_before[last] + 1)
                        nc.tensor.transpose(chain[0:np_, 0:PAIR], neg_max[:, 0:np_], ident[0:PAIR, 0:PAIR])\
                            .then_inc(max_turned, 1)

                    def attend(l):
                        tiles = key_tiles(l)
                        nt = len(tiles)
                        n0, n1 = steps_before[l], steps_before[l + 1]
                        kvh, hd = STEP_W[l], HD[l]
                        cols = GW // kvh
                        vt = v0 if l == 0 else v
                        if l == 0:
                            pe.wait_ge(max_moved, 32)
                        pe.wait_ge(max_rows, l + 2)
                        pe.wait_ge(qlo_ready, l + 1)
                        pe.wait_ge(unit_read, units_before[l + 1])
                        if l:
                            wait_v(l)
                            pe.wait_ge(chain_out, out_before[("c", l - 1, "ot")] + 1)
                        opened = set()

                        def scores_t(j):
                            g, t = divmod(j - n0, nt)
                            k, kn = tiles[t]
                            if j - n0 >= 4:
                                pe.wait_ge(exp_done, j - 3)
                            o = score[0:kn, j % 4, 0:GW]
                            if l == 0:
                                q = q0_hi[0:122, g * GW:(g + 1) * GW]
                                mm(o, k0_hi[0:122, k:k + kn], q, start=True, stop=False)
                                mm(o, k0_lo[0:122, k:k + kn], q, start=False, stop=False)
                                ins = mm(o, k0_hi[0:64, k:k + kn], q_x[0:64, g * GW:(g + 1) * GW],
                                         start=False, stop=True)
                            else:
                                mm3(o, k_hi[:, g, k:k + kn], k_lo[:, g, k:k + kn],
                                    q_x[:, g * GW:(g + 1) * GW], q_x[:, (2 + g) * GW:(3 + g) * GW], True, False)
                                ins = mm(o, ones8[:, 0:kn], diag_max[:, g * GW:(g + 1) * GW], start=False, stop=True)
                            ins.then_inc(step_ready, 1)

                        def values(j):
                            g, t = divmod(j - n0, nt)
                            kn = tiles[t][1]
                            pe.wait_ge(exp_done, j + 1)
                            for i in range(kvh):
                                h = g * kvh + i
                                quad, c = h % 4, (h // 4) * cols
                                ins = mm(accum[32 * quad:32 * quad + hd + 1, c:c + cols], vt[0:kn, t, h, :],
                                         probs[0:kn, j % NPR, i * cols:(i + 1) * cols],
                                         start=quad not in opened, stop=(t == nt - 1), skip_group_check=True)
                                opened.add(quad)
                            ins.then_inc(pv_done, 1)

                        for j in range(n0, n1 + 2):
                            if j < n1:
                                scores_t(j)
                            if j >= n0 + 2:
                                values(j - 2)

                    def chain_part(s):
                        _, l, name = s
                        if name not in ON_PE:
                            return
                        if name == "xt":
                            if l == 0:
                                pe.wait_ge(x_loaded, 16)
                            if l == 3:
                                pe.wait_ge(ln1_ready, 1)
                        if out_before[s]:
                            pe.wait_ge(chain_out, out_before[s])
                        if name in ("norm", "norm_a", "norm_b"):
                            base = 4 if name == "norm_b" else 0
                            for c in range(4):
                                ins = nc.tensor.transpose(chain[0:LQ, c * 128:(c + 1) * 128],
                                                          ot[:, (base + c) * LQ:(base + c + 1) * LQ], ident)
                        elif name in ("xt", "ont", "yt"):
                            src = xcur if name == "xt" and l != 3 else ya
                            for k in range(KT):
                                ins = nc.tensor.transpose(chain[:, k * LQ:(k + 1) * LQ],
                                                          src[:, k * 128:(k + 1) * 128], ident[0:LQ, 0:LQ])
                        elif name == "o":
                            for k in range(KT):
                                ins = mm(chain[0:LQ, 0:D], xt[:, k, :], wo[l][:, k, :], start=(k == 0),
                                         stop=(k == KT - 1))
                        elif name == "q":
                            n, m = (4, 64) if l == 0 else (2, 128)
                            for g in range(n):
                                for k in range(KT):
                                    ins = mm(chain[0:m, g * LQ:(g + 1) * LQ], wq[l][:, k, g * m:(g + 1) * m],
                                             xt[:, k, :], start=(k == 0), stop=(k == KT - 1))
                        elif name == "lat":
                            o = KOFF[2]
                            for g in range(2):
                                for k in range(KT):
                                    mm3(chain[:, g * LQ:(g + 1) * LQ], wkv_hi[:, k, o + g * 128:o + (g + 1) * 128],
                                        wkv_lo[:, k, o + g * 128:o + (g + 1) * 128], xt_hi[:, k, :], xt_lo[:, k, :],
                                        k == 0, k == KT - 1)
                            for k in range(KT):
                                ins = mm3(chain[0:LQ, 256:512], xt_hi[:, k, :], xt_lo[:, k, :],
                                          wkv_hi[:, k, o + 256:o + 512], wkv_lo[:, k, o + 256:o + 512],
                                          k == 0, k == KT - 1)
                        elif name == "up":
                            pe.wait_ge(mlp_loaded, 16 if l == 2 else 32)
                            for t in range(8):
                                for k in range(KT):
                                    ins = mm(chain[:, t * LQ:(t + 1) * LQ], up_w[:, k, t * 128:(t + 1) * 128],
                                             xt[:, k, :], start=(k == 0), stop=(k == KT - 1))
                        elif name == "down":
                            for t in range(8):
                                ins = mm(chain[0:LQ, 0:D], hid[:, t * LQ:(t + 1) * LQ], down_w[:, t, :],
                                         start=(t == 0), stop=(t == 7))
                        ins.then_inc(chain_pe, 1)

                    for s in order:
                        if s[0] == "p":
                            project(s)
                        elif s[0] == "s":
                            score_unit(s)
                        elif s[0] == "m":
                            turn_max(s[1])
                        elif s[0] == "t":
                            attend(s[1])
                        elif s[0] == "c":
                            chain_part(s)
                        elif s[0] == "pre":
                            if chain_steps and looped:
                                last = [t for t in chain_steps if order.index(t) < order.index(s)][-1]
                                pe.wait_ge(chain_out, out_before[last] + 1)
                                pe.wait_ge(exp_done, steps_before[4])
                            pe.wait_ge(mask_ready, 2)
                            for m, (tile, p) in enumerate(((mask_row, 32), (mask_row, 0))):
                                for t, (k, kn) in enumerate(key_tiles(0)):
                                    ins = mm((score[:, 0], chain)[m][0:kn, t:t + 1], tile[p:p + 1, k:k + kn],
                                             one_bf[p:p + 1, :], start=True, stop=True)
                            ins.then_inc(bias_ready, 1)

            nc.all_engine_barrier(sems_to_clear=turn_sems)

        turn_block(first_order(), None, 0)
        with nc.Fori(0, NB) as i:
            turn_block(batch_order(), i, (i + 1) % NB)


def kernel(**inputs):
    import numpy as np
    import concourse.bacc as bacc
    from concourse.bass_utils import run_bass_kernel_spmd

    a = {n: np.asarray(v) for n, v in inputs.items()}
    P = lambda l, n: a["L%d_xattn_%s" % (l, n)]
    rows_of = lambda w: w.reshape(-1, 128, w.shape[1]).transpose(1, 0, 2).reshape(128, -1)

    kv2 = P(2, "kv_w").reshape(D, D, 2)
    w_kv = np.concatenate([P(0, "Wk"), P(0, "Wv"), P(1, "Wk").T, P(1, "Wv").T, kv2[..., 0], kv2[..., 1],
                           P(3, "k_w"), P(3, "v_w")], 1)
    wq0 = P(0, "Wq").reshape(D, 8, 4, 8).transpose(0, 2, 1, 3).reshape(D, D)
    w_f = [wq0, P(0, "Wo"), P(1, "Wq").T, P(1, "Wo").T, P(2, "q_w"), P(2, "out_w"), P(3, "q_w"), P(3, "cproj_w")]
    w_mlp = [np.concatenate([rows_of(P(2, "mlp_w1")), rows_of(P(2, "mlp_w2"))], 1),
             np.concatenate([rows_of(P(3, "fc_w")), rows_of(P(3, "proj_w"))], 1)]

    kvb = P(2, "kv_b").reshape(D, 2)
    bk0 = np.zeros((128, 1), np.float32)
    bk0[0:64, 0] = P(0, "bk")
    bq0 = np.zeros((128, 4), np.float32)
    bq0[0:64] = P(0, "bq").reshape(8, 4, 8).transpose(0, 2, 1).reshape(64, 4)
    by = lambda b: b.reshape(-1, 128).T
    part = np.arange(128)
    hm = (part[:, None] // 16 == np.arange(8)).astype(np.float32)
    hm0 = (part[:, None] // 8 == np.arange(8)).astype(np.float32)
    e56 = (part[:, None] - 64 == np.arange(LQ)).astype(np.float32)
    vecs = {"bk0": bk0, "bk2": by(kvb[:, 0]), "bk3": by(P(3, "k_b")), "bq0": bq0, "bq2": by(P(2, "q_b")),
            "bq3": by(P(3, "q_b")), "g1": by(P(1, "ln_gamma")), "b1": by(P(1, "ln_beta")),
            "pw": by(P(2, "postnorm_w")), "ln1w": by(P(3, "ln1_w")), "ln1b": by(P(3, "ln1_b")),
            "ln2w": by(P(3, "ln2_w")), "ln2b": by(P(3, "ln2_b")), "mb2": by(P(2, "mlp_b1")),
            "mb3": by(P(3, "fc_b")), "hm": hm, "hm0": hm0, "e56": e56, "ident": np.eye(128, dtype=np.float32)}
    bv0 = np.broadcast_to(P(0, "bv").reshape(8, 1, 8), (8, 4, 8)).reshape(D)
    rows = [bv0, P(0, "bo"), P(0, "gamma"), P(0, "beta"), kvb[:, 1], P(2, "out_b"), P(2, "mlp_b2"),
            P(3, "v_b"), P(3, "cproj_b"), P(3, "proj_b"), P(1, "gate")]
    arrays = {
        "ctx": a["ctx_2048"], "x": a["x"], "mask0": a["mask_Bx1xSxS2_ff0"].reshape(NB, LQ, LK),
        "mask_bool": a["mask_BxS2_bf1"].view(np.uint8).reshape(NB, 1, LK),
        "mask_int": a["mask_BxS2_ik0"].reshape(NB, 1, LK),
        "w_kv": rows_of(w_kv), "w_f": np.concatenate([rows_of(w) for w in w_f], 1), "w_mlp": np.stack(w_mlp),
        "vecs": np.concatenate([vecs[n] for n in VP], 1), "rows": np.concatenate(rows)[None],
    }
    arrays = {n: np.ascontiguousarray(v) for n, v in arrays.items()}
    nc = bacc.Bacc("TRN2", target_bir_lowering=False, num_devices=1)
    args = [nc.dram_tensor(n + "_dram", v.shape, mybir.dt.from_np(v.dtype), kind="ExternalInput").ap()
            for n, v in arrays.items()]
    out = nc.dram_tensor("out_dram", (NB, LQ, D), F32, kind="ExternalOutput").ap()
    fused_attention_kernel(nc, *args, out)
    r = run_bass_kernel_spmd(nc, [{n + "_dram": v for n, v in arrays.items()}], core_ids=[0])
    return r.results[0]["out_dram"]
```

```python
from contextlib import ExitStack

import concourse.bass as bass
from concourse import mybir

F32 = mybir.dt.float32
F32R = mybir.dt.float32r
BF16 = mybir.dt.bfloat16
U8 = mybir.dt.uint8
I32 = mybir.dt.int32
ALU = mybir.AluOpType
ACT = mybir.ActivationFunctionType
AX = mybir.AxisListType

NB = 8
LQ = 56
LK = 1500
D = 256
KT = D // 128
NT = -(-LK // 128)
LKP = NT * 128
LAST = LK - (NT - 1) * 128
PAIR = 2 * LQ
GW = 8 * LQ
NEG = -float(2.0 ** 100)
GELU_C = 0.044715
GELU_S = 0.7978845608028654

HEADS = (32, 16, 16, 16)
GROUPS = (4, 2, 2, 2)
SCALE = (8 ** -0.5, 0.25, 1.0 / 16, 0.25)
KEYS = (LK, LK, LK + LQ, LK)
KV = (64, 256, 256, 256)
KOFF = (0, 128, 640, 1152)
KVCOLS = 1664

VP = {}
for _name, _n in (("bk0", 1), ("bk2", 2), ("bk3", 2), ("bq0", 4), ("bq2", 2), ("bq3", 2), ("g1", 2), ("b1", 2),
                  ("pw", 2), ("ln1w", 2), ("ln1b", 2), ("ln2w", 2), ("ln2b", 2), ("mb2", 8), ("mb3", 8),
                  ("hm", 8), ("hm0", 8), ("e56", LQ), ("ident", 128)):
    VP[_name] = (sum(n for _, n in VP.values()), _n)
VPW = sum(n for _, n in VP.values())
RP = {n: i for i, n in enumerate(("bv0", "bo0", "g0", "be0", "bv2", "ob2", "b22", "bv3", "cb3", "b23", "bv1"))}
RPN = 10


def units(layer):
    return ((0, 376), (752, 374)) if layer != 2 else ((0, 390), (780, 388))


def key_tiles(layer):
    t = [(128 * i, 128) for i in range(NT - 1)] + [(128 * (NT - 1), LAST)]
    return t + [(LK, LQ)] if layer == 2 else t


KCHUNKS = ((0, 512), (512, 512), (1024, LK - 1024))


def project_uses():
    def chunk(c):
        return [("at", c, 0), ("at", c, 1), ("k", 1, 0, c), ("k", 1, 1, c), ("v", 1, 2 * c), ("v", 1, 2 * c + 1)]

    both = lambda l: ([("k", l, g, c) for c in range(3) for g in range(2)] + [("v", l, j) for j in range(NT // 2)])
    ahead = [("ct", j) for j in range(NT // 2)] + [("k", 0, 0, c) for c in range(3)] + [("v0", j) for j in range(2)]
    return {"c0": chunk(1) + chunk(2), "c1": both(2), "c2": both(3), "c3": ahead + chunk(0)}


CHAIN = {
    "post0": ["ot", "norm_a", "norm_b", "ont", "o"],
    "post1": ["ot", "norm", "ont", "o"],
    "post2": ["ot", "norm", "ont", "o"],
    "post3": ["ot", "norm", "ont", "o"],
    "mlp": ["yt", "up", "down"],
}


def spread(steps, uses):
    out, done = [], 0
    for i, s in enumerate(steps):
        out.append(s)
        want = len(uses) * (i + 1) // len(steps)
        out += [("p", *u) for u in uses[done:want]]
        done = want
    return out


def with_norm(steps):
    at = steps.index(("p", "ct", NT // 2 - 1))
    steps = steps[:at + 1] + [("ln",)] + steps[at + 1:]
    at = max(steps.index(("p", "v0", 1)), steps.index(("q0",))) + 1
    units = score_steps(0, 0)
    head, rest = steps[:at], steps[at:]
    for i, s in enumerate(rest):
        head.append(s)
        if i < len(units):
            head.append(units[i])
    return head + units[len(rest):] + [("m", 0, 0)]


def score_steps(layer, group):
    return [("s", layer, p, h) for p in range(4 * group, 4 * group + 4) for h in range(2)]


def attend_steps(layer):
    out = []
    for g in range(GROUPS[layer]):
        ahead = score_steps(layer, g + 1) if g + 1 < GROUPS[layer] else []
        for t in range(len(key_tiles(layer))):
            out.append(("t", layer, g, t))
            out += ahead[t:t + 1]
            if ahead and t == len(ahead) + 1:
                out.append(("m", layer, g + 1))
    return out + [("te", layer)]


def batch_order():
    u = project_uses()
    ch = lambda l, names: [("c", l, n) for n in names]
    first = lambda l: score_steps(l, 0) + [("m", l, 0)]
    o = attend_steps(0)
    o += spread(ch(0, CHAIN["post0"]) + ch(1, ["xt", "q"]), u["c0"]) + first(1) + attend_steps(1)
    o += spread(ch(1, CHAIN["post1"]) + ch(2, ["xt", "q", "lat"]), u["c1"]) + first(2) + attend_steps(2)
    o += spread(ch(2, CHAIN["post2"]) + ch(2, CHAIN["mlp"]) + ch(3, ["xt", "q"]), u["c2"]) + first(3)
    o += attend_steps(3)
    o += [("pre",)]
    tail = ch(3, CHAIN["post3"]) + ch(3, CHAIN["mlp"])
    return o + with_norm(spread(tail[:2] + [("xt0",), ("q0",)] + tail[2:], u["c3"]))


def first_order():
    return [("pre",)] + with_norm(spread([("xt0",), ("q0",)], project_uses()["c3"]))


ON_PE = {"xt", "q", "lat", "norm", "norm_a", "norm_b", "ont", "o", "yt", "up", "down"}


def fused_attention_kernel(nc, ctx, x, mask0, mask_bool, mask_int, w_kv, w_f, w_mlp, vecs, rows, out):
    with ExitStack() as es:
        def sb(name, shape, dt=F32):
            return es.enter_context(nc.sbuf_tensor(name, shape, dt))

        def pb(name, shape):
            return es.enter_context(nc.psum_tensor(name, shape, F32))

        score = pb("score", [128, 4, 512])
        accum = pb("accum", [128, 512])
        chain = pb("chain", [128, 512])
        proj = pb("proj", [128, 2, 512])

        raw = sb("raw", [128, NT, D])
        ctx_hi = sb("ctx_hi", [128, KT, LKP], F32R)
        ctx_lo = sb("ctx_lo", [128, KT, LKP], F32R)
        a_hi = sb("a_hi", [128, KT, 512], F32R)
        a_lo = sb("a_lo", [128, KT, 512], F32R)
        k0_hi = sb("k0_hi", [128, LK], F32R)
        k0_lo = sb("k0_lo", [128, LK], F32R)
        k_hi = sb("k_hi", [128, 2, LK + LQ], F32R)
        k_lo = sb("k_lo", [128, 2, LK + LQ], F32R)
        v0 = sb("v0", [128, NT, 8, 9])
        v = sb("v", [128, NT + 1, 16, 17])
        NPR = 4
        probs = sb("probs", [128, NPR, GW])
        q0_hi = sb("q0_hi", [128, 4 * GW], F32R)
        q_x = sb("q_x", [128, 4 * GW], F32R)
        rawmask = sb("rawmask", [128, LK])
        mask_row = sb("mask_row", [33, LK], BF16)
        mask_b = sb("mask_b", [128, LK], BF16)
        mask_i = sb("mask_i", [128, LK + LQ], BF16)
        key_bias = sb("key_bias", [128, 2, NT + 1])
        wkv_hi = sb("wkv_hi", [128, KT, KVCOLS], F32R)
        wkv_lo = sb("wkv_lo", [128, KT, KVCOLS], F32R)
        wf = sb("wf", [128, 8, KT, D])
        wmlp = sb("wmlp", [128, 4096])
        vp = sb("vp", [128, VPW])
        rp = sb("rp", [LQ, 11 * D])
        gate = sb("gate", [LQ, 1])
        tgate = sb("tgate", [LQ, 1])
        bk1 = sb("bk1", [128, 2])
        xcur = sb("xcur", [LQ, D])
        xres = sb("xres", [LQ, D])
        ya = sb("ya", [LQ, D])
        xt = sb("xt", [128, KT, LQ])
        x_next = sb("x_next", [LQ, D])
        xt_next = sb("xt_next", [128, KT, LQ])
        xres0 = sb("xres0", [LQ, D])
        q0s = sb("q0s", [64, 4 * LQ])
        xt_hi, xt_lo = a_hi[:, :, 0:LQ], a_lo[:, :, 0:LQ]
        hid, hu, ot, qs = probs[:, 0], probs[:, 1], probs[:, 2], probs[:, 2, 0:4 * LQ]
        ql = sb("ql", [128, 4 * LQ])
        qh = sb("qh", [128, 4 * LQ], F32R)
        row_max = sb("row_max", [PAIR, 16, 2])
        neg_max = sb("neg_max", [PAIR, 16])
        mx0_hi, mx0_lo = sb("mx0_hi", [4, 4, PAIR], F32R), sb("mx0_lo", [4, 4, PAIR], F32R)
        diag_max = q0_hi[0:4, 0:8 * PAIR]
        ones4 = sb("ones4", [4, 128], F32R)
        one_row = rawmask[0:1, :]
        one_bf = sb("one_bf", [33, 1], BF16)
        st = sb("st", [LQ, 16])
        rec = sb("rec", [LQ, 16])
        half_pow = sb("half_pow", [128, NT])
        cst = sb("cst", [128, NT, 6])
        cmv = sb("cmv", [128, NT, 2])
        cvar = sb("cvar", [128, NT])
        crs = sb("crs", [128, NT])
        cshift = sb("cshift", [128, NT])

        def vec(name, n=None, p0=0, p1=128):
            a, w = VP[name]
            return vp[p0:p1, a:a + w] if n is None else vp[p0:p1, a + n:a + n + 1]

        def row(name):
            return rp[:, RP[name] * D:(RP[name] + 1) * D]

        ident = vec("ident")
        up_w = wmlp[:, 0:2048].rearrange("p (k n) -> p k n", k=KT)
        down_w = wmlp[:, 2048:4096].rearrange("p (t n) -> p t n", t=8)
        wq = [wf[:, 2 * l] for l in range(4)]
        wo = [wf[:, 2 * l + 1] for l in range(4)]

        def sems(*names):
            return [es.enter_context(nc.semaphore(n)) for n in names]

        (setup_loaded, setup_mem, setup_gate, setup_split, setup_pe, setup_copied, setup_row, setup_fold) = sems(
            "setup_loaded", "setup_mem", "setup_gate", "setup_split", "setup_pe", "setup_copied", "setup_row",
            "setup_fold")
        turn = sems(
            "ctx_loaded", "x_loaded", "mask_loaded", "mlp_loaded", "max_moved", "out_stored",
            "proj_ready", "proj_hi", "proj_free0", "proj_free1",
            "unit_ready", "unit_read", "max_ready", "max_turned", "max_rows",
            "step_ready", "exp_done", "pv_done",
            "chain_pe", "chain_out", "dve_link", "var_ready", "rstd_ready", "act_in", "act_out",
            "q_ready", "qlo_ready", "mask_ready", "mask_wide", "bias_ready", "bias_done",
            "stats_ready", "shift_ready", "norm_done", "mask0_done", "ln1_ready", "q0_pe", "q0_out")
        (ctx_loaded, x_loaded, mask_loaded, mlp_loaded, max_moved, out_stored,
         proj_ready, proj_hi, proj_free0, proj_free1,
         unit_ready, unit_read, max_ready, max_turned, max_rows,
         step_ready, exp_done, pv_done,
         chain_pe, chain_out, dve_link, var_ready, rstd_ready, act_in, act_out,
         q_ready, qlo_ready, mask_ready, mask_wide, bias_ready, bias_done,
         stats_ready, shift_ready, norm_done, mask0_done, ln1_ready, q0_pe, q0_out) = turn
        turn_sems = range(turn[0].num, turn[-1].num + 1)
        assert len(turn_sems) == len(turn)
        proj_free = (proj_free0, proj_free1)

        unscaled = raw[:, 4:8, :].rearrange("p (k t) d -> p k (t d)", k=KT)
        with nc.Block() as block:
            @block.sync
            def _(sp):
                sp.dma_start(wmlp[:, 0:KT * KVCOLS], w_kv).then_inc(setup_loaded, 16)
                sp.dma_start(vp[:, :], vecs).then_inc(setup_loaded, 16)
                sp.dma_start(rp[:, 0:RPN * D], rows[0:1, 0:RPN * D].broadcast_to([LQ, RPN * D])).then_inc(setup_loaded, 16)
                sp.dma_start(gate[:, :], rows[0:1, RPN * D:RPN * D + 1].broadcast_to([LQ, 1])).then_inc(setup_loaded, 16)
                sp.dma_start(wf[:, :, :, :].rearrange("p a k n -> p (a k n)"), w_f).then_inc(setup_loaded, 16)
                sp.wait_ge(setup_mem, 6)
                sp.dma_start(k0_hi[120:121, :].bitcast(F32), one_row).then_inc(setup_row, 16)
                sp.dma_start(k0_lo[121:122, :].bitcast(F32), one_row).then_inc(setup_row, 16)
                sp.wait_ge(setup_row, 32)

            @block.gpsimd
            def _(pool):
                fills = [(k0_hi[96:128, :].bitcast(F32), 0.0), (k0_lo[96:128, :].bitcast(F32), 0.0), (one_row, 1.0),
                         (ones4[:, :].bitcast(F32), 1.0), (one_bf[:, :], 1.0), (half_pow[:, :], -0.5),
                         (raw[:, NT - 1, :], 0.0),
                         (v0[:, :, :, :], 1.0), (v[:, :, :, :], 1.0),
                         (mask_i[:, LK:LK + LQ], 0.0), (key_bias[:, :, :], 0.0)]
                for n, (tile, value) in enumerate(fills):
                    nc.gpsimd.memset(tile, value).then_inc(setup_mem, 1)
                    pool.wait_ge(setup_mem, n + 1)

            @block.scalar
            def _(act):
                act.wait_ge(setup_loaded, 80)
                nc.scalar.activation(tgate[:, :], gate[:, :], ACT.Tanh).then_inc(setup_gate, 1)

            @block.vector
            def _(dve):
                nc.vector.memset(accum[:, :], 0.0).then_inc(setup_split, 1)
                dve.wait_ge(setup_loaded, 80)
                src = wmlp[:, 0:KT * KVCOLS].rearrange("p (k n) -> p k n", k=KT)
                scaled = raw[:, 0:4, :].rearrange("p (k t) d -> p k (t d)", k=KT)
                for k in range(KT):
                    nc.vector.tensor_scalar(scaled[:, k, :], src[:, k, 128:640], vec("g1", k), None,
                                            ALU.mult).then_inc(setup_split, 1)
                dve.wait_ge(setup_split, 3)
                for k in range(KT):
                    nc.vector.tensor_copy(unscaled[:, k, :], src[:, k, 128:640]).then_inc(setup_split, 1)
                dve.wait_ge(setup_split, 5)
                for k in range(KT):
                    nc.vector.tensor_copy(src[:, k, 128:640], scaled[:, k, :]).then_inc(setup_split, 1)
                dve.wait_ge(setup_split, 7)
                nc.vector.tensor_copy(wkv_hi[:, :, :], src).then_inc(setup_split, 1)
                dve.wait_ge(setup_split, 8)
                nc.vector.tensor_tensor(wkv_lo[:, :, :], src, wkv_hi[:, :, :].bitcast(F32), ALU.subtract)\
                    .then_inc(setup_split, 1)
                for k in range(KT):
                    nc.vector.tensor_copy(xt[:, k, :], vec("b1", k).broadcast_to([128, LQ])).then_inc(setup_split, 1)
                e0, _ = VP["e56"]
                eye = vp[64:64 + LQ, e0:e0 + LQ].unsqueeze(1).broadcast_to([LQ, 32, LQ])
                nc.vector.tensor_copy(q0_hi[64:64 + LQ, :].rearrange("p (h q) -> p h q", h=32), eye)\
                    .then_inc(setup_split, 1)
                dve.wait_ge(setup_pe, 2)
                nc.vector.tensor_copy(bk1[:, :], chain[:, 0:2]).then_inc(setup_fold, 1)
                nc.vector.tensor_copy(row("bv1"), chain[0:LQ, 256:512]).then_inc(setup_fold, 1)

            @block.tensor
            def _(pe):
                pe.wait_ge(setup_split, 12)
                w = unscaled
                for g in range(2):
                    for k in range(KT):
                        mm = nc.tensor.matmul(chain[:, g:g + 1], w[:, k, g * 128:(g + 1) * 128],
                                              vec("b1", k), start=(k == 0), stop=(k == KT - 1))
                mm.then_inc(setup_pe, 1)
                for k in range(KT):
                    mm = nc.tensor.matmul(chain[0:LQ, 256:512], xt[:, k, :], w[:, k, 256:512],
                                          start=(k == 0), stop=(k == KT - 1))
                mm.then_inc(setup_pe, 1)

        def turn_block(order, batch, ahead):
            looped = batch is not None
            uses, use_no = [s for s in order if s[0] == "p"], {}
            for n, s in enumerate(uses):
                use_no[s] = n
            chain_steps = [s for s in order if s[0] == "c"]
            out_before = {s: n for n, s in enumerate(chain_steps)}
            pe_before = {s: sum(t[2] in ON_PE for t in chain_steps[:n]) for n, s in enumerate(chain_steps)}
            unit_steps = [s for s in order if s[0] == "s"]
            unit_no = {s: n for n, s in enumerate(unit_steps)}
            layers = range(4) if looped else ()
            steps_of = [GROUPS[l] * len(key_tiles(l)) for l in range(4)]
            steps_before = [sum(steps_of[:l]) for l in range(5)]
            max_steps = [s for s in order if s[0] == "m"]
            max_no = {s: n + 1 for n, s in enumerate(max_steps)}
            rows_no = {s: sum(1 + (r[1] == 0) for r in max_steps[:n + 1]) for n, s in enumerate(max_steps)}

            def slot(s):
                return 2 if s[2] >= 4 else unit_no[s] % 2

            def units_out_before(s):
                return sum(t[0] == "s" for t in order[:order.index(s)])


            def steps_out_before(s):
                return sum(t[0] == "c" for t in order[:order.index(s)])

            q_no = {1: 1, 2: 2, 3: 3, 0: 4} if looped else {0: 1}
            norm_no = {(0, "o"): 1, (2, "o"): 2, (3, "pre"): 3, (3, "o"): 5}
            ln_no = 4 if looped else 1

            def k_bias(l, g):
                return bk1[:, g:g + 1] if l == 1 else vec("bk%d" % l, g)

            with nc.Block() as block:
                @block.sync
                def _(sp):
                    def move_max(g):
                        sp.wait_ge(max_rows, rows_no[("m", 0, g)])
                        for row, part in ((120, mx0_hi), (121, mx0_lo)):
                            sp.dma_start(q0_hi[row:row + 1, g * GW:(g + 1) * GW].bitcast(F32),
                                         part[:, g, :].bitcast(F32)).then_inc(max_moved, 16)

                    sp.dma_start(x_next[:, :], x[ahead]).then_inc(x_loaded, 16)
                    sp.dma_start(rawmask[64:64 + LQ, :], mask0[ahead]).then_inc(mask_loaded, 16)
                    sp.dma_start(rawmask[0:1, :].bitcast(I32), mask_int[ahead]).then_inc(mask_loaded, 16)
                    sp.dma_start(rawmask[32:33, 0:LK // 4].bitcast(U8), mask_bool[ahead]).then_inc(mask_loaded, 16)
                    if looped:
                        sp.dma_start(wmlp[:, :], w_mlp[0]).then_inc(mlp_loaded, 16)
                        for g in (1, 2, 3):
                            move_max(g)
                        sp.wait_ge(proj_ready, use_no[("p", "at", 2, 1)] + 1)
                    sp.dma_start(raw[:, 0:NT - 1, :],
                                 ctx[ahead][0:128 * (NT - 1), :].rearrange("(t p) d -> p t d", p=128))\
                        .then_inc(ctx_loaded, 16)
                    sp.dma_start(raw[0:LAST, NT - 1, :], ctx[ahead][128 * (NT - 1):LK, :]).then_inc(ctx_loaded, 16)
                    if looped:
                        sp.wait_ge(chain_pe, pe_before[("c", 2, "down")] + 1)
                        sp.dma_start(wmlp[:, :], w_mlp[1]).then_inc(mlp_loaded, 16)
                        sp.wait_ge(chain_out, out_before[("c", 3, "down")] + 1)
                        sp.dma_start(out[batch], ya[:, :]).then_inc(out_stored, 16)
                    move_max(0)
                    if looped:
                        sp.wait_ge(out_stored, 16)
                    sp.wait_ge(max_moved, 128 if looped else 32)

                @block.gpsimd
                def _(pool):
                    def rstd(n, o, i, w):
                        pool.wait_ge(var_ready, n)
                        nc.gpsimd.tensor_tensor(o, i, w, ALU.pow).then_inc(rstd_ready, 1)
                        pool.wait_ge(rstd_ready, n)

                    for s in order:
                        if s[0] == "q0" or s[0] == "c" and s[2] == "q":
                            l = 0 if s[0] == "q0" else s[1]
                            pool.wait_ge(q_ready, q_no[l])
                            if l == 0:
                                hm = vec("hm0", None, 0, 64).unsqueeze(2).broadcast_to([64, 8, 4 * LQ])
                                src = ql[0:64, :].unsqueeze(1).broadcast_to([64, 8, 4 * LQ])
                                nc.gpsimd.tensor_tensor(q_x[0:64, :].rearrange("p (h c) -> p h c", h=8), src, hm,
                                                        ALU.mult).then_inc(qlo_ready, 1)
                            else:
                                for g in range(2):
                                    hm = vec("hm").unsqueeze(2).broadcast_to([128, 8, LQ])
                                    src = ql[:, g * LQ:(g + 1) * LQ].unsqueeze(1).broadcast_to([128, 8, LQ])
                                    ins = nc.gpsimd.tensor_tensor(
                                        q_x[:, (2 + g) * GW:(3 + g) * GW].rearrange("p (h q) -> p h q", h=8),
                                        src, hm, ALU.mult)
                                ins.then_inc(qlo_ready, 1)
                            pool.wait_ge(qlo_ready, q_no[l])
                        if s[0] == "c" and s[1:] in ((0, "o"), (2, "o"), (3, "o")):
                            rstd(norm_no[s[1:]], st[:, 9:10], st[:, 8:9], half_pow[0:LQ, 0:1])
                        if s[0] == "c" and s[1:] == (3, "xt"):
                            rstd(norm_no[(3, "pre")], st[:, 9:10], st[:, 8:9], half_pow[0:LQ, 0:1])
                        if s[0] == "pre":
                            pool.wait_ge(mask_ready, 2)
                            nc.gpsimd.partition_broadcast(mask_b[:, 0:LK], mask_row[32:33, :]).then_inc(mask_wide, 1)
                            pool.wait_ge(mask_wide, 1)
                            nc.gpsimd.partition_broadcast(mask_i[:, 0:LK], mask_row[0:1, :]).then_inc(mask_wide, 1)
                            pool.wait_ge(mask_wide, 2)
                            rstd(ln_no, crs[:, :], cvar[:, :], half_pow[:, :])
                        if s[0] == "ln":
                            pool.wait_ge(proj_ready, use_no[("p", "ct", NT // 2 - 1)] + 1)
                            pool.wait_ge(shift_ready, 1)
                            for t in range(NT):
                                ins = nc.gpsimd.tensor_scalar(raw[:, t, :], raw[:, t, :], crs[:, t:t + 1],
                                                              cshift[:, t:t + 1], ALU.mult, ALU.add)
                            ins.then_inc(norm_done, 1)

                @block.scalar
                def _(act):
                    def evacuate_hi(s):
                        n = use_no[s]
                        b = n % 2
                        act.wait_ge(proj_ready, n + 1)
                        kind = s[1]
                        if kind in ("ct", "at"):
                            src = proj[:, b, :].rearrange("p (t k c) -> p t k c", t=2, k=KT)
                            if kind == "ct":
                                dst = ctx_hi[:, :, s[2] * 256:(s[2] + 1) * 256]
                            else:
                                dst = a_hi[:, :, s[3] * 256:(s[3] + 1) * 256]
                            nc.scalar.activation(dst.rearrange("p k (t c) -> p t k c", t=2), src, ACT.Copy)\
                                .then_inc(proj_hi, 1)
                        elif kind == "k":
                            l, g, c = s[2:]
                            k, w = KCHUNKS[c]
                            if l == 0:
                                nc.scalar.activation(k0_hi[0:64, k:k + w], proj[0:64, b, 0:w], ACT.Identity,
                                                     bias=vec("bk0", 0, 0, 64)).then_inc(proj_hi, 1)
                            else:
                                nc.scalar.activation(k_hi[:, g, k:k + w], proj[:, b, 0:w], ACT.Identity,
                                                     bias=k_bias(l, g)).then_inc(proj_hi, 1)
                        elif kind == "v0":
                            j = s[2]
                            nc.scalar.activation(v0[:, 6 * j:6 * j + 6, :, 0:8],
                                                 proj[:, b, 0:384].rearrange("p (t h d) -> p t h d", t=6, h=8),
                                                 ACT.Copy).then_inc(proj_free[b], 1)
                        else:
                            j = s[3]
                            nc.scalar.activation(v[:, 2 * j:2 * j + 2, :, 0:16],
                                                 proj[:, b, :].rearrange("p (t h d) -> p t h d", t=2, h=16),
                                                 ACT.Copy).then_inc(proj_free[b], 1)

                    tanh_no = 0
                    for s in order:
                        if s[0] == "p":
                            evacuate_hi(s)
                        elif s[0] == "t":
                            _, l, g, t = s
                            j = steps_before[l] + g * len(key_tiles(l)) + t
                            kt = key_tiles(l)[t][1]
                            act.wait_ge(step_ready, j + 1)
                            if j >= NPR:
                                act.wait_ge(pv_done, j - NPR + 1)
                            bias = 0.0 if l == 0 else key_bias[0:kt, int(l == 2), t:t + 1]
                            nc.scalar.activation(probs[0:kt, j % NPR, :], score[0:kt, j % 4, 0:GW], ACT.Exp,
                                                 bias=bias).then_inc(exp_done, 1)
                        elif s[0] == "c" and s[2] == "up":
                            tanh_no += 1
                            act.wait_ge(act_in, tanh_no)
                            nc.scalar.activation(hu[:, :], hu[:, :], ACT.Tanh, scale=GELU_S).then_inc(act_out, 1)

                @block.vector
                def _(dve):
                    linked = [0]

                    def link(ins):
                        linked[0] += 1
                        ins.then_inc(dve_link, 1)
                        dve.wait_ge(dve_link, linked[0])

                    tt, ts, stt, cp = (nc.vector.tensor_tensor, nc.vector.tensor_scalar,
                                       nc.vector.scalar_tensor_tensor, nc.vector.tensor_copy)

                    def evacuate_lo(s):
                        n, kind = use_no[s], s[1]
                        b = n % 2
                        if kind in ("v", "v0"):
                            return
                        dve.wait_ge(proj_hi, sum(u[1] not in ("v", "v0") for u in uses[:n]) + 1)
                        if kind in ("ct", "at"):
                            src = proj[:, b, :].rearrange("p (t k c) -> p k t c", t=2, k=KT)
                            hi, lo = (ctx_hi, ctx_lo) if kind == "ct" else (a_hi, a_lo)
                            c = (s[2] if kind == "ct" else s[3]) * 256
                            for k in range(KT):
                                ins = tt(lo[:, k, c:c + 256].rearrange("p (t c) -> p t c", t=2), src[:, k],
                                         hi[:, k, c:c + 256].bitcast(F32).rearrange("p (t c) -> p t c", t=2),
                                         ALU.subtract)
                            ins.then_inc(proj_free[b], 1)
                        else:
                            l, g, c = s[2:]
                            k, w = KCHUNKS[c]
                            if l == 0:
                                stt(k0_lo[0:64, k:k + w], proj[0:64, b, 0:w], vec("bk0", 0, 0, 64),
                                    k0_hi[0:64, k:k + w].bitcast(F32), ALU.add, ALU.subtract)\
                                    .then_inc(proj_free[b], 1)
                            else:
                                stt(k_lo[:, g, k:k + w], proj[:, b, 0:w], k_bias(l, g),
                                    k_hi[:, g, k:k + w].bitcast(F32), ALU.add, ALU.subtract)\
                                    .then_inc(proj_free[b], 1)

                    def unit_max(s):
                        _, l, p, h = s
                        n = unit_no[s]
                        k, w = units(l)[h]
                        dve.wait_ge(unit_ready, n + 1)
                        at = slot(s)
                        src = proj[0:PAIR, :, 0:w] if at == 2 else score[0:PAIR, 2 * at:2 * at + 2, 0:w]
                        if l == 0:
                            ins = nc.vector.tensor_reduce(row_max[:, p, h:h + 1], src, AX.XY, ALU.max)
                        else:
                            m = mask_i if l == 2 else mask_b
                            ins = nc.vector.tensor_tensor_reduce(
                                src, src,
                                m[0:PAIR, k:k + 2 * w].rearrange("p (b w) -> p b w", b=2),
                                1.0, -3.0e38, ALU.add, ALU.max, row_max[:, p, h:h + 1])
                        ins.then_inc(unit_read, 1)

                    def max_to_rows(s):
                        _, l, g = s
                        dve.wait_ge(unit_read, units_out_before(s))
                        nc.vector.tensor_reduce(neg_max[:, 4 * g:4 * g + 4], row_max[:, 4 * g:4 * g + 4, :], AX.X,
                                                ALU.max, negate=True).then_inc(max_ready, 1)
                        dve.wait_ge(max_turned, max_no[s])
                        if l == 0:
                            cp(mx0_hi[:, g, :], chain[0:4, 0:PAIR]).then_inc(max_rows, 1)
                            dve.wait_ge(max_rows, rows_no[s] - 1)
                            tt(mx0_lo[:, g, :], chain[0:4, 0:PAIR], mx0_hi[:, g, :].bitcast(F32), ALU.subtract)\
                                .then_inc(max_rows, 1)
                        else:
                            tt(diag_max[:, g * GW:(g + 1) * GW].rearrange("p (h c) -> p h c", h=4),
                               chain[0:4, 0:PAIR].unsqueeze(1).broadcast_to([4, 4, PAIR]),
                               vec("ident", None, 0, 4)[:, 0:4].unsqueeze(2).broadcast_to([4, 4, PAIR]),
                               ALU.mult).then_inc(max_rows, 1)

                    def stats(src, n, centred):
                        if centred:
                            link(nc.vector.bn_stats(st[:, 0:6], src))
                            link(nc.vector.bn_aggr(st[:, 6:8], st[:, 0:6]))
                            ts(st[:, 8:9], st[:, 7:8], 1e-6 if n == 1 else 1e-5, None, ALU.add).then_inc(var_ready, 1)
                        else:
                            link(nc.vector.tensor_tensor_reduce(hid[0:LQ, 0:D], src, src, 1.0, 0.0, ALU.mult, ALU.add,
                                                                st[:, 7:8]))
                            ts(st[:, 8:9], st[:, 7:8], 1.0 / D, 1e-6, ALU.mult, ALU.add).then_inc(var_ready, 1)
                        dve.wait_ge(rstd_ready, n)

                    def spread_queries(l, src, scaled):
                        p, n = (64, 4) if l == 0 else (128, 2)
                        w = n * LQ
                        if l == 1:
                            link(ts(scaled[:, 0:w], src[:, 0:w], SCALE[l], None, ALU.mult))
                        else:
                            for g in range(n):
                                ins = ts(scaled[0:p, g * LQ:(g + 1) * LQ], src[0:p, g * LQ:(g + 1) * LQ],
                                         vec("bq%d" % l, g, 0, p), SCALE[l], ALU.add, ALU.mult)
                            link(ins)
                        link(cp(qh[0:p, 0:w], scaled[0:p, 0:w]))
                        if q_no[l] > 1:
                            dve.wait_ge(qlo_ready, q_no[l] - 1)
                        tt(ql[0:p, 0:w], scaled[0:p, 0:w], qh[0:p, 0:w].bitcast(F32), ALU.subtract)\
                            .then_inc(q_ready, 1)
                        if l == 0:
                            return tt(q0_hi[0:64, :].rearrange("p (h c) -> p h c", h=8),
                                      qh[0:64, :].bitcast(F32).unsqueeze(1).broadcast_to([64, 8, w]),
                                      vec("hm0", None, 0, 64).unsqueeze(2).broadcast_to([64, 8, w]), ALU.mult)
                        for g in range(2):
                            ins = tt(q_x[:, g * GW:(g + 1) * GW].rearrange("p (h q) -> p h q", h=8),
                                     qh[:, g * LQ:(g + 1) * LQ].bitcast(F32).unsqueeze(1).broadcast_to([128, 8, LQ]),
                                     vec("hm").unsqueeze(2).broadcast_to([128, 8, LQ]), ALU.mult)
                        return ins

                    def chain_step(s):
                        _, l, name = s
                        if name in ON_PE:
                            dve.wait_ge(chain_pe, pe_before[s] + 1)
                        if out_before[s]:
                            dve.wait_ge(chain_out, out_before[s])
                        last = None
                        if name == "ot":
                            dve.wait_ge(pv_done, steps_before[l + 1])
                            w = 448 if l == 0 else 224
                            last = cp(ot[:, 0:w], accum[:, 0:w])
                        elif name in ("norm", "norm_a", "norm_b"):
                            half, hd = name == "norm_b", 8 if l == 0 else 16
                            full = chain[0:LQ, :].rearrange("q (c j e) -> q c j e", c=4, j=4)
                            link(nc.vector.reciprocal(rec[:, :].rearrange("q (c j) -> q c j", c=4), full[:, :, :, hd]))
                            if l == 0:
                                dst = ya[:, half * 128:half * 128 + 128].rearrange("q (j c d) -> q c j d", j=4, c=4)
                            else:
                                dst = ya[:, :].rearrange("q (c j d) -> q c j d", c=4, j=4)
                            for c in range(4):
                                ins = tt(dst[:, c], full[:, c, :, 0:hd],
                                         rec[:, 4 * c:4 * c + 4].unsqueeze(2).broadcast_to([LQ, 4, hd]), ALU.mult)
                            if name == "norm_a":
                                last = ins
                            else:
                                link(ins)
                                last = tt(ya[:, :], ya[:, :], row("bv%d" % l), ALU.add)
                        elif name == "ont":
                            last = cp(xt[:, :, :], chain[:, 0:KT * LQ].rearrange("p (k q) -> p k q", k=KT))
                        elif name == "o":
                            y = chain[0:LQ, 0:D]
                            if l == 0:
                                link(tt(ya[:, :], y, xres0[:, :], ALU.add))
                                stats(ya[:, :], norm_no[(0, "o")], True)
                                link(ts(ya[:, :], ya[:, :], st[:, 6:7], st[:, 9:10], ALU.subtract, ALU.mult))
                                link(tt(ya[:, :], ya[:, :], row("g0"), ALU.mult))
                                last = tt(xcur[:, :], ya[:, :], row("be0"), ALU.add)
                            elif l == 1:
                                last = stt(xcur[:, :], y, tgate[:, 0:1], xcur[:, :], ALU.mult, ALU.add)
                            elif l == 2:
                                link(tt(ya[:, :], y, xres[:, :], ALU.add))
                                stats(ya[:, :], norm_no[(2, "o")], False)
                                last = ts(ya[:, :], ya[:, :], st[:, 9:10], None, ALU.mult)
                            else:
                                link(tt(xcur[:, :], y, xres[:, :], ALU.add))
                                stats(xcur[:, :], norm_no[(3, "o")], True)
                                last = ts(ya[:, :], xcur[:, :], st[:, 6:7], st[:, 9:10], ALU.subtract, ALU.mult)
                        elif name == "yt":
                            src = chain[:, 0:KT * LQ].rearrange("p (k q) -> p k q", k=KT)
                            for k in range(KT):
                                if l == 2:
                                    last = ts(xt[:, k, :], src[:, k, :], vec("pw", k), None, ALU.mult)
                                else:
                                    last = ts(xt[:, k, :], src[:, k, :], vec("ln2w", k), vec("ln2b", k),
                                              ALU.mult, ALU.add)
                        elif name == "up":
                            b = vec("mb%d" % l).unsqueeze(2).broadcast_to([128, 8, LQ])
                            link(tt(hid[:, :].rearrange("p (t q) -> p t q", t=8),
                                    chain[:, 0:GW].rearrange("p (t q) -> p t q", t=8), b, ALU.add))
                            link(tt(hu[:, :], hid[:, :], hid[:, :], ALU.mult))
                            link(ts(hu[:, :], hu[:, :], GELU_C, 1.0, ALU.mult, ALU.add))
                            tt(hu[:, :], hu[:, :], hid[:, :], ALU.mult).then_inc(act_in, 1)
                            dve.wait_ge(act_out, 1 if l == 2 else 2)
                            last = stt(hid[:, :], hu[:, :], 1.0, hid[:, :], ALU.add, ALU.mult)
                        elif name == "down":
                            link(tt(xres[:, :], xcur[:, :], row("b22" if l == 2 else "b23"), ALU.add))
                            last = stt(xcur[:, :] if l == 2 else ya[:, :], chain[0:LQ, 0:D], 0.5, xres[:, :],
                                       ALU.mult, ALU.add)
                        elif name == "xt":
                            src = chain[:, 0:KT * LQ].rearrange("p (k q) -> p k q", k=KT)
                            if l == 3:
                                for k in range(KT):
                                    last = ts(xt[:, k, :], src[:, k, :], vec("ln1w", k), vec("ln1b", k),
                                              ALU.mult, ALU.add)
                            elif l == 2:
                                link(cp(xt[:, :, :], src))
                                link(cp(xt_hi, xt[:, :, :]))
                                last = tt(xt_lo, xt[:, :, :], xt_hi.bitcast(F32), ALU.subtract)
                            else:
                                last = cp(xt[:, :, :], src)
                        elif name == "q":
                            last = spread_queries(l, chain, qs)
                        elif name == "lat":
                            for g in range(2):
                                link(ts(qs[:, g * LQ:(g + 1) * LQ], chain[:, g * LQ:(g + 1) * LQ],
                                        vec("bk2", g), None, ALU.add))
                            for g in range(2):
                                link(cp(k_hi[:, g, LK:LK + LQ], qs[:, g * LQ:(g + 1) * LQ]))
                            for g in range(2):
                                tt(k_lo[:, g, LK:LK + LQ], qs[:, g * LQ:(g + 1) * LQ],
                                   k_hi[:, g, LK:LK + LQ].bitcast(F32), ALU.subtract)
                            last = cp(v[0:LQ, NT, :, 0:16], chain[0:LQ, 256:512].rearrange("q (h d) -> q h d", h=16))
                        last.then_inc(chain_out, 1)

                    def before(s):
                        _, l, name = s
                        if name == "xt":
                            if l in (2, 3):
                                if out_before[s]:
                                    dve.wait_ge(chain_out, out_before[s])
                                ins = tt(xres[:, :], xcur[:, :], row("ob2" if l == 2 else "cb3"), ALU.add)
                                if l == 3:
                                    stats(xcur[:, :], norm_no[(3, "pre")], True)
                                    ts(ya[:, :], xcur[:, :], st[:, 6:7], st[:, 9:10], ALU.subtract, ALU.mult)\
                                        .then_inc(ln1_ready, 1)

                    for s in order:
                        if s[0] == "p":
                            evacuate_lo(s)
                        elif s[0] == "s":
                            unit_max(s)
                        elif s[0] == "m":
                            max_to_rows(s)
                        elif s[0] == "xt0":
                            dve.wait_ge(x_loaded, 16)
                            tt(xres0[:, :], x_next[:, :], row("bo0"), ALU.add)
                            dve.wait_ge(q0_pe, 1)
                            cp(xt_next[:, :, :], score[:, 2, 0:KT * LQ].rearrange("p (k q) -> p k q", k=KT))\
                                .then_inc(q0_out, 1)
                        elif s[0] == "q0":
                            dve.wait_ge(q0_pe, 2)
                            spread_queries(0, score[:, 3], q0s).then_inc(q0_out, 1)
                        elif s[0] == "c":
                            before(s)
                            chain_step(s)
                        elif s[0] == "pre":
                            dve.wait_ge(mask_loaded, 48)
                            link(cp(k0_hi[64:64 + LQ, :], rawmask[64:64 + LQ, :]))
                            tt(k0_lo[64:64 + LQ, :], rawmask[64:64 + LQ, :], k0_hi[64:64 + LQ, :].bitcast(F32),
                               ALU.subtract).then_inc(mask0_done, 1)
                            ts(mask_row[0:1, :], rawmask[0:1, :].bitcast(I32), 0, NEG, ALU.is_equal, ALU.mult)\
                                .then_inc(mask_ready, 1)
                            ts(mask_row[32:33, :], rawmask[32:33, 0:LK // 4].bitcast(U8), 0, NEG, ALU.is_equal,
                               ALU.mult).then_inc(mask_ready, 1)
                            dve.wait_ge(bias_ready, 1)
                            if looped:
                                dve.wait_ge(exp_done, steps_before[4])
                            for m in range(2):
                                src = (score[:, 0], chain)[m]
                                cp(key_bias[:, m, 0:NT - 1], src[:, 0:NT - 1])
                                ins = cp(key_bias[0:LAST, m, NT - 1:NT], src[0:LAST, NT - 1:NT])
                            ins.then_inc(bias_done, 1)
                            dve.wait_ge(ctx_loaded, 32)
                            for t in range(NT):
                                ins = nc.vector.bn_stats(cst[:, t, :], raw[:, t, :])
                            link(ins)
                            for t in range(NT):
                                ins = nc.vector.bn_aggr(cmv[:, t, :], cst[:, t, :])
                            link(ins)
                            ts(cvar[:, :], cmv[:, :, 1], 1e-5, None, ALU.add).then_inc(var_ready, 1)
                        elif s[0] == "ln":
                            dve.wait_ge(rstd_ready, ln_no)
                            stt(cshift[:, :], cmv[:, :, 0], -1.0, crs[:, :], ALU.mult, ALU.mult)\
                                .then_inc(shift_ready, 1)

                @block.tensor
                def _(pe):
                    mm = nc.tensor.matmul

                    def mm3(o, lh, ll, rh, rl, first=True, last=True):
                        mm(o, lh, rh, start=first, stop=False)
                        mm(o, ll, rh, start=False, stop=False)
                        return mm(o, lh, rl, start=False, stop=last)

                    def project(s):
                        n, kind = use_no[s], s[1]
                        b = n % 2
                        if n >= 2:
                            pe.wait_ge(proj_free[b], n // 2)
                        if kind in ("ct", "at"):
                            if kind == "ct":
                                pe.wait_ge(ctx_loaded, 32)
                            elif s[2] == 0:
                                pe.wait_ge(norm_done, 1)
                            t0 = 2 * s[2] if kind == "ct" else 4 * s[2] + 2 * s[3]
                            for t in range(2):
                                for k in range(KT):
                                    ins = nc.tensor.transpose(proj[:, b, (2 * t + k) * 128:(2 * t + k + 1) * 128],
                                                              raw[:, t0 + t, k * 128:(k + 1) * 128], ident)
                        elif kind == "k":
                            l, g, c = s[2:]
                            k0, w = KCHUNKS[c]
                            m = min(KV[l], 128)
                            if l == 1:
                                sh, sl, at = a_hi, a_lo, 0
                                wait_lo(("p", "at", c, 1))
                            else:
                                sh, sl, at = ctx_hi, ctx_lo, k0
                                if l == 0:
                                    wait_lo(("p", "ct", NT // 2 - 1))
                            o = KOFF[l] + g * 128
                            for k in range(KT):
                                ins = mm3(proj[0:m, b, 0:w], wkv_hi[:, k, o:o + m], wkv_lo[:, k, o:o + m],
                                          sh[:, k, at:at + w], sl[:, k, at:at + w], k == 0, k == KT - 1)
                        else:
                            if kind == "v0":
                                l, tiles, o = 0, range(6 * s[2], 6 * s[2] + 6), KOFF[0] + 64
                            else:
                                l, tiles, o = s[2], range(2 * s[3], 2 * s[3] + 2), KOFF[s[2]] + 256
                            for i, t in enumerate(tiles):
                                if l == 1:
                                    sh, sl, at = a_hi, a_lo, (t % 4) * 128
                                else:
                                    sh, sl, at = ctx_hi, ctx_lo, t * 128
                                w = KV[l]
                                for k in range(KT):
                                    ins = mm3(proj[:, b, i * w:(i + 1) * w], sh[:, k, at:at + 128],
                                              sl[:, k, at:at + 128], wkv_hi[:, k, o:o + w], wkv_lo[:, k, o:o + w],
                                              k == 0, k == KT - 1)
                        ins.then_inc(proj_ready, 1)

                    def wait_lo(s):
                        n = use_no[s]
                        pe.wait_ge(proj_free[n % 2], n // 2 + 1)
                        pe.wait_ge(proj_free[1 - n % 2], (n + 1) // 2)

                    def last_use_before(s):
                        done = [t for t in order[:order.index(s)] if t[0] == "p"]
                        return done[-1] if done else None

                    def score_unit(s):
                        _, l, p, h = s
                        n, at = unit_no[s], slot(s)
                        if p == 0 and h == 0:
                            if l:
                                pe.wait_ge(exp_done, steps_before[l])
                                pe.wait_ge(chain_out, out_before[("c", l, "q")] + 1)
                                if l == 2:
                                    pe.wait_ge(chain_out, out_before[("c", 2, "lat")] + 1)
                                wait_lo(("p", "k", l, 1, 2))
                            else:
                                pe.wait_ge(bias_done, 1)
                                pe.wait_ge(q0_out, 2)
                                wait_lo(("p", "k", 0, 0, 2))
                        elif p == 4 and h == 0:
                            use = last_use_before(s)
                            if use:
                                wait_lo(use)
                        before = [m for u, m in unit_no.items() if m < n and slot(u) == at]
                        if before:
                            pe.wait_ge(unit_read, before[-1] + 1)
                        k, w = units(l)[h]
                        for b in range(2):
                            o = proj[0:PAIR, b, 0:w] if at == 2 else score[0:PAIR, 2 * at + b, 0:w]
                            c = k + b * w
                            if l == 0:
                                q = q0_hi[0:120, p * PAIR:(p + 1) * PAIR]
                                mm(o, q, k0_hi[0:120, c:c + w], start=True, stop=False)
                                ins = mm(o, q, k0_lo[0:120, c:c + w], start=False, stop=True)
                            else:
                                ins = mm(o, q_x[:, p * PAIR:(p + 1) * PAIR], k_hi[:, p // 4, c:c + w],
                                         start=True, stop=True)
                        ins.then_inc(unit_ready, 1)

                    def turn_max(s):
                        _, l, g = s
                        pe.wait_ge(max_ready, max_no[s])
                        if chain_steps and steps_out_before(s):
                            pe.wait_ge(chain_out, steps_out_before(s))
                        if max_no[s] > 1:
                            pe.wait_ge(max_rows, rows_no[max_steps[max_no[s] - 2]])
                        nc.tensor.transpose(chain[0:4, 0:PAIR], neg_max[:, 4 * g:4 * g + 4], ident[0:PAIR, 0:PAIR])\
                            .then_inc(max_turned, 1)

                    opened = [None, set()]

                    def scores_t(l, g, t):
                        j = steps_before[l] + g * len(key_tiles(l)) + t
                        k, kn = key_tiles(l)[t]
                        if t == 0:
                            if l:
                                pe.wait_ge(max_rows, rows_no[("m", l, g)])
                            elif g:
                                pe.wait_ge(max_moved, 32 * g)
                        if l and g == 0 and t == 0:
                            pe.wait_ge(qlo_ready, q_no[l])
                            pe.wait_ge(unit_read, units_out_before(("m", l, 0)))
                            wait_lo(("p", "v", l, NT // 2 - 1))
                            pe.wait_ge(chain_out, out_before[("c", l - 1, "ot")] + 1)
                        if j - steps_before[l] >= 4:
                            pe.wait_ge(exp_done, j - 3)
                        o = score[0:kn, j % 4, 0:GW]
                        if l == 0:
                            q = q0_hi[0:122, g * GW:(g + 1) * GW]
                            mm(o, k0_hi[0:122, k:k + kn], q, start=True, stop=False)
                            mm(o, k0_lo[0:122, k:k + kn], q, start=False, stop=False)
                            ins = mm(o, k0_hi[0:64, k:k + kn], q_x[0:64, g * GW:(g + 1) * GW],
                                     start=False, stop=True)
                        else:
                            mm3(o, k_hi[:, g, k:k + kn], k_lo[:, g, k:k + kn],
                                q_x[:, g * GW:(g + 1) * GW], q_x[:, (2 + g) * GW:(3 + g) * GW], True, False)
                            ins = mm(o, ones4[:, 0:kn], diag_max[:, g * GW:(g + 1) * GW], start=False, stop=True)
                        ins.then_inc(step_ready, 1)

                    def values(l, g, t):
                        j = steps_before[l] + g * len(key_tiles(l)) + t
                        kn = key_tiles(l)[t][1]
                        if opened[0] != l:
                            opened[:] = l, set()
                        pe.wait_ge(exp_done, j + 1)
                        heads, hd, vt = (2, 8, v0) if l == 0 else (8, 16, v)
                        w = GW // heads
                        for i in range(heads):
                            h = g * heads + i
                            quad, c = h % 4, (h // 4) * w
                            ins = mm(accum[32 * quad:32 * quad + hd + 1, c:c + w], vt[0:kn, t, h, :],
                                     probs[0:kn, j % NPR, i * w:(i + 1) * w],
                                     start=quad not in opened[1], stop=(t == len(key_tiles(l)) - 1),
                                     skip_group_check=True)
                            opened[1].add(quad)
                        ins.then_inc(pv_done, 1)

                    lagging = [s[1:] for s in order if s[0] == "t"]

                    def chain_part(s):
                        _, l, name = s
                        if name not in ON_PE:
                            return
                        if name == "xt":
                            if l == 3:
                                pe.wait_ge(ln1_ready, 1)
                        if out_before[s]:
                            pe.wait_ge(chain_out, out_before[s])
                        if name in ("norm", "norm_a", "norm_b"):
                            base = 4 if name == "norm_b" else 0
                            for c in range(4):
                                ins = nc.tensor.transpose(chain[0:LQ, c * 128:(c + 1) * 128],
                                                          ot[:, (base + c) * LQ:(base + c + 1) * LQ], ident)
                        elif name in ("xt", "ont", "yt"):
                            src = xcur if name == "xt" and l != 3 else ya
                            for k in range(KT):
                                ins = nc.tensor.transpose(chain[:, k * LQ:(k + 1) * LQ],
                                                          src[:, k * 128:(k + 1) * 128], ident[0:LQ, 0:LQ])
                        elif name == "o":
                            for k in range(KT):
                                ins = mm(chain[0:LQ, 0:D], xt[:, k, :], wo[l][:, k, :], start=(k == 0),
                                         stop=(k == KT - 1))
                        elif name == "q":
                            for g in range(2):
                                for k in range(KT):
                                    ins = mm(chain[:, g * LQ:(g + 1) * LQ], wq[l][:, k, g * 128:(g + 1) * 128],
                                             xt[:, k, :], start=(k == 0), stop=(k == KT - 1))
                        elif name == "lat":
                            o = KOFF[2]
                            for g in range(2):
                                for k in range(KT):
                                    mm3(chain[:, g * LQ:(g + 1) * LQ], wkv_hi[:, k, o + g * 128:o + (g + 1) * 128],
                                        wkv_lo[:, k, o + g * 128:o + (g + 1) * 128], xt_hi[:, k, :], xt_lo[:, k, :],
                                        k == 0, k == KT - 1)
                            for k in range(KT):
                                ins = mm3(chain[0:LQ, 256:512], xt_hi[:, k, :], xt_lo[:, k, :],
                                          wkv_hi[:, k, o + 256:o + 512], wkv_lo[:, k, o + 256:o + 512],
                                          k == 0, k == KT - 1)
                        elif name == "up":
                            pe.wait_ge(mlp_loaded, 16 if l == 2 else 32)
                            for t in range(8):
                                for k in range(KT):
                                    ins = mm(chain[:, t * LQ:(t + 1) * LQ], up_w[:, k, t * 128:(t + 1) * 128],
                                             xt[:, k, :], start=(k == 0), stop=(k == KT - 1))
                        elif name == "down":
                            for t in range(8):
                                ins = mm(chain[0:LQ, 0:D], hid[:, t * LQ:(t + 1) * LQ], down_w[:, t, :],
                                         start=(t == 0), stop=(t == 7))
                        ins.then_inc(chain_pe, 1)

                    for s in order:
                        if s[0] == "p":
                            project(s)
                        elif s[0] == "s":
                            score_unit(s)
                        elif s[0] == "m":
                            turn_max(s)
                        elif s[0] == "t":
                            scores_t(*s[1:])
                            n = lagging.index(s[1:])
                            if n >= 2 and lagging[n - 2][0] == s[1]:
                                values(*lagging[n - 2])
                        elif s[0] == "te":
                            for step in [t for t in lagging if t[0] == s[1]][-2:]:
                                values(*step)
                        elif s[0] == "c":
                            chain_part(s)
                        elif s[0] == "xt0":
                            pe.wait_ge(x_loaded, 16)
                            for k in range(KT):
                                ins = nc.tensor.transpose(score[:, 2, k * LQ:(k + 1) * LQ],
                                                          x_next[:, k * 128:(k + 1) * 128], ident[0:LQ, 0:LQ])
                            ins.then_inc(q0_pe, 1)
                        elif s[0] == "q0":
                            pe.wait_ge(q0_out, 1)
                            for g in range(4):
                                for k in range(KT):
                                    ins = mm(score[0:64, 3, g * LQ:(g + 1) * LQ], wq[0][:, k, g * 64:(g + 1) * 64],
                                             xt_next[:, k, :], start=(k == 0), stop=(k == KT - 1))
                            ins.then_inc(q0_pe, 1)
                        elif s[0] == "pre":
                            if chain_steps and looped:
                                pe.wait_ge(chain_out, steps_out_before(s))
                                pe.wait_ge(exp_done, steps_before[4])
                            pe.wait_ge(mask_ready, 2)
                            for m, (tile, p) in enumerate(((mask_row, 32), (mask_row, 0))):
                                for t, (k, kn) in enumerate(key_tiles(0)):
                                    ins = mm((score[:, 0], chain)[m][0:kn, t:t + 1], tile[p:p + 1, k:k + kn],
                                             one_bf[p:p + 1, :], start=True, stop=True)
                            ins.then_inc(bias_ready, 1)

            nc.all_engine_barrier(sems_to_clear=turn_sems)

        turn_block(first_order(), None, 0)
        with nc.Fori(0, NB) as i:
            turn_block(batch_order(), i, (i + 1) % NB)


def kernel(**inputs):
    import numpy as np
    import concourse.bacc as bacc
    from concourse.bass_utils import run_bass_kernel_spmd

    a = {n: np.asarray(v) for n, v in inputs.items()}
    P = lambda l, n: a["L%d_xattn_%s" % (l, n)]
    rows_of = lambda w: w.reshape(-1, 128, w.shape[1]).transpose(1, 0, 2).reshape(128, -1)

    kv2 = P(2, "kv_w").reshape(D, D, 2)
    w_kv = np.concatenate([P(0, "Wk"), P(0, "Wv"), P(1, "Wk").T, P(1, "Wv").T, kv2[..., 0], kv2[..., 1],
                           P(3, "k_w"), P(3, "v_w")], 1)
    wq0 = P(0, "Wq").reshape(D, 8, 4, 8).transpose(0, 2, 1, 3).reshape(D, D)
    w_f = [wq0, P(0, "Wo"), P(1, "Wq").T, P(1, "Wo").T, P(2, "q_w"), P(2, "out_w"), P(3, "q_w"), P(3, "cproj_w")]
    w_mlp = [np.concatenate([rows_of(P(2, "mlp_w1")), rows_of(P(2, "mlp_w2"))], 1),
             np.concatenate([rows_of(P(3, "fc_w")), rows_of(P(3, "proj_w"))], 1)]

    kvb = P(2, "kv_b").reshape(D, 2)
    bk0 = np.zeros((128, 1), np.float32)
    bk0[0:64, 0] = P(0, "bk")
    bq0 = np.zeros((128, 4), np.float32)
    bq0[0:64] = P(0, "bq").reshape(8, 4, 8).transpose(0, 2, 1).reshape(64, 4)
    by = lambda b: b.reshape(-1, 128).T
    part = np.arange(128)
    hm = (part[:, None] // 16 == np.arange(8)).astype(np.float32)
    hm0 = (part[:, None] // 8 == np.arange(8)).astype(np.float32)
    e56 = (part[:, None] - 64 == np.arange(LQ)).astype(np.float32)
    vecs = {"bk0": bk0, "bk2": by(kvb[:, 0]), "bk3": by(P(3, "k_b")), "bq0": bq0, "bq2": by(P(2, "q_b")),
            "bq3": by(P(3, "q_b")), "g1": by(P(1, "ln_gamma")), "b1": by(P(1, "ln_beta")),
            "pw": by(P(2, "postnorm_w")), "ln1w": by(P(3, "ln1_w")), "ln1b": by(P(3, "ln1_b")),
            "ln2w": by(P(3, "ln2_w")), "ln2b": by(P(3, "ln2_b")), "mb2": by(P(2, "mlp_b1")),
            "mb3": by(P(3, "fc_b")), "hm": hm, "hm0": hm0, "e56": e56, "ident": np.eye(128, dtype=np.float32)}
    bv0 = np.broadcast_to(P(0, "bv").reshape(8, 1, 8), (8, 4, 8)).reshape(D)
    rows = [bv0, P(0, "bo"), P(0, "gamma"), P(0, "beta"), kvb[:, 1], P(2, "out_b"), P(2, "mlp_b2"),
            P(3, "v_b"), P(3, "cproj_b"), P(3, "proj_b"), P(1, "gate")]
    arrays = {
        "ctx": a["ctx_2048"], "x": a["x"], "mask0": a["mask_Bx1xSxS2_ff0"].reshape(NB, LQ, LK),
        "mask_bool": a["mask_BxS2_bf1"].view(np.uint8).reshape(NB, 1, LK),
        "mask_int": a["mask_BxS2_ik0"].reshape(NB, 1, LK),
        "w_kv": rows_of(w_kv), "w_f": np.concatenate([rows_of(w) for w in w_f], 1), "w_mlp": np.stack(w_mlp),
        "vecs": np.concatenate([vecs[n] for n in VP], 1), "rows": np.concatenate(rows)[None],
    }
    arrays = {n: np.ascontiguousarray(v) for n, v in arrays.items()}
    nc = bacc.Bacc("TRN2", target_bir_lowering=False, num_devices=1,
                   dynamic_dma_scratch_size=1024)
    args = [nc.dram_tensor(n + "_dram", v.shape, mybir.dt.from_np(v.dtype), kind="ExternalInput").ap()
            for n, v in arrays.items()]
    out = nc.dram_tensor("out_dram", (NB, LQ, D), F32, kind="ExternalOutput").ap()
    fused_attention_kernel(nc, *args, out)
    r = run_bass_kernel_spmd(nc, [{n + "_dram": v for n, v in arrays.items()}], core_ids=[0])
    return r.results[0]["out_dram"]
```

```python
from contextlib import ExitStack

import concourse.bass as bass
from concourse import mybir

F32 = mybir.dt.float32
F32R = mybir.dt.float32r
BF16 = mybir.dt.bfloat16
U8 = mybir.dt.uint8
I32 = mybir.dt.int32
ALU = mybir.AluOpType
ACT = mybir.ActivationFunctionType
AX = mybir.AxisListType

NB = 8
LQ = 56
LK = 1500
D = 256
KT = D // 128
NT = -(-LK // 128)
LKP = NT * 128
LAST = LK - (NT - 1) * 128
PAIR = 2 * LQ
GW = 8 * LQ
NEG = -float(2.0 ** 100)
GELU_C = 0.044715
GELU_S = 0.7978845608028654

GROUPS = (4, 2, 2, 2)
SCALE = (8 ** -0.5, 0.25, 1.0 / 16, 0.25)
KV = (128, 256, 256, 256)
KOFF = (0, 128, 640, 1152)
KVCOLS = 1664

VP = {}
for _name, _n in (("bk0", 1), ("bk2", 2), ("bk3", 2), ("bq0", 4), ("bq2", 2), ("bq3", 2), ("g1", 2), ("b1", 2),
                  ("pw", 2), ("ln1w", 2), ("ln1b", 2), ("ln2w", 2), ("ln2b", 2), ("mb2", 8), ("mb3", 8),
                  ("hm", 8), ("hm0", 8), ("e56", LQ), ("ident", 128)):
    VP[_name] = (sum(n for _, n in VP.values()), _n)
VPW = sum(n for _, n in VP.values())
RP = {n: i for i, n in enumerate(("bv0", "bo0", "g0", "be0", "bv2", "ob2", "b22", "bv3", "cb3", "b23", "bv1"))}
RPN = 10


def units(layer):
    if layer != 2:
        return ((0, 500), (500, 500), (1000, 500))
    return ((0, 390), (390, 390), (780, 388), (1168, 388))


def key_tiles(layer):
    t = [(128 * i, 128) for i in range(NT - 1)] + [(128 * (NT - 1), LAST)]
    return t + [(LK, LQ)] if layer == 2 else t


BEFORE_MAX = (6, 3, 3, 3)
KCHUNKS = ((0, 512), (512, 512), (1024, LK - 1024))


def project(*use):
    return ("p", *use)


def keys_of(layer):
    return [project("k", layer, g, c) for g in range(KV[layer] // 128) for c in range(len(KCHUNKS))]


def values_of(layer):
    return [project("v", layer, j) for j in range(NT // 2)]


def mixed(layer, room):
    keys, values = keys_of(layer), values_of(layer)
    return [(keys if c == "k" else values).pop(0) for c in "".join(room)] + keys + values


def chunk_of_layer1(c):
    return [project("at", c, 0), project("at", c, 1), project("k", 1, 0, c), project("k", 1, 1, c),
            project("v", 1, 2 * c), project("v", 1, 2 * c + 1)]


def fill(steps, work, room):
    assert len(steps) == len(room) and sum(room) == len(work), (len(steps), len(room), sum(room), len(work))
    out, done = [], 0
    for s, n in zip(steps, room):
        out += [s] + work[done:done + n]
        done += n
    return out


def score_steps(layer, group):
    return [("s", layer, p, h) for p in range(4 * group, 4 * group + 4) for h in range(len(units(layer)))]


def attend_steps(layer):
    out = []
    for g in range(GROUPS[layer]):
        ahead = score_steps(layer, g + 1) if g + 1 < GROUPS[layer] else []
        nt = len(key_tiles(layer))
        span = nt - BEFORE_MAX[layer]
        for t in range(nt):
            out.append(("t", layer, g, t))
            if t < span:
                out += ahead[len(ahead) * t // span:len(ahead) * (t + 1) // span]
            if ahead and t == span + (layer > 0):
                out.append(("m", layer, g + 1))
                out += [("mask",), ("stats",)] if layer == 3 else []
    return out + [("te", layer)]


def first_scores(layer, work, before, after):
    units = score_steps(layer, 0)
    n = len(work) - before - after
    room = [n * (i + 1) // len(units) - n * i // len(units) for i in range(len(units))]
    return (fill(units, work[:n], room) + work[n:n + before] + [("m", layer, 0)] + work[n + before:])


def batch_order():
    def chain(*names):
        return [("c", int(n[0]), n[1:]) for n in names]

    o = attend_steps(0)
    work = chunk_of_layer1(1) + chunk_of_layer1(2)
    o += fill(chain("0ot", "0norm_a", "0norm_b", "0ont", "0o", "1xt", "1q"), work[:sum(C0)], C0)
    o += first_scores(1, work[sum(C0):], 1, 1) + attend_steps(1)
    work, n = mixed(2, C1), len("".join(C1))
    o += fill(chain("1ot", "1norm", "1ont", "1o", "2xt", "2q", "2lat"), work[:n], [len(r) for r in C1])
    o += first_scores(2, work[n:], 1, 1) + attend_steps(2)
    work, n = mixed(3, C2), len("".join(C2))
    o += fill(chain("2ot", "2norm", "2ont", "2o", "2yt", "2up", "2down", "3xt", "3q"), work[:n],
              [len(r) for r in C2])
    o += first_scores(3, work[n:], 1, 1) + attend_steps(3)
    c = chain("3ot", "3norm", "3ont", "3o", "3yt", "3up", "3down")
    return o + fill([c[0], ("bias",), c[1], ("xt0",), ("q0",)] + c[2:], next_batch(), C3)


def first_order():
    work = next_batch()
    return [("mask",), ("stats",), ("bias",), ("xt0",), ("q0",)] + work


def next_batch():
    units = score_steps(0, 0)
    return ([project("ct", j) for j in range(NT // 2)] + [("ln",)] + [project("k", 0, 0, c) for c in range(3)]
            + [project("v0", j) for j in range(2)] + units + chunk_of_layer1(0)[:4] + [("m", 0, 0)]
            + chunk_of_layer1(0)[4:])


C0 = (1, 1, 1, 1, 3, 1, 1)
C1 = ("v", "v", "", "k", "k", "kk", "kk")
C2 = ("v", "k", "", "kv", "", "kk", "vv", "k", "k")
C3 = (2, 1, 2, 2, 2, 1, 6, 10, 2, 3)

ON_PE = {"xt", "q", "lat", "norm", "norm_a", "norm_b", "ont", "o", "yt", "up", "down"}


def fused_attention_kernel(nc, ctx, x, mask0, mask_bool, mask_int, w_kv, w_f, w_mlp, vecs, rows, out):
    with ExitStack() as es:
        def sb(name, shape, dt=F32):
            return es.enter_context(nc.sbuf_tensor(name, shape, dt))

        def pb(name, shape):
            return es.enter_context(nc.psum_tensor(name, shape, F32))

        score = pb("score", [128, 4, 512])
        accum = pb("accum", [128, 512])
        chain = pb("chain", [128, 512])
        proj = pb("proj", [128, 2, 512])

        raw = sb("raw", [128, NT, D])
        ctx_hi = sb("ctx_hi", [128, KT, LKP], F32R)
        ctx_lo = sb("ctx_lo", [128, KT, LKP], F32R)
        a_hi = sb("a_hi", [128, KT, 512], F32R)
        a_lo = sb("a_lo", [128, KT, 512], F32R)
        k0_hi = sb("k0_hi", [128, LK], F32R)
        k0_lo = sb("k0_lo", [128, LK], F32R)
        k_hi = sb("k_hi", [128, 2, LK + LQ], F32R)
        k_lo = sb("k_lo", [128, 2, LK + LQ], F32R)
        v0 = sb("v0", [128, NT, 8, 9])
        v = sb("v", [128, NT + 1, 16, 17])
        NPR = 4
        probs = sb("probs", [128, NPR, GW])
        q0_hi = sb("q0_hi", [128, 4 * GW], F32R)
        q_x = sb("q_x", [128, 4 * GW], F32R)
        rawmask = sb("rawmask", [128, LK])
        mask_row = sb("mask_row", [33, LK], BF16)
        mask_b = sb("mask_b", [128, LK], BF16)
        mask_i = sb("mask_i", [128, LK + LQ], BF16)
        key_bias = sb("key_bias", [128, 2, NT + 1])
        wkv_hi = sb("wkv_hi", [128, KT, KVCOLS], F32R)
        wkv_lo = sb("wkv_lo", [128, KT, KVCOLS], F32R)
        wf = sb("wf", [128, 8, KT, D])
        wmlp = sb("wmlp", [128, 4096])
        vp = sb("vp", [128, VPW])
        rp = sb("rp", [LQ, 11 * D])
        gate = sb("gate", [LQ, 1])
        tgate = sb("tgate", [LQ, 1])
        bk1 = sb("bk1", [128, 2])
        xcur = sb("xcur", [LQ, D])
        xres = sb("xres", [LQ, D])
        ya = sb("ya", [LQ, D])
        xt = sb("xt", [128, KT, LQ])
        x_next = sb("x_next", [LQ, D])
        xt_next = sb("xt_next", [128, KT, LQ])
        xres0 = sb("xres0", [LQ, D])
        q0s = sb("q0s", [64, 4 * LQ])
        xt_hi, xt_lo = a_hi[:, :, 0:LQ], a_lo[:, :, 0:LQ]
        hid, hu, ot, qs = probs[:, 0], probs[:, 1], probs[:, 2], probs[:, 2, 0:4 * LQ]
        ql = sb("ql", [128, 4 * LQ])
        qh = sb("qh", [128, 4 * LQ], F32R)
        row_max = sb("row_max", [PAIR, 16, 4])
        neg_max = sb("neg_max", [PAIR, 16])
        mx0_hi, mx0_lo = sb("mx0_hi", [4, 4, PAIR], F32R), sb("mx0_lo", [4, 4, PAIR], F32R)
        diag_max = q0_hi[0:4, 0:8 * PAIR]
        ones4 = sb("ones4", [4, 128], F32R)
        one_row = rawmask[0:1, :]
        one_bf = sb("one_bf", [33, 1], BF16)
        st = sb("st", [LQ, 16])
        rec = sb("rec", [LQ, 16])
        half_pow = sb("half_pow", [128, NT])
        cst = sb("cst", [128, NT, 6])
        cmv = sb("cmv", [128, NT, 2])
        cvar = sb("cvar", [128, NT])
        crs = sb("crs", [128, NT])
        cshift = sb("cshift", [128, NT])

        def vec(name, n=None, p0=0, p1=128):
            a, w = VP[name]
            return vp[p0:p1, a:a + w] if n is None else vp[p0:p1, a + n:a + n + 1]

        def row(name):
            return rp[:, RP[name] * D:(RP[name] + 1) * D]

        ident = vec("ident")
        up_w = wmlp[:, 0:2048].rearrange("p (k n) -> p k n", k=KT)
        down_w = wmlp[:, 2048:4096].rearrange("p (t n) -> p t n", t=8)
        wq = [wf[:, 2 * l] for l in range(4)]
        wo = [wf[:, 2 * l + 1] for l in range(4)]

        def sems(*names):
            return [es.enter_context(nc.semaphore(n)) for n in names]

        (setup_loaded, setup_mem, setup_gate, setup_split, setup_pe, setup_copied, setup_row, setup_fold) = sems(
            "setup_loaded", "setup_mem", "setup_gate", "setup_split", "setup_pe", "setup_copied", "setup_row",
            "setup_fold")
        turn = sems(
            "ctx_loaded", "x_loaded", "mask_loaded", "mlp_loaded", "max_moved", "out_stored",
            "proj_ready", "proj_hi", "proj_free0", "proj_free1",
            "unit_ready", "unit_read", "max_ready", "max_turned", "max_rows",
            "step_ready", "exp_done", "pv_done",
            "chain_pe", "chain_out", "dve_link", "var_ready", "rstd_ready", "act_in", "act_out",
            "q_ready", "qlo_ready", "mask_ready", "mask_wide", "bias_ready", "bias_done",
            "shift_ready", "norm_done", "ln1_ready", "q0_pe", "q0_out")
        (ctx_loaded, x_loaded, mask_loaded, mlp_loaded, max_moved, out_stored,
         proj_ready, proj_hi, proj_free0, proj_free1,
         unit_ready, unit_read, max_ready, max_turned, max_rows,
         step_ready, exp_done, pv_done,
         chain_pe, chain_out, dve_link, var_ready, rstd_ready, act_in, act_out,
         q_ready, qlo_ready, mask_ready, mask_wide, bias_ready, bias_done,
         shift_ready, norm_done, ln1_ready, q0_pe, q0_out) = turn
        turn_sems = range(turn[0].num, turn[-1].num + 1)
        assert len(turn_sems) == len(turn)
        proj_free = (proj_free0, proj_free1)

        unscaled = raw[:, 4:8, :].rearrange("p (k t) d -> p k (t d)", k=KT)
        with nc.Block() as block:
            @block.sync
            def _(sp):
                sp.dma_start(wmlp[:, 0:KT * KVCOLS], w_kv).then_inc(setup_loaded, 16)
                sp.dma_start(vp[:, :], vecs).then_inc(setup_loaded, 16)
                sp.dma_start(rp[:, 0:RPN * D], rows[0:1, 0:RPN * D].broadcast_to([LQ, RPN * D])).then_inc(setup_loaded, 16)
                sp.dma_start(gate[:, :], rows[0:1, RPN * D:RPN * D + 1].broadcast_to([LQ, 1])).then_inc(setup_loaded, 16)
                sp.dma_start(wf[:, :, :, :].rearrange("p a k n -> p (a k n)"), w_f).then_inc(setup_loaded, 16)
                sp.wait_ge(setup_mem, 6)
                sp.dma_start(k0_hi[120:121, :].bitcast(F32), one_row).then_inc(setup_row, 16)
                sp.dma_start(k0_lo[121:122, :].bitcast(F32), one_row).then_inc(setup_row, 16)
                sp.wait_ge(setup_row, 32)

            @block.gpsimd
            def _(pool):
                fills = [(k0_hi[96:128, :].bitcast(F32), 0.0), (k0_lo[96:128, :].bitcast(F32), 0.0), (one_row, 1.0),
                         (ones4[:, :].bitcast(F32), 1.0), (one_bf[:, :], 1.0), (half_pow[:, :], -0.5),
                         (raw[:, NT - 1, :], 0.0),
                         (v0[:, :, :, :], 1.0), (v[:, :, :, :], 1.0),
                         (mask_i[:, LK:LK + LQ], 0.0), (key_bias[:, :, :], 0.0)]
                for n, (tile, value) in enumerate(fills):
                    nc.gpsimd.memset(tile, value).then_inc(setup_mem, 1)
                    pool.wait_ge(setup_mem, n + 1)

            @block.scalar
            def _(act):
                act.wait_ge(setup_loaded, 80)
                nc.scalar.activation(tgate[:, :], gate[:, :], ACT.Tanh).then_inc(setup_gate, 1)

            @block.vector
            def _(dve):
                nc.vector.memset(accum[:, :], 0.0).then_inc(setup_split, 1)
                dve.wait_ge(setup_loaded, 80)
                src = wmlp[:, 0:KT * KVCOLS].rearrange("p (k n) -> p k n", k=KT)
                scaled = raw[:, 0:4, :].rearrange("p (k t) d -> p k (t d)", k=KT)
                for k in range(KT):
                    nc.vector.tensor_scalar(scaled[:, k, :], src[:, k, 128:640], vec("g1", k), None,
                                            ALU.mult).then_inc(setup_split, 1)
                dve.wait_ge(setup_split, 3)
                for k in range(KT):
                    nc.vector.tensor_copy(unscaled[:, k, :], src[:, k, 128:640]).then_inc(setup_split, 1)
                dve.wait_ge(setup_split, 5)
                for k in range(KT):
                    nc.vector.tensor_copy(src[:, k, 128:640], scaled[:, k, :]).then_inc(setup_split, 1)
                dve.wait_ge(setup_split, 7)
                nc.vector.tensor_copy(wkv_hi[:, :, :], src).then_inc(setup_split, 1)
                dve.wait_ge(setup_split, 8)
                nc.vector.tensor_tensor(wkv_lo[:, :, :], src, wkv_hi[:, :, :].bitcast(F32), ALU.subtract)\
                    .then_inc(setup_split, 1)
                for k in range(KT):
                    nc.vector.tensor_copy(xt[:, k, :], vec("b1", k).broadcast_to([128, LQ])).then_inc(setup_split, 1)
                e0, _ = VP["e56"]
                eye = vp[64:64 + LQ, e0:e0 + LQ].unsqueeze(1).broadcast_to([LQ, 32, LQ])
                nc.vector.tensor_copy(q0_hi[64:64 + LQ, :].rearrange("p (h q) -> p h q", h=32), eye)\
                    .then_inc(setup_split, 1)
                dve.wait_ge(setup_pe, 2)
                nc.vector.tensor_copy(bk1[:, :], chain[:, 0:2]).then_inc(setup_fold, 1)
                nc.vector.tensor_copy(row("bv1"), chain[0:LQ, 256:512]).then_inc(setup_fold, 1)

            @block.tensor
            def _(pe):
                pe.wait_ge(setup_split, 12)
                w = unscaled
                for g in range(2):
                    for k in range(KT):
                        mm = nc.tensor.matmul(chain[:, g:g + 1], w[:, k, g * 128:(g + 1) * 128],
                                              vec("b1", k), start=(k == 0), stop=(k == KT - 1))
                mm.then_inc(setup_pe, 1)
                for k in range(KT):
                    mm = nc.tensor.matmul(chain[0:LQ, 256:512], xt[:, k, :], w[:, k, 256:512],
                                          start=(k == 0), stop=(k == KT - 1))
                mm.then_inc(setup_pe, 1)

        def turn_block(order, batch, ahead):
            looped = batch is not None
            uses, use_no = [s for s in order if s[0] == "p"], {}
            for n, s in enumerate(uses):
                use_no[s] = n
            chain_steps = [s for s in order if s[0] == "c"]
            out_before = {s: n for n, s in enumerate(chain_steps)}
            pe_before = {s: sum(t[2] in ON_PE for t in chain_steps[:n]) for n, s in enumerate(chain_steps)}
            unit_steps = [s for s in order if s[0] == "s"]
            unit_no = {s: n for n, s in enumerate(unit_steps)}
            layers = range(4) if looped else ()
            steps_of = [GROUPS[l] * len(key_tiles(l)) for l in range(4)]
            steps_before = [sum(steps_of[:l]) for l in range(5)]
            max_steps = [s for s in order if s[0] == "m"]
            max_no = {s: n + 1 for n, s in enumerate(max_steps)}
            rows_no = {s: sum(1 + (r[1] == 0) for r in max_steps[:n + 1]) for n, s in enumerate(max_steps)}

            def slot(s):
                n = unit_no[s]
                return score[:, n % 4] if s[2] < 4 else proj[:, n % 2]

            def slot_mates(s):
                n = unit_no[s]
                return [m for u, m in unit_no.items() if m < n and (u[2] < 4) == (s[2] < 4)
                        and (n - m) % (4 if s[2] < 4 else 2) == 0]

            def max_before(s):
                before = [m for m in max_steps if order.index(m) < order.index(s)]
                return before[-1] if before else None

            def units_out_before(s):
                return sum(t[0] == "s" for t in order[:order.index(s)])


            def steps_out_before(s):
                return sum(t[0] == "c" for t in order[:order.index(s)])

            q_no = {1: 1, 2: 2, 3: 3, 0: 4} if looped else {0: 1}
            norm_no = {(0, "o"): 1, (2, "o"): 2, (3, "pre"): 3, (3, "o"): 5}
            ln_no = 4 if looped else 1

            def k_bias(l, g):
                return bk1[:, g:g + 1] if l == 1 else vec("bk%d" % l, g)

            with nc.Block() as block:
                @block.sync
                def _(sp):
                    def move_max(g):
                        sp.wait_ge(max_rows, rows_no[("m", 0, g)])
                        for row, part in ((120, mx0_hi), (121, mx0_lo)):
                            sp.dma_start(q0_hi[row:row + 1, g * GW:(g + 1) * GW].bitcast(F32),
                                         part[:, g, :].bitcast(F32)).then_inc(max_moved, 16)

                    sp.dma_start(x_next[:, :], x[ahead]).then_inc(x_loaded, 16)
                    sp.dma_start(rawmask[64:64 + LQ, :], mask0[ahead]).then_inc(mask_loaded, 16)
                    sp.dma_start(rawmask[0:1, :].bitcast(I32), mask_int[ahead]).then_inc(mask_loaded, 16)
                    sp.dma_start(rawmask[32:33, 0:LK // 4].bitcast(U8), mask_bool[ahead]).then_inc(mask_loaded, 16)
                    if looped:
                        sp.dma_start(wmlp[:, :], w_mlp[0]).then_inc(mlp_loaded, 16)
                        for g in (1, 2, 3):
                            move_max(g)
                        sp.wait_ge(proj_ready, use_no[("p", "at", 2, 1)] + 1)
                    sp.dma_start(raw[:, 0:NT - 1, :],
                                 ctx[ahead][0:128 * (NT - 1), :].rearrange("(t p) d -> p t d", p=128))\
                        .then_inc(ctx_loaded, 16)
                    sp.dma_start(raw[0:LAST, NT - 1, :], ctx[ahead][128 * (NT - 1):LK, :]).then_inc(ctx_loaded, 16)
                    if looped:
                        sp.wait_ge(chain_pe, pe_before[("c", 2, "down")] + 1)
                        sp.dma_start(wmlp[:, :], w_mlp[1]).then_inc(mlp_loaded, 16)
                        sp.wait_ge(chain_out, out_before[("c", 3, "down")] + 1)
                        sp.dma_start(out[batch], ya[:, :]).then_inc(out_stored, 16)
                    move_max(0)
                    if looped:
                        sp.wait_ge(out_stored, 16)
                    sp.wait_ge(max_moved, 128 if looped else 32)

                @block.gpsimd
                def _(pool):
                    def rstd(n, o, i, w):
                        pool.wait_ge(var_ready, n)
                        nc.gpsimd.tensor_tensor(o, i, w, ALU.pow).then_inc(rstd_ready, 1)
                        pool.wait_ge(rstd_ready, n)

                    for s in order:
                        if s[0] == "q0" or s[0] == "c" and s[2] == "q":
                            l = 0 if s[0] == "q0" else s[1]
                            pool.wait_ge(q_ready, q_no[l])
                            if l == 0:
                                hm = vec("hm0", None, 0, 64).unsqueeze(2).broadcast_to([64, 8, 4 * LQ])
                                src = ql[0:64, :].unsqueeze(1).broadcast_to([64, 8, 4 * LQ])
                                nc.gpsimd.tensor_tensor(q_x[0:64, :].rearrange("p (h c) -> p h c", h=8), src, hm,
                                                        ALU.mult).then_inc(qlo_ready, 1)
                            else:
                                for g in range(2):
                                    hm = vec("hm").unsqueeze(2).broadcast_to([128, 8, LQ])
                                    src = ql[:, g * LQ:(g + 1) * LQ].unsqueeze(1).broadcast_to([128, 8, LQ])
                                    ins = nc.gpsimd.tensor_tensor(
                                        q_x[:, (2 + g) * GW:(3 + g) * GW].rearrange("p (h q) -> p h q", h=8),
                                        src, hm, ALU.mult)
                                ins.then_inc(qlo_ready, 1)
                            pool.wait_ge(qlo_ready, q_no[l])
                        if s[0] == "c" and s[1:] in ((0, "o"), (2, "o"), (3, "o")):
                            rstd(norm_no[s[1:]], st[:, 9:10], st[:, 8:9], half_pow[0:LQ, 0:1])
                        if s[0] == "c" and s[1:] == (3, "xt"):
                            rstd(norm_no[(3, "pre")], st[:, 9:10], st[:, 8:9], half_pow[0:LQ, 0:1])
                        if s[0] == "mask":
                            pool.wait_ge(mask_ready, 2)
                            if looped:
                                pool.wait_ge(unit_read, units_out_before(s))
                            nc.gpsimd.partition_broadcast(mask_b[:, 0:LK], mask_row[32:33, :]).then_inc(mask_wide, 1)
                            pool.wait_ge(mask_wide, 1)
                            nc.gpsimd.partition_broadcast(mask_i[:, 0:LK], mask_row[0:1, :]).then_inc(mask_wide, 1)
                            pool.wait_ge(mask_wide, 2)
                        if s[0] == "stats":
                            rstd(ln_no, crs[:, :], cvar[:, :], half_pow[:, :])
                        if s[0] == "ln":
                            pool.wait_ge(proj_ready, use_no[("p", "ct", NT // 2 - 1)] + 1)
                            pool.wait_ge(shift_ready, 1)
                            for t in range(NT):
                                ins = nc.gpsimd.tensor_scalar(raw[:, t, :], raw[:, t, :], crs[:, t:t + 1],
                                                              cshift[:, t:t + 1], ALU.mult, ALU.add)
                            ins.then_inc(norm_done, 1)

                @block.scalar
                def _(act):
                    def evacuate_hi(s):
                        n = use_no[s]
                        b = n % 2
                        act.wait_ge(proj_ready, n + 1)
                        kind = s[1]
                        if kind in ("ct", "at"):
                            src = proj[:, b, :].rearrange("p (t k c) -> p t k c", t=2, k=KT)
                            if kind == "ct":
                                dst = ctx_hi[:, :, s[2] * 256:(s[2] + 1) * 256]
                            else:
                                dst = a_hi[:, :, s[3] * 256:(s[3] + 1) * 256]
                            nc.scalar.activation(dst.rearrange("p k (t c) -> p t k c", t=2), src, ACT.Copy)\
                                .then_inc(proj_hi, 1)
                        elif kind == "k":
                            l, g, c = s[2:]
                            k, w = KCHUNKS[c]
                            if l == 0:
                                nc.scalar.activation(rawmask[64:128, k:k + w], proj[64:128, b, 0:w], ACT.Copy)
                                nc.scalar.activation(k0_hi[0:64, k:k + w], proj[0:64, b, 0:w], ACT.Identity,
                                                     bias=vec("bk0", 0, 0, 64)).then_inc(proj_hi, 1)
                            else:
                                nc.scalar.activation(k_hi[:, g, k:k + w], proj[:, b, 0:w], ACT.Identity,
                                                     bias=k_bias(l, g)).then_inc(proj_hi, 1)
                        elif kind == "v0":
                            j = s[2]
                            nc.scalar.activation(v0[:, 6 * j:6 * j + 6, :, 0:8],
                                                 proj[:, b, 0:384].rearrange("p (t h d) -> p t h d", t=6, h=8),
                                                 ACT.Copy).then_inc(proj_free[b], 1)
                        else:
                            j = s[3]
                            nc.scalar.activation(v[:, 2 * j:2 * j + 2, :, 0:16],
                                                 proj[:, b, :].rearrange("p (t h d) -> p t h d", t=2, h=16),
                                                 ACT.Copy).then_inc(proj_free[b], 1)

                    tanh_no = 0
                    for s in order:
                        if s[0] == "p":
                            evacuate_hi(s)
                        elif s[0] == "t":
                            _, l, g, t = s
                            j = steps_before[l] + g * len(key_tiles(l)) + t
                            kt = key_tiles(l)[t][1]
                            act.wait_ge(step_ready, j + 1)
                            if j >= NPR:
                                act.wait_ge(pv_done, j - NPR + 1)
                            bias = 0.0 if l == 0 else key_bias[0:kt, int(l == 2), t:t + 1]
                            nc.scalar.activation(probs[0:kt, j % NPR, :], score[0:kt, j % 4, 0:GW], ACT.Exp,
                                                 bias=bias).then_inc(exp_done, 1)
                        elif s[0] == "c" and s[2] == "up":
                            tanh_no += 1
                            act.wait_ge(act_in, tanh_no)
                            nc.scalar.activation(hu[:, :], hu[:, :], ACT.Tanh, scale=GELU_S).then_inc(act_out, 1)

                @block.vector
                def _(dve):
                    linked = [0]

                    def link(ins):
                        linked[0] += 1
                        ins.then_inc(dve_link, 1)
                        dve.wait_ge(dve_link, linked[0])

                    tt, ts, stt, cp = (nc.vector.tensor_tensor, nc.vector.tensor_scalar,
                                       nc.vector.scalar_tensor_tensor, nc.vector.tensor_copy)

                    def evacuate_lo(s):
                        n, kind = use_no[s], s[1]
                        b = n % 2
                        if kind in ("v", "v0"):
                            return
                        dve.wait_ge(proj_hi, sum(u[1] not in ("v", "v0") for u in uses[:n]) + 1)
                        if kind in ("ct", "at"):
                            src = proj[:, b, :].rearrange("p (t k c) -> p k t c", t=2, k=KT)
                            hi, lo = (ctx_hi, ctx_lo) if kind == "ct" else (a_hi, a_lo)
                            c = (s[2] if kind == "ct" else s[3]) * 256
                            for k in range(KT):
                                ins = tt(lo[:, k, c:c + 256].rearrange("p (t c) -> p t c", t=2), src[:, k],
                                         hi[:, k, c:c + 256].bitcast(F32).rearrange("p (t c) -> p t c", t=2),
                                         ALU.subtract)
                            ins.then_inc(proj_free[b], 1)
                        else:
                            l, g, c = s[2:]
                            k, w = KCHUNKS[c]
                            if l == 0:
                                stt(k0_lo[0:64, k:k + w], proj[0:64, b, 0:w], vec("bk0", 0, 0, 64),
                                    k0_hi[0:64, k:k + w].bitcast(F32), ALU.add, ALU.subtract)\
                                    .then_inc(proj_free[b], 1)
                            else:
                                stt(k_lo[:, g, k:k + w], proj[:, b, 0:w], k_bias(l, g),
                                    k_hi[:, g, k:k + w].bitcast(F32), ALU.add, ALU.subtract)\
                                    .then_inc(proj_free[b], 1)

                    def unit_max(s):
                        _, l, p, h = s
                        n = unit_no[s]
                        k, w = units(l)[h]
                        dve.wait_ge(unit_ready, n + 1)
                        src = slot(s)[0:PAIR, 0:w]
                        if l == 0:
                            ins = nc.vector.tensor_reduce(row_max[:, p, h:h + 1], src, AX.X, ALU.max)
                        else:
                            m = mask_i if l == 2 else mask_b
                            ins = nc.vector.tensor_tensor_reduce(src, src, m[0:PAIR, k:k + w], 1.0, -3.0e38,
                                                                 ALU.add, ALU.max, row_max[:, p, h:h + 1])
                        ins.then_inc(unit_read, 1)

                    def max_to_rows(s):
                        _, l, g = s
                        dve.wait_ge(unit_read, units_out_before(s))
                        nc.vector.tensor_reduce(neg_max[:, 4 * g:4 * g + 4], row_max[:, 4 * g:4 * g + 4, 0:len(units(l))], AX.X,
                                                ALU.max, negate=True).then_inc(max_ready, 1)
                        dve.wait_ge(max_turned, max_no[s])
                        if l == 0:
                            cp(mx0_hi[:, g, :], chain[0:4, 0:PAIR]).then_inc(max_rows, 1)
                            dve.wait_ge(max_rows, rows_no[s] - 1)
                            tt(mx0_lo[:, g, :], chain[0:4, 0:PAIR], mx0_hi[:, g, :].bitcast(F32), ALU.subtract)\
                                .then_inc(max_rows, 1)
                        else:
                            tt(diag_max[:, g * GW:(g + 1) * GW].rearrange("p (h c) -> p h c", h=4),
                               chain[0:4, 0:PAIR].unsqueeze(1).broadcast_to([4, 4, PAIR]),
                               vec("ident", None, 0, 4)[:, 0:4].unsqueeze(2).broadcast_to([4, 4, PAIR]),
                               ALU.mult).then_inc(max_rows, 1)

                    def stats(src, n, centred):
                        if centred:
                            link(nc.vector.bn_stats(st[:, 0:6], src))
                            link(nc.vector.bn_aggr(st[:, 6:8], st[:, 0:6]))
                            ts(st[:, 8:9], st[:, 7:8], 1e-6 if n == 1 else 1e-5, None, ALU.add).then_inc(var_ready, 1)
                        else:
                            link(nc.vector.tensor_tensor_reduce(hid[0:LQ, 0:D], src, src, 1.0, 0.0, ALU.mult, ALU.add,
                                                                st[:, 7:8]))
                            ts(st[:, 8:9], st[:, 7:8], 1.0 / D, 1e-6, ALU.mult, ALU.add).then_inc(var_ready, 1)
                        dve.wait_ge(rstd_ready, n)

                    def spread_queries(l, src, scaled):
                        p, n = (64, 4) if l == 0 else (128, 2)
                        w = n * LQ
                        if l == 1:
                            link(ts(scaled[:, 0:w], src[:, 0:w], SCALE[l], None, ALU.mult))
                        else:
                            for g in range(n):
                                ins = ts(scaled[0:p, g * LQ:(g + 1) * LQ], src[0:p, g * LQ:(g + 1) * LQ],
                                         vec("bq%d" % l, g, 0, p), SCALE[l], ALU.add, ALU.mult)
                            link(ins)
                        link(cp(qh[0:p, 0:w], scaled[0:p, 0:w]))
                        if q_no[l] > 1:
                            dve.wait_ge(qlo_ready, q_no[l] - 1)
                        tt(ql[0:p, 0:w], scaled[0:p, 0:w], qh[0:p, 0:w].bitcast(F32), ALU.subtract)\
                            .then_inc(q_ready, 1)
                        if l == 0:
                            return tt(q0_hi[0:64, :].rearrange("p (h c) -> p h c", h=8),
                                      qh[0:64, :].bitcast(F32).unsqueeze(1).broadcast_to([64, 8, w]),
                                      vec("hm0", None, 0, 64).unsqueeze(2).broadcast_to([64, 8, w]), ALU.mult)
                        for g in range(2):
                            ins = tt(q_x[:, g * GW:(g + 1) * GW].rearrange("p (h q) -> p h q", h=8),
                                     qh[:, g * LQ:(g + 1) * LQ].bitcast(F32).unsqueeze(1).broadcast_to([128, 8, LQ]),
                                     vec("hm").unsqueeze(2).broadcast_to([128, 8, LQ]), ALU.mult)
                        return ins

                    def chain_step(s):
                        _, l, name = s
                        if name in ON_PE:
                            dve.wait_ge(chain_pe, pe_before[s] + 1)
                        if out_before[s]:
                            dve.wait_ge(chain_out, out_before[s])
                        last = None
                        if name == "ot":
                            dve.wait_ge(pv_done, steps_before[l + 1])
                            w = 448 if l == 0 else 224
                            last = cp(ot[:, 0:w], accum[:, 0:w])
                        elif name in ("norm", "norm_a", "norm_b"):
                            half, hd = name == "norm_b", 8 if l == 0 else 16
                            full = chain[0:LQ, :].rearrange("q (c j e) -> q c j e", c=4, j=4)
                            link(nc.vector.reciprocal(rec[:, :].rearrange("q (c j) -> q c j", c=4), full[:, :, :, hd]))
                            by_head = rec[:, :].rearrange("q (c j) -> q c j", c=4)
                            if l == 0:
                                dst = ya[:, half * 128:half * 128 + 128]\
                                    .rearrange("q (g j x d) -> q g x j d", g=2, j=4, x=2)
                                for c in range(4):
                                    ins = tt(dst[:, c // 2, c % 2], full[:, c, :, 0:hd],
                                             by_head[:, c].unsqueeze(2).broadcast_to([LQ, 4, hd]), ALU.mult)
                            else:
                                ins = tt(ya[:, :].rearrange("q (h d) -> q h d", h=16),
                                         chain[0:LQ, :].rearrange("q (h e) -> q h e", h=16)[:, :, 0:hd],
                                         rec[:, :].unsqueeze(2).broadcast_to([LQ, 16, hd]), ALU.mult)
                            if name == "norm_a":
                                last = ins
                            else:
                                link(ins)
                                last = tt(ya[:, :], ya[:, :], row("bv%d" % l), ALU.add)
                        elif name == "ont":
                            last = cp(xt[:, :, :], chain[:, 0:KT * LQ].rearrange("p (k q) -> p k q", k=KT))
                        elif name == "o":
                            y = chain[0:LQ, 0:D]
                            if l == 0:
                                link(tt(ya[:, :], y, xres0[:, :], ALU.add))
                                stats(ya[:, :], norm_no[(0, "o")], True)
                                link(ts(ya[:, :], ya[:, :], st[:, 6:7], st[:, 9:10], ALU.subtract, ALU.mult))
                                link(tt(ya[:, :], ya[:, :], row("g0"), ALU.mult))
                                last = tt(xcur[:, :], ya[:, :], row("be0"), ALU.add)
                            elif l == 1:
                                last = stt(xcur[:, :], y, tgate[:, 0:1], xcur[:, :], ALU.mult, ALU.add)
                            elif l == 2:
                                link(tt(ya[:, :], y, xres[:, :], ALU.add))
                                stats(ya[:, :], norm_no[(2, "o")], False)
                                last = ts(ya[:, :], ya[:, :], st[:, 9:10], None, ALU.mult)
                            else:
                                link(tt(xcur[:, :], y, xres[:, :], ALU.add))
                                stats(xcur[:, :], norm_no[(3, "o")], True)
                                last = ts(ya[:, :], xcur[:, :], st[:, 6:7], st[:, 9:10], ALU.subtract, ALU.mult)
                        elif name == "yt":
                            src = chain[:, 0:KT * LQ].rearrange("p (k q) -> p k q", k=KT)
                            for k in range(KT):
                                if l == 2:
                                    last = ts(xt[:, k, :], src[:, k, :], vec("pw", k), None, ALU.mult)
                                else:
                                    last = ts(xt[:, k, :], src[:, k, :], vec("ln2w", k), vec("ln2b", k),
                                              ALU.mult, ALU.add)
                        elif name == "up":
                            b = vec("mb%d" % l).unsqueeze(2).broadcast_to([128, 8, LQ])
                            link(tt(hid[:, :].rearrange("p (t q) -> p t q", t=8),
                                    chain[:, 0:GW].rearrange("p (t q) -> p t q", t=8), b, ALU.add))
                            link(stt(hu[:, :], hid[:, :], GELU_C, hid[:, :], ALU.mult, ALU.mult))
                            stt(hu[:, :], hu[:, :], 1.0, hid[:, :], ALU.add, ALU.mult).then_inc(act_in, 1)
                            dve.wait_ge(act_out, 1 if l == 2 else 2)
                            last = stt(hid[:, :], hu[:, :], 1.0, hid[:, :], ALU.add, ALU.mult)
                        elif name == "down":
                            link(tt(xres[:, :], xcur[:, :], row("b22" if l == 2 else "b23"), ALU.add))
                            last = stt(xcur[:, :] if l == 2 else ya[:, :], chain[0:LQ, 0:D], 0.5, xres[:, :],
                                       ALU.mult, ALU.add)
                        elif name == "xt":
                            src = chain[:, 0:KT * LQ].rearrange("p (k q) -> p k q", k=KT)
                            if l == 3:
                                for k in range(KT):
                                    last = ts(xt[:, k, :], src[:, k, :], vec("ln1w", k), vec("ln1b", k),
                                              ALU.mult, ALU.add)
                            elif l == 2:
                                link(cp(xt[:, :, :], src))
                                link(cp(xt_hi, xt[:, :, :]))
                                last = tt(xt_lo, xt[:, :, :], xt_hi.bitcast(F32), ALU.subtract)
                            else:
                                last = cp(xt[:, :, :], src)
                        elif name == "q":
                            last = spread_queries(l, chain, qs)
                        elif name == "lat":
                            for g in range(2):
                                link(ts(qs[:, g * LQ:(g + 1) * LQ], chain[:, g * LQ:(g + 1) * LQ],
                                        vec("bk2", g), None, ALU.add))
                            for g in range(2):
                                link(cp(k_hi[:, g, LK:LK + LQ], qs[:, g * LQ:(g + 1) * LQ]))
                            for g in range(2):
                                tt(k_lo[:, g, LK:LK + LQ], qs[:, g * LQ:(g + 1) * LQ],
                                   k_hi[:, g, LK:LK + LQ].bitcast(F32), ALU.subtract)
                            last = cp(v[0:LQ, NT, :, 0:16], chain[0:LQ, 256:512].rearrange("q (h d) -> q h d", h=16))
                        last.then_inc(chain_out, 1)

                    def before(s):
                        _, l, name = s
                        if name == "xt":
                            if l in (2, 3):
                                if out_before[s]:
                                    dve.wait_ge(chain_out, out_before[s])
                                ins = tt(xres[:, :], xcur[:, :], row("ob2" if l == 2 else "cb3"), ALU.add)
                                if l == 3:
                                    stats(xcur[:, :], norm_no[(3, "pre")], True)
                                    ts(ya[:, :], xcur[:, :], st[:, 6:7], st[:, 9:10], ALU.subtract, ALU.mult)\
                                        .then_inc(ln1_ready, 1)

                    for s in order:
                        if s[0] == "p":
                            evacuate_lo(s)
                        elif s[0] == "s":
                            unit_max(s)
                        elif s[0] == "m":
                            max_to_rows(s)
                        elif s[0] == "xt0":
                            dve.wait_ge(x_loaded, 16)
                            tt(xres0[:, :], x_next[:, :], row("bo0"), ALU.add)
                            dve.wait_ge(q0_pe, 1)
                            cp(xt_next[:, :, :], score[:, 2, 0:KT * LQ].rearrange("p (k q) -> p k q", k=KT))\
                                .then_inc(q0_out, 1)
                        elif s[0] == "q0":
                            dve.wait_ge(q0_pe, 2)
                            spread_queries(0, score[:, 3], q0s).then_inc(q0_out, 1)
                        elif s[0] == "c":
                            before(s)
                            chain_step(s)
                        elif s[0] == "mask":
                            dve.wait_ge(mask_loaded, 48)
                            link(cp(k0_hi[64:64 + LQ, :], rawmask[64:64 + LQ, :]))
                            tt(k0_lo[64:64 + LQ, :], rawmask[64:64 + LQ, :], k0_hi[64:64 + LQ, :].bitcast(F32),
                               ALU.subtract)
                            ts(mask_row[0:1, :], rawmask[0:1, :].bitcast(I32), 0, NEG, ALU.is_equal, ALU.mult)\
                                .then_inc(mask_ready, 1)
                            ts(mask_row[32:33, :], rawmask[32:33, 0:LK // 4].bitcast(U8), 0, NEG, ALU.is_equal,
                               ALU.mult).then_inc(mask_ready, 1)
                        elif s[0] == "bias":
                            dve.wait_ge(bias_ready, 1)
                            if looped:
                                dve.wait_ge(exp_done, steps_before[4])
                            for m in range(2):
                                src = (score[:, 0], chain)[m]
                                cp(key_bias[:, m, 0:NT - 1], src[:, 0:NT - 1])
                                ins = cp(key_bias[0:LAST, m, NT - 1:NT], src[0:LAST, NT - 1:NT])
                            ins.then_inc(bias_done, 1)
                        elif s[0] == "stats":
                            dve.wait_ge(ctx_loaded, 32)
                            for t in range(NT):
                                ins = nc.vector.bn_stats(cst[:, t, :], raw[:, t, :])
                            link(ins)
                            for t in range(NT):
                                ins = nc.vector.bn_aggr(cmv[:, t, :], cst[:, t, :])
                            link(ins)
                            ts(cvar[:, :], cmv[:, :, 1], 1e-5, None, ALU.add).then_inc(var_ready, 1)
                        elif s[0] == "ln":
                            dve.wait_ge(rstd_ready, ln_no)
                            stt(cshift[:, :], cmv[:, :, 0], -1.0, crs[:, :], ALU.mult, ALU.mult)\
                                .then_inc(shift_ready, 1)

                @block.tensor
                def _(pe):
                    mm = nc.tensor.matmul

                    def mm3(o, lh, ll, rh, rl, first=True, last=True):
                        mm(o, lh, rh, start=first, stop=False)
                        mm(o, ll, rh, start=False, stop=False)
                        return mm(o, lh, rl, start=False, stop=last)

                    def project_use(s):
                        n, kind = use_no[s], s[1]
                        b = n % 2
                        if n >= 2:
                            pe.wait_ge(proj_free[b], n // 2)
                        if kind in ("ct", "at"):
                            if kind == "ct":
                                pe.wait_ge(ctx_loaded, 32)
                            elif s[2] == 0:
                                pe.wait_ge(norm_done, 1)
                            t0 = 2 * s[2] if kind == "ct" else 4 * s[2] + 2 * s[3]
                            for t in range(2):
                                for k in range(KT):
                                    ins = nc.tensor.transpose(proj[:, b, (2 * t + k) * 128:(2 * t + k + 1) * 128],
                                                              raw[:, t0 + t, k * 128:(k + 1) * 128], ident)
                        elif kind == "k":
                            l, g, c = s[2:]
                            k0, w = KCHUNKS[c]
                            m = 128
                            if l == 1:
                                sh, sl, at = a_hi, a_lo, 0
                                wait_lo(("p", "at", c, 1))
                            else:
                                sh, sl, at = ctx_hi, ctx_lo, k0
                                if l == 0:
                                    wait_lo(("p", "ct", NT // 2 - 1))
                            o = KOFF[l] + g * 128
                            for k in range(KT):
                                ins = mm3(proj[0:m, b, 0:w], wkv_hi[:, k, o:o + m], wkv_lo[:, k, o:o + m],
                                          sh[:, k, at:at + w], sl[:, k, at:at + w], k == 0, k == KT - 1)
                        elif kind == "v0":
                            if s[2] == 0:
                                wait_lo(("p", "k", 0, 0, 2))
                            for i in range(6):
                                k, kn = key_tiles(0)[6 * s[2] + i]
                                ins = nc.tensor.transpose(proj[0:kn, b, i * 64:(i + 1) * 64],
                                                          rawmask[64:128, k:k + kn],
                                                          ident[64:128, 64:128])
                        else:
                            l, o = s[2], KOFF[s[2]] + 256
                            for i, t in enumerate((2 * s[3], 2 * s[3] + 1)):
                                if l == 1:
                                    sh, sl, at = a_hi, a_lo, (t % 4) * 128
                                else:
                                    sh, sl, at = ctx_hi, ctx_lo, t * 128
                                w = KV[l]
                                for k in range(KT):
                                    ins = mm3(proj[:, b, i * w:(i + 1) * w], sh[:, k, at:at + 128],
                                              sl[:, k, at:at + 128], wkv_hi[:, k, o:o + w], wkv_lo[:, k, o:o + w],
                                              k == 0, k == KT - 1)
                        ins.then_inc(proj_ready, 1)

                    def wait_lo(s):
                        n = use_no[s]
                        pe.wait_ge(proj_free[n % 2], n // 2 + 1)
                        pe.wait_ge(proj_free[1 - n % 2], (n + 1) // 2)

                    def last_use_before(s):
                        done = [t for t in order[:order.index(s)] if t[0] == "p"]
                        return done[-1] if done else None

                    def score_unit(s):
                        _, l, p, h = s
                        bank = slot(s)
                        if p == 0 and h == 0:
                            if l:
                                pe.wait_ge(exp_done, steps_before[l])
                                pe.wait_ge(chain_out, out_before[("c", l, "q")] + 1)
                                if l == 2:
                                    pe.wait_ge(chain_out, out_before[("c", 2, "lat")] + 1)
                                wait_lo(("p", "k", l, 0, 2))
                            else:
                                pe.wait_ge(bias_done, 1)
                                pe.wait_ge(q0_out, 2)
                                wait_lo(("p", "k", 0, 0, 2))
                        elif p == 4 and h == 0:
                            use = last_use_before(s)
                            if use:
                                wait_lo(use)
                        if slot_mates(s):
                            pe.wait_ge(unit_read, slot_mates(s)[-1] + 1)
                        c, w = units(l)[h]
                        o = bank[0:PAIR, 0:w]
                        if l == 0:
                            q = q0_hi[0:120, p * PAIR:(p + 1) * PAIR]
                            mm(o, q, k0_hi[0:120, c:c + w], start=True, stop=False)
                            ins = mm(o, q, k0_lo[0:120, c:c + w], start=False, stop=True)
                        else:
                            ins = mm(o, q_x[:, p * PAIR:(p + 1) * PAIR], k_hi[:, p // 4, c:c + w],
                                     start=True, stop=True)
                        ins.then_inc(unit_ready, 1)

                    def turn_max(s):
                        _, l, g = s
                        pe.wait_ge(max_ready, max_no[s])
                        if chain_steps and steps_out_before(s):
                            pe.wait_ge(chain_out, steps_out_before(s))
                        if max_no[s] > 1:
                            pe.wait_ge(max_rows, rows_no[max_steps[max_no[s] - 2]])
                        nc.tensor.transpose(chain[0:4, 0:PAIR], neg_max[:, 4 * g:4 * g + 4], ident[0:PAIR, 0:PAIR])\
                            .then_inc(max_turned, 1)

                    opened = [None, set()]

                    def scores_t(l, g, t):
                        j = steps_before[l] + g * len(key_tiles(l)) + t
                        k, kn = key_tiles(l)[t]
                        if t == 0:
                            if l:
                                pe.wait_ge(max_rows, rows_no[("m", l, g)])
                            elif g:
                                pe.wait_ge(max_moved, 32 * g)
                        if l and g == 0 and t == 0:
                            pe.wait_ge(qlo_ready, q_no[l])
                            pe.wait_ge(unit_read, units_out_before(("m", l, 0)))
                            pe.wait_ge(chain_out, out_before[("c", l - 1, "ot")] + 1)
                        if j - steps_before[l] >= 4:
                            pe.wait_ge(exp_done, j - 3)
                        o = score[0:kn, j % 4, 0:GW]
                        if l == 0:
                            q = q0_hi[0:122, g * GW:(g + 1) * GW]
                            mm(o, k0_hi[0:122, k:k + kn], q, start=True, stop=False)
                            mm(o, k0_lo[0:122, k:k + kn], q, start=False, stop=False)
                            ins = mm(o, k0_hi[0:64, k:k + kn], q_x[0:64, g * GW:(g + 1) * GW],
                                     start=False, stop=True)
                        else:
                            mm3(o, k_hi[:, g, k:k + kn], k_lo[:, g, k:k + kn],
                                q_x[:, g * GW:(g + 1) * GW], q_x[:, (2 + g) * GW:(3 + g) * GW], True, False)
                            ins = mm(o, ones4[:, 0:kn], diag_max[:, g * GW:(g + 1) * GW], start=False, stop=True)
                        ins.then_inc(step_ready, 1)

                    def values(l, g, t):
                        j = steps_before[l] + g * len(key_tiles(l)) + t
                        kn = key_tiles(l)[t][1]
                        if opened[0] != l:
                            opened[:] = l, set()
                            if l:
                                wait_lo(("p", "v", l, NT // 2 - 1))
                        pe.wait_ge(exp_done, j + 1)
                        parts, hd, vt = (4, 8, v0) if l == 0 else (8, 16, v)
                        w = GW // parts
                        for i in range(parts):
                            n = g * parts + i
                            h = n // 2 if l == 0 else n
                            quad, c = n % 4, (n // 4) * w
                            ins = mm(accum[32 * quad:32 * quad + hd + 1, c:c + w], vt[0:kn, t, h, :],
                                     probs[0:kn, j % NPR, i * w:(i + 1) * w],
                                     start=quad not in opened[1], stop=(t == len(key_tiles(l)) - 1),
                                     skip_group_check=True)
                            opened[1].add(quad)
                        ins.then_inc(pv_done, 1)

                    lagging = [s[1:] for s in order if s[0] == "t"]

                    def chain_part(s):
                        _, l, name = s
                        if name not in ON_PE:
                            return
                        if name == "xt":
                            if l == 3:
                                pe.wait_ge(ln1_ready, 1)
                        if out_before[s]:
                            pe.wait_ge(chain_out, out_before[s])
                        if s == ("c", 3, "norm"):
                            pe.wait_ge(bias_done, 1)
                        if l == 3 and max_before(s):
                            pe.wait_ge(max_rows, rows_no[max_before(s)])
                        if name in ("norm", "norm_a", "norm_b"):
                            base = 4 if name == "norm_b" else 0
                            for c in range(4):
                                ins = nc.tensor.transpose(chain[0:LQ, c * 128:(c + 1) * 128],
                                                          ot[:, (base + c) * LQ:(base + c + 1) * LQ], ident)
                        elif name in ("xt", "ont", "yt"):
                            src = xcur if name == "xt" and l != 3 else ya
                            for k in range(KT):
                                ins = nc.tensor.transpose(chain[:, k * LQ:(k + 1) * LQ],
                                                          src[:, k * 128:(k + 1) * 128], ident[0:LQ, 0:LQ])
                        elif name == "o":
                            for k in range(KT):
                                ins = mm(chain[0:LQ, 0:D], xt[:, k, :], wo[l][:, k, :], start=(k == 0),
                                         stop=(k == KT - 1))
                        elif name == "q":
                            for g in range(2):
                                for k in range(KT):
                                    ins = mm(chain[:, g * LQ:(g + 1) * LQ], wq[l][:, k, g * 128:(g + 1) * 128],
                                             xt[:, k, :], start=(k == 0), stop=(k == KT - 1))
                        elif name == "lat":
                            o = KOFF[2]
                            for g in range(2):
                                for k in range(KT):
                                    mm3(chain[:, g * LQ:(g + 1) * LQ], wkv_hi[:, k, o + g * 128:o + (g + 1) * 128],
                                        wkv_lo[:, k, o + g * 128:o + (g + 1) * 128], xt_hi[:, k, :], xt_lo[:, k, :],
                                        k == 0, k == KT - 1)
                            for k in range(KT):
                                ins = mm3(chain[0:LQ, 256:512], xt_hi[:, k, :], xt_lo[:, k, :],
                                          wkv_hi[:, k, o + 256:o + 512], wkv_lo[:, k, o + 256:o + 512],
                                          k == 0, k == KT - 1)
                        elif name == "up":
                            pe.wait_ge(mlp_loaded, 16 if l == 2 else 32)
                            for t in range(8):
                                for k in range(KT):
                                    ins = mm(chain[:, t * LQ:(t + 1) * LQ], up_w[:, k, t * 128:(t + 1) * 128],
                                             xt[:, k, :], start=(k == 0), stop=(k == KT - 1))
                        elif name == "down":
                            for t in range(8):
                                ins = mm(chain[0:LQ, 0:D], hid[:, t * LQ:(t + 1) * LQ], down_w[:, t, :],
                                         start=(t == 0), stop=(t == 7))
                        ins.then_inc(chain_pe, 1)

                    for s in order:
                        if s[0] == "p":
                            project_use(s)
                        elif s[0] == "s":
                            score_unit(s)
                        elif s[0] == "m":
                            turn_max(s)
                        elif s[0] == "t":
                            scores_t(*s[1:])
                            n = lagging.index(s[1:])
                            if n >= 2 and lagging[n - 2][0] == s[1]:
                                values(*lagging[n - 2])
                        elif s[0] == "te":
                            for step in [t for t in lagging if t[0] == s[1]][-2:]:
                                values(*step)
                        elif s[0] == "c":
                            chain_part(s)
                        elif s[0] == "xt0":
                            pe.wait_ge(x_loaded, 16)
                            for k in range(KT):
                                ins = nc.tensor.transpose(score[:, 2, k * LQ:(k + 1) * LQ],
                                                          x_next[:, k * 128:(k + 1) * 128], ident[0:LQ, 0:LQ])
                            ins.then_inc(q0_pe, 1)
                        elif s[0] == "q0":
                            pe.wait_ge(q0_out, 1)
                            for g in range(4):
                                for k in range(KT):
                                    ins = mm(score[0:64, 3, g * LQ:(g + 1) * LQ], wq[0][:, k, g * 64:(g + 1) * 64],
                                             xt_next[:, k, :], start=(k == 0), stop=(k == KT - 1))
                            ins.then_inc(q0_pe, 1)
                        elif s[0] == "bias":
                            if chain_steps and looped:
                                pe.wait_ge(chain_out, steps_out_before(s))
                                pe.wait_ge(exp_done, steps_before[4])
                            pe.wait_ge(mask_ready, 2)
                            for m, (tile, p) in enumerate(((mask_row, 32), (mask_row, 0))):
                                for t, (k, kn) in enumerate(key_tiles(0)):
                                    ins = mm((score[:, 0], chain)[m][0:kn, t:t + 1], tile[p:p + 1, k:k + kn],
                                             one_bf[p:p + 1, :], start=True, stop=True)
                            ins.then_inc(bias_ready, 1)

            nc.all_engine_barrier(sems_to_clear=turn_sems)

        turn_block(first_order(), None, 0)
        with nc.Fori(0, NB) as i:
            turn_block(batch_order(), i, (i + 1) % NB)


def kernel(**inputs):
    import numpy as np
    import concourse.bacc as bacc
    from concourse.bass_utils import run_bass_kernel_spmd

    a = {n: np.asarray(v) for n, v in inputs.items()}
    P = lambda l, n: a["L%d_xattn_%s" % (l, n)]
    rows_of = lambda w: w.reshape(-1, 128, w.shape[1]).transpose(1, 0, 2).reshape(128, -1)

    kv2 = P(2, "kv_w").reshape(D, D, 2)
    w_kv = np.concatenate([P(0, "Wk"), P(0, "Wv"), P(1, "Wk").T, P(1, "Wv").T, kv2[..., 0], kv2[..., 1],
                           P(3, "k_w"), P(3, "v_w")], 1)
    wq0 = P(0, "Wq").reshape(D, 8, 4, 8).transpose(0, 2, 1, 3).reshape(D, D)
    w_f = [wq0, P(0, "Wo"), P(1, "Wq").T, P(1, "Wo").T, P(2, "q_w"), P(2, "out_w"), P(3, "q_w"), P(3, "cproj_w")]
    w_mlp = [np.concatenate([rows_of(P(2, "mlp_w1")), rows_of(P(2, "mlp_w2"))], 1),
             np.concatenate([rows_of(P(3, "fc_w")), rows_of(P(3, "proj_w"))], 1)]

    kvb = P(2, "kv_b").reshape(D, 2)
    bk0 = np.zeros((128, 1), np.float32)
    bk0[0:64, 0] = P(0, "bk")
    bq0 = np.zeros((128, 4), np.float32)
    bq0[0:64] = P(0, "bq").reshape(8, 4, 8).transpose(0, 2, 1).reshape(64, 4)
    by = lambda b: b.reshape(-1, 128).T
    part = np.arange(128)
    hm = (part[:, None] // 16 == np.arange(8)).astype(np.float32)
    hm0 = (part[:, None] // 8 == np.arange(8)).astype(np.float32)
    e56 = (part[:, None] - 64 == np.arange(LQ)).astype(np.float32)
    vecs = {"bk0": bk0, "bk2": by(kvb[:, 0]), "bk3": by(P(3, "k_b")), "bq0": bq0, "bq2": by(P(2, "q_b")),
            "bq3": by(P(3, "q_b")), "g1": by(P(1, "ln_gamma")), "b1": by(P(1, "ln_beta")),
            "pw": by(P(2, "postnorm_w")), "ln1w": by(P(3, "ln1_w")), "ln1b": by(P(3, "ln1_b")),
            "ln2w": by(P(3, "ln2_w")), "ln2b": by(P(3, "ln2_b")), "mb2": by(P(2, "mlp_b1")),
            "mb3": by(P(3, "fc_b")), "hm": hm, "hm0": hm0, "e56": e56, "ident": np.eye(128, dtype=np.float32)}
    bv0 = np.broadcast_to(P(0, "bv").reshape(8, 1, 8), (8, 4, 8)).reshape(D)
    rows = [bv0, P(0, "bo"), P(0, "gamma"), P(0, "beta"), kvb[:, 1], P(2, "out_b"), P(2, "mlp_b2"),
            P(3, "v_b"), P(3, "cproj_b"), P(3, "proj_b"), P(1, "gate")]
    arrays = {
        "ctx": a["ctx_2048"], "x": a["x"], "mask0": a["mask_Bx1xSxS2_ff0"].reshape(NB, LQ, LK),
        "mask_bool": a["mask_BxS2_bf1"].view(np.uint8).reshape(NB, 1, LK),
        "mask_int": a["mask_BxS2_ik0"].reshape(NB, 1, LK),
        "w_kv": rows_of(w_kv), "w_f": np.concatenate([rows_of(w) for w in w_f], 1), "w_mlp": np.stack(w_mlp),
        "vecs": np.concatenate([vecs[n] for n in VP], 1), "rows": np.concatenate(rows)[None],
    }
    arrays = {n: np.ascontiguousarray(v) for n, v in arrays.items()}
    nc = bacc.Bacc("TRN2", target_bir_lowering=False, num_devices=1,
                   dynamic_dma_scratch_size=1024)
    args = [nc.dram_tensor(n + "_dram", v.shape, mybir.dt.from_np(v.dtype), kind="ExternalInput").ap()
            for n, v in arrays.items()]
    out = nc.dram_tensor("out_dram", (NB, LQ, D), F32, kind="ExternalOutput").ap()
    fused_attention_kernel(nc, *args, out)
    r = run_bass_kernel_spmd(nc, [{n + "_dram": v for n, v in arrays.items()}], core_ids=[0])
    return r.results[0]["out_dram"]
```
